# Optimizing a Trainium2 kernel written in Bass

```python
import numpy as np
import jax
import jax.numpy as jnp

def _softmax(x, axis=-1):
    return jax.nn.softmax(x, axis=axis)

def _gelu(x):
    return jax.nn.gelu(x, approximate=True)

def _silu(x):
    return jax.nn.silu(x)

def _sigmoid(x):
    return jax.nn.sigmoid(x)

def _layernorm(x, axis=-1, eps=1e-05):
    m = jnp.mean(x, axis=axis, keepdims=True)
    v = jnp.var(x, axis=axis, keepdims=True)
    return (x - m) / jnp.sqrt(v + eps)

def _scatter_add(tgt, idx, src, axis=0):
    return tgt.at[idx].add(src)

def _segment_sum(src, seg, n):
    return jax.ops.segment_sum(src, seg, n)
kernel_name = 'mk_xattn_ffn_d4_seqx_r8_2c2b5d'

def setup_inputs(seed: int=0):
    np.random.seed(seed)
    _w = jnp.asarray

    def _rec_inputs():
        import jax
        import jax.numpy as jnp
        _rk = jax.random.key(seed)
        x = 0.002226 + 0.9996 * jax.random.normal(jax.random.fold_in(_rk, 1), (2, 512, 128), jnp.float32)
        _lenS = 512 - jax.random.randint(jax.random.fold_in(_rk, 7), (2,), 0, max(1, 512 // 4) + 1, jnp.int32)
        _lenS2 = 77 - jax.random.randint(jax.random.fold_in(_rk, 8), (2,), 0, max(1, 77 // 4) + 1, jnp.int32)
        _ctx_1024P = jax.random.normal(jax.random.fold_in(_rk, 11), (2, 16, 128), jnp.float32)
        _ctx_1024c = jax.random.dirichlet(jax.random.fold_in(_rk, 511), 0.3 * jnp.ones((16,), jnp.float32), (2, 77))
        _ctx_1024t = jnp.einsum('bsk,bkd->bsd', _ctx_1024c, _ctx_1024P)
        _ctx_1024t = _ctx_1024t * jax.lax.rsqrt(jnp.mean(jnp.square(_ctx_1024t)) + 1e-12) * 0.953939
        ctx_1024 = -0.000125008 + 0.999885 * (_ctx_1024t + 0.3 * jax.random.normal(jax.random.fold_in(_rk, 611), (2, 77, 128), jnp.float32))
        _validS = jnp.arange(512)[None, :] < _lenS[:, None]
        _validS2 = jnp.arange(77)[None, :] < _lenS2[:, None]
        _causal = jnp.tril(jnp.ones((512, 512), dtype=bool))
        mask_Bx16xSxS2_bk1 = jnp.broadcast_to(_validS2[:, None, None, :], (2, 16, 512, 77))
        return (x, ctx_1024, mask_Bx16xSxS2_bk1)
    x, ctx_1024, mask_Bx16xSxS2_bk1 = _rec_inputs()

    def _L0_xattn_setup():
        import jax, jax.numpy as jnp
        import numpy as np
        B, M, N, DIM, DH, H = (8, 512, 64, 128, 128, 8)
        INNER = DH * H
        EPS = 1e-05

        def _layernorm(x, g, b):
            mu = jnp.mean(x, axis=-1, keepdims=True)
            var = jnp.var(x, axis=-1, keepdims=True)
            return (x - mu) * jax.lax.rsqrt(var + EPS) * g + b
        key = jax.random.key(seed)
        ks = jax.random.split(key, 8)
        sd = 0.02
        return {'x': jax.random.normal(ks[0], (B, M, DIM), jnp.float32), 'latents': jax.random.normal(ks[1], (B, N, DIM), jnp.float32), 'gamma_media': jnp.ones((DIM,), jnp.float32), 'beta_media': jnp.zeros((DIM,), jnp.float32), 'gamma_lat': jnp.ones((DIM,), jnp.float32), 'beta_lat': jnp.zeros((DIM,), jnp.float32), 'Wq': jax.random.normal(ks[2], (DIM, INNER), jnp.float32) * sd, 'bq': jnp.zeros((INNER,), jnp.float32), 'Wkv': jax.random.normal(ks[3], (DIM, 2 * INNER), jnp.float32) * sd, 'bkv': jnp.zeros((2 * INNER,), jnp.float32), 'Wo': jax.random.normal(ks[4], (INNER, DIM), jnp.float32) * sd, 'bo': jnp.zeros((DIM,), jnp.float32)}
    _L0_xattn_all = _L0_xattn_setup()
    _L0_xattn_in = {k: v for k, v in _L0_xattn_all.items() if k in ('gamma_media', 'beta_media', 'gamma_lat', 'beta_lat', 'Wq', 'bq', 'Wkv', 'bkv', 'Wo', 'bo')}
    del _L0_xattn_all

    def _L0_ffn_setup():
        import jax, jax.numpy as jnp
        import numpy as np
        HIDDEN = 128
        NUM_EXPERTS = 8
        TOP_K = 2
        B, S = (4, 128)
        key = jax.random.key(seed)
        ks = jax.random.split(key, 8)
        H, E = (HIDDEN, NUM_EXPERTS)
        sc = lambda fan_in: 1.0 / np.sqrt(fan_in)
        x = jax.random.normal(ks[0], (B, S, H), dtype=jnp.float32)
        Wr = jax.random.uniform(ks[1], (H, E), minval=-sc(H), maxval=sc(H), dtype=jnp.float32)
        br = jax.random.uniform(ks[2], (E,), minval=-sc(H), maxval=sc(H), dtype=jnp.float32)
        W1 = jax.random.uniform(ks[3], (E, H, 2 * H), minval=-sc(H), maxval=sc(H), dtype=jnp.float32)
        b1 = jax.random.uniform(ks[4], (E, 2 * H), minval=-sc(H), maxval=sc(H), dtype=jnp.float32)
        W2 = jax.random.uniform(ks[5], (E, 2 * H, H), minval=-sc(2 * H), maxval=sc(2 * H), dtype=jnp.float32)
        b2 = jax.random.uniform(ks[6], (E, H), minval=-sc(2 * H), maxval=sc(2 * H), dtype=jnp.float32)
        return {'x': x, 'Wr': Wr, 'br': br, 'W1': W1, 'b1': b1, 'W2': W2, 'b2': b2}
    _L0_ffn_all = _L0_ffn_setup()
    _L0_ffn_in = {k: v for k, v in _L0_ffn_all.items() if k in ('Wr', 'br', 'W1', 'b1', 'W2', 'b2')}
    del _L0_ffn_all

    def _L1_xattn_setup():
        import jax, jax.numpy as jnp
        import numpy as np
        DIM = 128
        NUM_HEADS = 8
        SCALE = (DIM // NUM_HEADS) ** (-0.5)
        key = jax.random.key(seed)
        ks = jax.random.split(key, 7)
        B, N, C = (4, 256, DIM)
        s = C ** (-0.5)
        return {'m_q': jax.random.normal(ks[0], (B, N, C), jnp.float32), 'm_kv': jax.random.normal(ks[1], (B, N, C), jnp.float32), 'Wq': jax.random.normal(ks[2], (C, C), jnp.float32) * s, 'Wk': jax.random.normal(ks[3], (C, C), jnp.float32) * s, 'Wv': jax.random.normal(ks[4], (C, C), jnp.float32) * s, 'Wp': jax.random.normal(ks[5], (C, C), jnp.float32) * s, 'bp': jax.random.normal(ks[6], (C,), jnp.float32) * 0.01}
    _L1_xattn_all = _L1_xattn_setup()
    _L1_xattn_in = {k: v for k, v in _L1_xattn_all.items() if k in ('Wq', 'Wk', 'Wv', 'Wp', 'bp')}
    del _L1_xattn_all

    def _L1_ffn_setup():
        import jax, jax.numpy as jnp
        import numpy as np
        D_MODEL = 128
        key = jax.random.key(seed)
        k_x, k_w, k_a1, k_a2 = jax.random.split(key, 4)
        x = jax.random.normal(k_x, (4, 256, D_MODEL), dtype=jnp.float32)
        weight = jax.random.normal(k_w, (D_MODEL, D_MODEL), dtype=jnp.float32) * 0.02
        aux_weight1 = jax.random.normal(k_a1, (D_MODEL, D_MODEL), dtype=jnp.float32) * 0.02
        aux_weight2 = jax.random.normal(k_a2, (D_MODEL, D_MODEL), dtype=jnp.float32) * 0.02
        bias = jnp.zeros((D_MODEL,), dtype=jnp.float32)
        return {'x': x, 'weight': weight, 'aux_weight1': aux_weight1, 'aux_weight2': aux_weight2, 'bias': bias}
    _L1_ffn_all = _L1_ffn_setup()
    _L1_ffn_in = {k: v for k, v in _L1_ffn_all.items() if k in ('weight', 'aux_weight1', 'aux_weight2', 'bias')}
    del _L1_ffn_all

    def _L2_xattn_setup():
        import jax, jax.numpy as jnp
        import numpy as np
        import math
        B, S, D, H = (2, 256, 128, 16)
        DH = D // H
        key = jax.random.key(seed)
        ks = jax.random.split(key, 13)
        sc = 1.0 / math.sqrt(D)
        return {'q': jax.random.normal(ks[0], (B, S, D), jnp.float32), 'k': jax.random.normal(ks[1], (B, S, D), jnp.float32), 'v': jax.random.normal(ks[2], (B, S, D), jnp.float32), 'mask': jax.random.randint(ks[3], (B, H, S, S), 0, 2) == 1, 'Wq': jax.random.normal(ks[4], (D, D), jnp.float32) * sc, 'bq': jnp.zeros((D,), jnp.float32), 'Wk': jax.random.normal(ks[5], (D, D), jnp.float32) * sc, 'bk': jnp.zeros((D,), jnp.float32), 'Wv': jax.random.normal(ks[6], (D, D), jnp.float32) * sc, 'bv': jnp.zeros((D,), jnp.float32), 'Wo': jax.random.normal(ks[7], (D, D), jnp.float32) * sc, 'bo': jnp.zeros((D,), jnp.float32)}
    _L2_xattn_all = _L2_xattn_setup()
    _L2_xattn_in = {k: v for k, v in _L2_xattn_all.items() if k in ('Wq', 'bq', 'Wk', 'bk', 'Wv', 'bv', 'Wo', 'bo')}
    del _L2_xattn_all

    def _L2_ffn_setup():
        import jax, jax.numpy as jnp
        import numpy as np
        QMAX = 127.0

        def _ste_round(v):
            return v + jax.lax.stop_gradient(jnp.round(v) - v)

        def _act_fake_quant(x, clip_factor):
            scale = jax.nn.sigmoid(clip_factor) * jnp.max(jnp.abs(x)) / QMAX
            return jnp.clip(_ste_round(x / scale), -QMAX - 1.0, QMAX) * scale

        def _weight_fake_quant(w):
            scale = jnp.max(jnp.abs(w), axis=1, keepdims=True) / QMAX
            return jnp.clip(_ste_round(w / scale), -QMAX - 1.0, QMAX) * scale
        key = jax.random.key(seed)
        k1, k2, k3, k4 = jax.random.split(key, 4)
        B, S, H, I = (8, 1024, 128, 352)
        return {'x': jax.random.normal(k1, (B, S, H), dtype=jnp.float32), 'clip_x': jnp.full((1,), 4.0, dtype=jnp.float32), 'clip_down': jnp.full((1,), 4.0, dtype=jnp.float32), 'w_gate': jax.random.normal(k2, (I, H), dtype=jnp.float32) * 0.02, 'w_up': jax.random.normal(k3, (I, H), dtype=jnp.float32) * 0.02, 'w_down': jax.random.normal(k4, (H, I), dtype=jnp.float32) * 0.02}
    _L2_ffn_all = _L2_ffn_setup()
    _L2_ffn_in = {k: v for k, v in _L2_ffn_all.items() if k in ('clip_x', 'clip_down', 'w_gate', 'w_up', 'w_down')}
    del _L2_ffn_all

    def _L3_xattn_setup():
        import jax, jax.numpy as jnp
        import numpy as np
        H = 16
        D_MODEL = 128
        D_K = D_MODEL // H
        key = jax.random.key(seed)
        ks = jax.random.split(key, 11)
        B, S = (2, 256)
        scale = 1.0 / np.sqrt(D_MODEL)
        inp = {'query': jax.random.normal(ks[0], (B, S, D_MODEL), jnp.float32), 'key': jax.random.normal(ks[1], (B, S, D_MODEL), jnp.float32), 'value': jax.random.normal(ks[2], (B, S, D_MODEL), jnp.float32), 'Wq': jax.random.normal(ks[3], (D_MODEL, D_MODEL), jnp.float32) * scale, 'bq': jnp.zeros((D_MODEL,), jnp.float32), 'Wk': jax.random.normal(ks[4], (D_MODEL, D_MODEL), jnp.float32) * scale, 'bk': jnp.zeros((D_MODEL,), jnp.float32), 'Wv': jax.random.normal(ks[5], (D_MODEL, D_MODEL), jnp.float32) * scale, 'bv': jnp.zeros((D_MODEL,), jnp.float32), 'Wo': jax.random.normal(ks[6], (D_MODEL, D_MODEL), jnp.float32) * scale, 'bo': jnp.zeros((D_MODEL,), jnp.float32)}
        return inp
    _L3_xattn_all = _L3_xattn_setup()
    _L3_xattn_in = {k: v for k, v in _L3_xattn_all.items() if k in ('Wq', 'bq', 'Wk', 'bk', 'Wv', 'bv', 'Wo', 'bo')}
    del _L3_xattn_all

    def _L3_ffn_setup():
        import jax, jax.numpy as jnp
        import numpy as np
        BLOCK = 32
        W_BITS = 4
        ACT_BITS = 16

        def act_qdq(x):
            qmax = 2.0 ** (ACT_BITS - 1) - 1.0
            scale = jnp.maximum(jnp.max(jnp.abs(x)) / qmax, 1e-12)
            return jnp.clip(jnp.round(x / scale), -qmax - 1.0, qmax) * scale

        def fixed_qdq_u16(x):
            scale = 1.0 / 65536.0
            return jnp.clip(jnp.round(x / scale), 0.0, 65535.0) * scale

        def lpbq_dequant(w):
            O, I = w.shape
            qmax = 2.0 ** (W_BITS - 1) - 1.0
            wb = w.reshape(O, I // BLOCK, BLOCK)
            s = jnp.maximum(jnp.max(jnp.abs(wb), axis=-1, keepdims=True) / qmax, 1e-12)
            wq = jnp.clip(jnp.round(wb / s), -qmax - 1.0, qmax) * s
            return wq.reshape(O, I)
        key = jax.random.key(seed)
        k1, k2, k3, k4 = jax.random.split(key, 4)
        B, S, H, I = (2, 512, 128, 384)
        x = jax.random.normal(k1, (B, S, H), jnp.float32)
        w_gate = jax.random.normal(k2, (I, H), jnp.float32) * 0.02
        w_up = jax.random.normal(k3, (I, H), jnp.float32) * 0.02
        w_down = jax.random.normal(k4, (H, I), jnp.float32) * 0.02
        return {'x': x, 'w_gate': w_gate, 'w_up': w_up, 'w_down': w_down}
    _L3_ffn_all = _L3_ffn_setup()
    _L3_ffn_in = {k: v for k, v in _L3_ffn_all.items() if k in ('w_gate', 'w_up', 'w_down')}
    del _L3_ffn_all
    return {'x': x, 'ctx_1024': ctx_1024, 'mask_Bx16xSxS2_bk1': mask_Bx16xSxS2_bk1, 'L0_xattn_gamma_media': _L0_xattn_in['gamma_media'], 'L0_xattn_beta_media': _L0_xattn_in['beta_media'], 'L0_xattn_gamma_lat': _L0_xattn_in['gamma_lat'], 'L0_xattn_beta_lat': _L0_xattn_in['beta_lat'], 'L0_xattn_Wq': _L0_xattn_in['Wq'], 'L0_xattn_bq': _L0_xattn_in['bq'], 'L0_xattn_Wkv': _L0_xattn_in['Wkv'], 'L0_xattn_bkv': _L0_xattn_in['bkv'], 'L0_xattn_Wo': _L0_xattn_in['Wo'], 'L0_xattn_bo': _L0_xattn_in['bo'], 'L0_ffn_Wr': _L0_ffn_in['Wr'], 'L0_ffn_br': _L0_ffn_in['br'], 'L0_ffn_W1': _L0_ffn_in['W1'], 'L0_ffn_b1': _L0_ffn_in['b1'], 'L0_ffn_W2': _L0_ffn_in['W2'], 'L0_ffn_b2': _L0_ffn_in['b2'], 'L1_xattn_Wq': _L1_xattn_in['Wq'], 'L1_xattn_Wk': _L1_xattn_in['Wk'], 'L1_xattn_Wv': _L1_xattn_in['Wv'], 'L1_xattn_Wp': _L1_xattn_in['Wp'], 'L1_xattn_bp': _L1_xattn_in['bp'], 'L1_ffn_weight': _L1_ffn_in['weight'], 'L1_ffn_aux_weight1': _L1_ffn_in['aux_weight1'], 'L1_ffn_aux_weight2': _L1_ffn_in['aux_weight2'], 'L1_ffn_bias': _L1_ffn_in['bias'], 'L2_xattn_Wq': _L2_xattn_in['Wq'], 'L2_xattn_bq': _L2_xattn_in['bq'], 'L2_xattn_Wk': _L2_xattn_in['Wk'], 'L2_xattn_bk': _L2_xattn_in['bk'], 'L2_xattn_Wv': _L2_xattn_in['Wv'], 'L2_xattn_bv': _L2_xattn_in['bv'], 'L2_xattn_Wo': _L2_xattn_in['Wo'], 'L2_xattn_bo': _L2_xattn_in['bo'], 'L2_ffn_clip_x': _L2_ffn_in['clip_x'], 'L2_ffn_clip_down': _L2_ffn_in['clip_down'], 'L2_ffn_w_gate': _L2_ffn_in['w_gate'], 'L2_ffn_w_up': _L2_ffn_in['w_up'], 'L2_ffn_w_down': _L2_ffn_in['w_down'], 'L3_xattn_Wq': _L3_xattn_in['Wq'], 'L3_xattn_bq': _L3_xattn_in['bq'], 'L3_xattn_Wk': _L3_xattn_in['Wk'], 'L3_xattn_bk': _L3_xattn_in['bk'], 'L3_xattn_Wv': _L3_xattn_in['Wv'], 'L3_xattn_bv': _L3_xattn_in['bv'], 'L3_xattn_Wo': _L3_xattn_in['Wo'], 'L3_xattn_bo': _L3_xattn_in['bo'], 'L3_ffn_w_gate': _L3_ffn_in['w_gate'], 'L3_ffn_w_up': _L3_ffn_in['w_up'], 'L3_ffn_w_down': _L3_ffn_in['w_down']}

def reference(x, ctx_1024, mask_Bx16xSxS2_bk1, L0_xattn_gamma_media, L0_xattn_beta_media, L0_xattn_gamma_lat, L0_xattn_beta_lat, L0_xattn_Wq, L0_xattn_bq, L0_xattn_Wkv, L0_xattn_bkv, L0_xattn_Wo, L0_xattn_bo, L0_ffn_Wr, L0_ffn_br, L0_ffn_W1, L0_ffn_b1, L0_ffn_W2, L0_ffn_b2, L1_xattn_Wq, L1_xattn_Wk, L1_xattn_Wv, L1_xattn_Wp, L1_xattn_bp, L1_ffn_weight, L1_ffn_aux_weight1, L1_ffn_aux_weight2, L1_ffn_bias, L2_xattn_Wq, L2_xattn_bq, L2_xattn_Wk, L2_xattn_bk, L2_xattn_Wv, L2_xattn_bv, L2_xattn_Wo, L2_xattn_bo, L2_ffn_clip_x, L2_ffn_clip_down, L2_ffn_w_gate, L2_ffn_w_up, L2_ffn_w_down, L3_xattn_Wq, L3_xattn_bq, L3_xattn_Wk, L3_xattn_bk, L3_xattn_Wv, L3_xattn_bv, L3_xattn_Wo, L3_xattn_bo, L3_ffn_w_gate, L3_ffn_w_up, L3_ffn_w_down):
    import jax
    import jax.numpy as jnp

    def _L0_xattn_ref(x, latents, gamma_media, beta_media, gamma_lat, beta_lat, Wq, bq, Wkv, bkv, Wo, bo):
        import jax, jax.numpy as jnp
        import numpy as np
        B, M, N, DIM, DH, H = (8, 512, 64, 128, 128, 8)
        INNER = DH * H
        EPS = 1e-05

        def _layernorm(x, g, b):
            mu = jnp.mean(x, axis=-1, keepdims=True)
            var = jnp.var(x, axis=-1, keepdims=True)
            return (x - mu) * jax.lax.rsqrt(var + EPS) * g + b
        b = x.shape[0]
        xn = _layernorm(x, gamma_media, beta_media)
        ln = _layernorm(latents, gamma_lat, beta_lat)
        q = ln @ Wq + bq
        kv_input = jnp.concatenate([xn, ln], axis=1)
        kv = kv_input @ Wkv + bkv
        k, v = jnp.split(kv, 2, axis=-1)

        def to_heads(t):
            return t.reshape(b, t.shape[1], H, DH).transpose(0, 2, 1, 3)
        q, k, v = (to_heads(q), to_heads(k), to_heads(v))
        q = q * DH ** (-0.5)
        sim = jnp.einsum('bhid,bhjd->bhij', q, k)
        attn = jax.nn.softmax(sim, axis=-1)
        out = jnp.einsum('bhij,bhjd->bhid', attn, v)
        out = out.transpose(0, 2, 1, 3).reshape(b, -1, INNER)
        return out @ Wo + bo

    def _L0_ffn_ref(x, Wr, br, W1, b1, W2, b2):
        import jax, jax.numpy as jnp
        import numpy as np
        HIDDEN = 128
        NUM_EXPERTS = 8
        TOP_K = 2
        B, S = (4, 128)
        B_, S_, H = x.shape
        xf = x.reshape(-1, H)
        logits = xf @ Wr + br
        topk_w, topk_idx = jax.lax.top_k(logits, TOP_K)
        topk_w = jax.nn.softmax(topk_w, axis=-1)
        gate = jnp.sum(jax.nn.one_hot(topk_idx, NUM_EXPERTS, dtype=xf.dtype) * topk_w[..., None], axis=1)
        h = jax.nn.relu(jnp.einsum('th,ehf->etf', xf, W1) + b1[:, None, :])
        y = jnp.einsum('etf,efh->eth', h, W2) + b2[:, None, :]
        out = jnp.einsum('te,eth->th', gate, y)
        return out.reshape(B_, S_, H)

    def _L1_xattn_ref(m_q, m_kv, Wq, Wk, Wv, Wp, bp):
        import jax, jax.numpy as jnp
        import numpy as np
        DIM = 128
        NUM_HEADS = 8
        SCALE = (DIM // NUM_HEADS) ** (-0.5)
        B, N, C = m_q.shape
        q = m_q @ Wq
        k = m_kv @ Wk
        v = m_kv @ Wv
        attn = jnp.einsum('bnc,bmc->bnm', q, k) * SCALE
        attn = jax.nn.softmax(attn, axis=-1)
        x = jnp.einsum('bnm,bmc->bnc', attn, v)
        x = jnp.swapaxes(x, 1, 2).reshape(B, N, C)
        return x @ Wp + bp

    def _L1_ffn_ref(x, weight, aux_weight1, aux_weight2, bias):
        import jax, jax.numpy as jnp
        import numpy as np
        D_MODEL = 128
        h = jnp.einsum('btc,cd->btd', x, weight)
        h = jnp.einsum('btc,cd->btd', h, aux_weight1)
        h = jnp.einsum('btc,cd->btd', h, aux_weight2)
        return jnp.tanh(h + bias)

    def _L2_xattn_ref(q, k, v, mask, Wq, bq, Wk, bk, Wv, bv, Wo, bo):
        import jax, jax.numpy as jnp
        import numpy as np
        import math
        B, S, D, H = (2, 256, 128, 16)
        DH = D // H
        b = q.shape[0]

        def proj(x, W, bias):
            return (x @ W + bias).reshape(b, -1, H, DH).transpose(0, 2, 1, 3)
        qh, kh, vh = (proj(q, Wq, bq), proj(k, Wk, bk), proj(v, Wv, bv))
        scores = jnp.einsum('bhqd,bhkd->bhqk', qh, kh) / math.sqrt(DH)
        scores = jnp.where(mask, -jnp.inf, scores)
        attn = jax.nn.softmax(scores, axis=-1)
        out = jnp.einsum('bhqk,bhkd->bhqd', attn, vh)
        out = out.transpose(0, 2, 1, 3).reshape(b, -1, D)
        return out @ Wo + bo

    def _L2_ffn_ref(x, clip_x, clip_down, w_gate, w_up, w_down):
        import jax, jax.numpy as jnp
        import numpy as np
        QMAX = 127.0

        def _ste_round(v):
            return v + jax.lax.stop_gradient(jnp.round(v) - v)

        def _act_fake_quant(x, clip_factor):
            scale = jax.nn.sigmoid(clip_factor) * jnp.max(jnp.abs(x)) / QMAX
            return jnp.clip(_ste_round(x / scale), -QMAX - 1.0, QMAX) * scale

        def _weight_fake_quant(w):
            scale = jnp.max(jnp.abs(w), axis=1, keepdims=True) / QMAX
            return jnp.clip(_ste_round(w / scale), -QMAX - 1.0, QMAX) * scale
        xq = _act_fake_quant(x, clip_x[0])
        gate = jnp.einsum('bsh,ih->bsi', xq, _weight_fake_quant(w_gate))
        up = jnp.einsum('bsh,ih->bsi', xq, _weight_fake_quant(w_up))
        h = _act_fake_quant(jax.nn.silu(gate) * up, clip_down[0])
        return jnp.einsum('bsi,hi->bsh', h, _weight_fake_quant(w_down))

    def _L3_xattn_ref(query, key, value, Wq, bq, Wk, bk, Wv, bv, Wo, bo):
        import jax, jax.numpy as jnp
        import numpy as np
        H = 16
        D_MODEL = 128
        D_K = D_MODEL // H
        B, S, _ = query.shape

        def proj(x, W, b):
            y = jnp.einsum('bsd,df->bsf', x, W) + b
            return y.reshape(B, -1, H, D_K).transpose(0, 2, 1, 3)
        q = proj(query, Wq, bq)
        k = proj(key, Wk, bk)
        v = proj(value, Wv, bv)
        scores = jnp.einsum('bhqd,bhkd->bhqk', q, k) / jnp.sqrt(jnp.float32(D_K))
        p = jax.nn.softmax(scores, axis=-1)
        x = jnp.einsum('bhqk,bhkd->bhqd', p, v)
        x = x.transpose(0, 2, 1, 3).reshape(B, -1, H * D_K)
        return jnp.einsum('bsd,df->bsf', x, Wo) + bo

    def _L3_ffn_ref(x, w_gate, w_up, w_down):
        import jax, jax.numpy as jnp
        import numpy as np
        BLOCK = 32
        W_BITS = 4
        ACT_BITS = 16

        def act_qdq(x):
            qmax = 2.0 ** (ACT_BITS - 1) - 1.0
            scale = jnp.maximum(jnp.max(jnp.abs(x)) / qmax, 1e-12)
            return jnp.clip(jnp.round(x / scale), -qmax - 1.0, qmax) * scale

        def fixed_qdq_u16(x):
            scale = 1.0 / 65536.0
            return jnp.clip(jnp.round(x / scale), 0.0, 65535.0) * scale

        def lpbq_dequant(w):
            O, I = w.shape
            qmax = 2.0 ** (W_BITS - 1) - 1.0
            wb = w.reshape(O, I // BLOCK, BLOCK)
            s = jnp.maximum(jnp.max(jnp.abs(wb), axis=-1, keepdims=True) / qmax, 1e-12)
            wq = jnp.clip(jnp.round(wb / s), -qmax - 1.0, qmax) * s
            return wq.reshape(O, I)
        x = act_qdq(x)
        up = act_qdq(x @ lpbq_dequant(w_up).T)
        gate = act_qdq(x @ lpbq_dequant(w_gate).T)
        sig = fixed_qdq_u16(jax.nn.sigmoid(gate))
        gate = act_qdq(gate * sig)
        o = act_qdq(gate * up)
        return o @ lpbq_dequant(w_down).T
    x = x + _L0_xattn_ref(ctx_1024, _layernorm(x, axis=-1), L0_xattn_gamma_media, L0_xattn_beta_media, L0_xattn_gamma_lat, L0_xattn_beta_lat, L0_xattn_Wq, L0_xattn_bq, L0_xattn_Wkv, L0_xattn_bkv, L0_xattn_Wo, L0_xattn_bo)
    x = x + _L0_ffn_ref(_layernorm(x, axis=-1), L0_ffn_Wr, L0_ffn_br, L0_ffn_W1, L0_ffn_b1, L0_ffn_W2, L0_ffn_b2)
    x = x + _L1_xattn_ref(_layernorm(x, axis=-1), ctx_1024, L1_xattn_Wq, L1_xattn_Wk, L1_xattn_Wv, L1_xattn_Wp, L1_xattn_bp)
    x = x + _L1_ffn_ref(_layernorm(x, axis=-1), L1_ffn_weight, L1_ffn_aux_weight1, L1_ffn_aux_weight2, L1_ffn_bias)
    x = x + _L2_xattn_ref(_layernorm(x, axis=-1), ctx_1024, ctx_1024, mask_Bx16xSxS2_bk1, L2_xattn_Wq, L2_xattn_bq, L2_xattn_Wk, L2_xattn_bk, L2_xattn_Wv, L2_xattn_bv, L2_xattn_Wo, L2_xattn_bo)
    x = x + _L2_ffn_ref(_layernorm(x, axis=-1), L2_ffn_clip_x, L2_ffn_clip_down, L2_ffn_w_gate, L2_ffn_w_up, L2_ffn_w_down)
    x = x + _L3_xattn_ref(_layernorm(x, axis=-1), ctx_1024, ctx_1024, L3_xattn_Wq, L3_xattn_bq, L3_xattn_Wk, L3_xattn_bk, L3_xattn_Wv, L3_xattn_bv, L3_xattn_Wo, L3_xattn_bo)
    x = x + _L3_ffn_ref(_layernorm(x, axis=-1), L3_ffn_w_gate, L3_ffn_w_up, L3_ffn_w_down)
    return x

_drawn_inputs = setup_inputs


def setup_inputs(seed=0):
    import zlib

    import numpy as np

    out = dict(_drawn_inputs(seed))
    spreads = {'L0_xattn_gamma_media': (1.0, 0.6),
     'L0_xattn_beta_media': (0.0, 0.8),
     'L0_xattn_gamma_lat': (1.0, 0.6),
     'L0_xattn_beta_lat': (0.0, 0.385),
     'L0_xattn_bq': (0.0, 0.8),
     'L0_xattn_bkv': (0.0, 0.1),
     'L0_xattn_bo': (0.0, 0.1),
     'L1_ffn_bias': (0.0, 0.1),
     'L2_xattn_bq': (0.0, 0.34),
     'L2_xattn_bk': (0.0, 2.0),
     'L2_xattn_bv': (0.0, 0.1),
     'L2_xattn_bo': (0.0, 0.1),
     'L3_xattn_bq': (0.0, 1.337),
     'L3_xattn_bk': (0.0, 2.0),
     'L3_xattn_bv': (0.0, 0.467),
     'L3_xattn_bo': (0.0, 0.432)}
    factors = {'L0_xattn_Wq': 8.0,
     'L0_ffn_b1': 4.437,
     'L1_xattn_bp': 8.0,
     'L1_ffn_weight': 7.706,
     'L1_ffn_aux_weight1': 7.559,
     'L1_ffn_aux_weight2': 7.677,
     'L2_ffn_w_gate': 8.0,
     'L2_ffn_w_up': 8.0,
     'L2_ffn_w_down': 8.0,
     'L3_ffn_w_gate': 8.0,
     'L3_ffn_w_up': 8.0,
     'L3_ffn_w_down': 8.0}
    for name, (base, spread) in spreads.items():
        noise = np.random.default_rng([zlib.crc32(name.encode()), seed]).standard_normal(out[name].shape)
        drawn = base * np.exp(spread * noise) if base else spread * noise
        out[name] = jnp.asarray(drawn.astype(out[name].dtype))
    for name, factor in factors.items():
        out[name] = (out[name] * factor).astype(out[name].dtype)
    return out
```

```python
from contextlib import ExitStack

import concourse.bass as bass
from concourse import mybir

ALU = mybir.AluOpType
ACT = mybir.ActivationFunctionType
AX = mybir.AxisListType
F32 = mybir.dt.float32
BF16 = mybir.dt.bfloat16
U8 = mybir.dt.uint8

P = 128
B = 2
NT = 8
TPB = NT // B
EPS = 1e-5
RNE = 1.5 * 2.0 ** 23
MASKED = -3e38


class Steps:

    def __init__(self, engine, semaphore):
        self.engine, self.semaphore, self.made = engine, semaphore, 0

    def add(self, instruction):
        instruction.then_inc(self.semaphore, 1)
        self.made += 1

    def settle(self):
        self.engine.wait_ge(self.semaphore, self.made)


def build(nc, a, out):
    S = a["x"].shape[1]
    D = a["x"].shape[2]
    NC = a["ctx_1024"].shape[1]
    H0 = a["L0_xattn_Wq"].shape[1] // D
    NK = S + NC
    NCH = TPB + 1
    U0 = H0 * B
    SC0 = float(D) ** -0.5
    E, _, F1 = a["L0_ffn_W1"].shape
    FT = F1 // P
    SC1 = 16 ** -0.5
    HM = a["mask_Bx16xSxS2_bk1"].shape[1]
    DH = D // HM
    SC16 = float(DH) ** -0.5
    PK = 64
    LK = NC - PK
    NPAIR = HM // 2
    LH = HM // 2
    LP = LH * LK
    BK = HM // 4
    I2 = a["L2_ffn_w_gate"].shape[0]
    I3 = a["L3_ffn_w_gate"].shape[0]
    IT = 3
    rows2 = [P, P, I2 - 2 * P]
    assert LP <= P and I3 == IT * P
    assert D == P and S == TPB * P

    with ExitStack() as ctx:
        def sb(name, shape, dt=F32):
            return ctx.enter_context(nc.sbuf_tensor(name, shape, dt))

        def sem(name):
            return ctx.enter_context(nc.semaphore(name))

        bank = ctx.enter_context(nc.psum_tensor("bank", [P, 8, 512], F32))

        x = sb("x_residual", [P, NT, D])
        ident = sb("ident", [P, P])
        ones = sb("ones", [P, P])
        minus_half = sb("minus_half", [P, 16])
        xn = sb("xn", [P, NT, D])
        xnT = sb("xnT", [P, B, S])
        stats = sb("stats", [P, NT, 6])
        meanvar = sb("meanvar", [P, NT, 2])
        var_eps = sb("var_eps", [P, NT])
        rstd = sb("rstd", [P, NT])
        rstd_again = sb("rstd_again", [P, NT])

        ctx_tok = sb("ctx_tok", [NC, B, D])
        ctxT = sb("ctxT", [P, B, NC])
        ctx_stats = sb("ctx_stats", [NC, B, 6])
        ctx_meanvar = sb("ctx_meanvar", [NC, B, 2])
        ctx_var_eps = sb("ctx_var_eps", [NC, B])
        ctx_rstd = sb("ctx_rstd", [NC, B])
        ctx_norm = sb("ctx_norm", [NC, B, D])
        gamma_ctx = sb("gamma_ctx", [NC, D])
        beta_ctx = sb("beta_ctx", [NC, D])
        gamma_lat = sb("gamma_lat", [P, D])
        beta_lat = sb("beta_lat", [P, D])
        bo0 = sb("bo0", [P, D])
        out_bias0 = sb("out_bias0", [P, D])
        kvT = sb("kvT", [P, B, NK])

        VROWS = ["L0_xattn_bq", "bv0", "L0_ffn_b1", "L2_xattn_bq", "L2_xattn_bk", "L3_xattn_bq", "L3_xattn_bk",
                 "L2_xattn_bv", "L3_xattn_bv"]
        vsrc = {n: a[n] for n in VROWS if n != "bv0"}
        vsrc["bv0"] = a["L0_xattn_bkv"][H0 * D:]
        vsrc["L0_ffn_b1"] = a["L0_ffn_b1"].rearrange("e f -> (e f)")
        vrow, nrow = {}, 0
        for n in VROWS:
            k = vsrc[n].shape[0] // D
            vrow[n] = (nrow, k)
            nrow += k
        vec_rows = sb("vec_rows", [nrow, D])
        vec_cols = sb("vec_cols", [P, nrow])
        bq0_scaled = sb("bq0_scaled", [P, H0])
        bv0_wide = sb("bv0_wide", [P, 2, P])

        shared = sb("shared", [P, 4 * H0 * D + B * TPB * NK])
        wq0 = shared[:, 0:H0 * D]
        wkv0 = shared[:, H0 * D:3 * H0 * D]
        wo0 = shared[:, 3 * H0 * D:4 * H0 * D].rearrange("p (h d) -> p h d", h=H0)
        wT0 = sb("wT0", [P, 2, 3, P])
        ab0 = sb("ab0", [P, H0, 2 * P + 1])
        a_now = sb("a_now", [P, P])
        q_both = sb("q_both", [P, B, S])
        qT = [q_both[:, b, :] for b in range(B)]
        at = 4 * H0 * D
        prob = [shared[:, at + b * TPB * NK:at + (b + 1) * TPB * NK].rearrange("p (i k) -> p i k", i=TPB)
                for b in range(B)]
        probT = sb("probT", [P, NCH, S])
        uT = sb("uT", [P, S])
        neg_max = sb("neg_max", [P, B, TPB])
        row_sum = sb("row_sum", [P, B, TPB])
        row_inv = sb("row_inv", [P, B, TPB])

        w1 = sb("w1", [P, E, F1])
        w2 = sb("w2", [P, E, FT, D])
        w1_now = sb("w1_now", [P, 2, F1])
        wr = sb("wr", [P, E])
        br = sb("br", [P, E])
        b2 = sb("b2", [E, D])
        rank = sb("rank", [P, NT, E])
        logit = sb("logit", [P, NT, E])
        logit2 = sb("logit2", [P, NT, E])
        key = sb("key", [P, NT, E])
        pick = [sb(f"pick{i}", [P, NT, E]) for i in range(2)]
        top = [sb(f"top{i}", [P, NT]) for i in range(2)]
        top_key = sb("top_key", [P, NT])
        top_diff = sb("top_diff", [P, NT])
        top_exp = sb("top_exp", [P, NT])
        top_den = sb("top_den", [P, NT])
        top_w = [sb(f"top_w{i}", [P, NT]) for i in range(2)]
        gate = sb("gate", [P, NT, E])
        gateT = sb("gateT", [E, NT, P])
        hT = sb("hT", [P, 2, FT, B, S])

        l1w = sb("l1w", [P, 7, D])
        L1Q, L1K, L1V, L1P, L1F, L1A, L1B = range(7)
        bp1 = sb("bp1", [P, D])
        fbias1 = sb("fbias1", [P, D])
        l1T = sb("l1T", [P, 2, P])
        k1T = sb("k1T", [P, B, NC])
        kq1 = sb("kq1", [P, B, NC])
        v1 = sb("v1", [NC, B, D])
        wa1T = sb("wa1T", [P, P])
        waa1 = sb("waa1", [P, D])
        s1 = sb("s1", [P, NT, NC])
        neg_max1 = sb("neg_max1", [P, NT])
        sum1 = sb("sum1", [P, NT])
        inv1 = sb("inv1", [P, NT])
        p1T = sb("p1T", [NC, NT, P])
        turned = hT[:].rearrange("p a j b s -> p (a j b s)")[:, 0:B * S].rearrange("p (b s) -> p b s", b=B)
        tanh_in = sb("tanh_in", [P, NT, D])

        maskb = sb("maskb", [P, NT, HM * NC], U8)
        mask_neg = shared[:, 0:NT * HM * NC // 2].bitcast(BF16).rearrange("p (t n) -> p t n", t=NT)
        w16 = sb("w16", [P, 2, 4, D])
        WQ, WK, WV, WO = range(4)
        bo16 = sb("bo16", [P, 2, D])
        bq16 = sb("bq16", [P, 2])
        head_of_row = sb("head_of_row", [P, HM])
        half_of_row = sb("half_of_row", [P, 2])
        left_of_row = sb("left_of_row", [LP, LH])
        ctx_pair = sb("ctx_pair", [P, B, 2, PK])
        ctx_left = sb("ctx_left", [P, B, LH, LK])
        k16T = sb("k16T", [P, 2, B, NC])
        k_blocks = sb("k_blocks", [P, 2, B, HM, NC])
        v_pair = sb("v_pair", [P, 2, B, D])
        v_left = sb("v_left", [LP, 2, B, D])
        va_pair = sb("va_pair", [P, 2, B, NPAIR, 2, DH + 1])
        va_left = sb("va_left", [LP, 2, B, HM, DH + 1])
        q16T = q_both
        s16 = probT[:].rearrange("p c s -> p (c s)")[:, 0:2 * HM * NC].rearrange("p (z h k) -> p z h k", z=2, h=HM)
        neg_max16 = sb("neg_max16", [P, 2, HM])
        keep16 = sb("keep16", [P, 2, HM])
        spoil16 = sb("spoil16", [P, 2, HM])
        inv16 = sb("inv16", [P, 2, HM])
        p16 = hT[:].rearrange("p a j b s -> p (a j b s)")[:, 0:2 * HM * NC].rearrange("p (z n) -> p z n", z=2)
        p16T = w2[:].rearrange("p e j d -> p (e j) d")[:, 0:NPAIR + 2, :]
        o16 = kvT[:].rearrange("p b k -> p (b k)")[:, 0:NT * D].rearrange("p (t d) -> p t d", t=NT)

        def late(at, *dims):
            n = 1
            for d in dims:
                n *= d
            v = shared[:, at:at + n]
            return v.rearrange("p (i b s) -> p i b s", i=dims[0], b=dims[1]), at + n

        val, at = late(0, IT, B, S)
        val2, at = late(at, IT, B, S)
        tanh_out = shared[:, at:at + 2 * S].rearrange("p (n s) -> p n s", n=2)
        silu_in = shared[:, at + 2 * S:at + 3 * S]
        t3 = hT[:].rearrange("p a j b s -> p (a j b s)")[:, 0:IT * B * S].rearrange("p (i b s) -> p i b s", i=IT, b=B)
        w1_half = w1[:].rearrange("p e f -> p (e f)").bitcast(BF16)
        xqT = w1_half[:, 0:B * S].rearrange("p (b s) -> p b s", b=B)
        hq = w1_half[:, B * S:(1 + IT) * B * S].rearrange("p (i b s) -> p i b s", i=IT, b=B)
        wn2 = sb("wn2", [P, 3, IT * P])
        wmax2 = sb("wmax2", [P, 7])
        wscale2 = sb("wscale2", [P, 7])
        winv2 = sb("winv2", [P, 7])
        ab0_flat = ab0[:].rearrange("p h n -> p (h n)")
        w3T = ab0_flat[:, 0:3 * IT * P].rearrange("p (m n) -> p m n", m=3)
        w2T = ab0_flat[:, 3 * IT * P:3 * IT * P + 3 * IT * P // 2].bitcast(BF16).rearrange("p (m n) -> p m n", m=3)
        diag_down = sb("diag_down", [P, P])
        down_row = sb("down_row", [P, D])
        down_scale = sb("down_scale", [P, D])
        clip = sb("clip", [P, 2])
        clip_sig = sb("clip_sig", [P, 2])
        minus_rne = sb("minus_rne", [P, 1])
        plus_rne = sb("plus_rne", [P, 1])
        wn3 = sb("wn3", [P, 3 * IT * 4, 32])
        wmax3 = sb("wmax3", [P, 3 * IT * 4])
        wscale3 = sb("wscale3", [P, 3 * IT * 4])
        winv3 = sb("winv3", [P, 3 * IT * 4])
        pmax = sb("pmax", [P, 2])
        gmax_row = sb("gmax_row", [1, 2])
        unit_max = sb("unit_max", [P, 2, IT * B])
        x_scale = sb("x_scale", [P, 1])
        x_inv = sb("x_inv", [P, 1])
        h_scale = sb("h_scale", [P, 1])
        h_inv = sb("h_inv", [P, 1])
        c_gate = sb("c_gate", [P, IT])
        c_both = sb("c_both", [P, IT])
        ug_scale = sb("ug_scale", [P, 2])
        ug_inv = sb("ug_inv", [P, 2])
        half_sg = sb("half_sg", [P, 1])
        amax3 = sb("amax3", [P, 2])
        scale3 = sb("scale3", [P, 2])
        inv3 = sb("inv3", [P, 2])
        ratio3 = sb("ratio3", [P, 2])

        in_x = [sem("in_x0"), sem("in_x1")]
        in_ctx = sem("in_ctx")
        in_vec = sem("in_vec")
        in_norm = sem("in_norm")
        in_w0 = [sem(f"in_w0_{h}") for h in range(H0)]
        const_made = sem("const_made")
        ident_made = sem("ident_made")
        dve_step = sem("dve_step")
        act_step = sem("act_step")
        pool_step = sem("pool_step")
        ctx_var_ok = sem("ctx_var_ok")
        ctx_rstd_ok = sem("ctx_rstd_ok")
        ctx_norm_ok = sem("ctx_norm_ok")
        var_ok = sem("var_ok")
        rstd_ok = sem("rstd_ok")
        xn_ok = sem("xn_ok")
        xT_in_psum = sem("xT_in_psum")
        xnT_b_ok = [sem("xnT0_ok"), sem("xnT1_ok")]
        cT_in_psum = sem("cT_in_psum")
        cT_ok = sem("cT_ok")
        vcol_in_psum = sem("vcol_in_psum")
        vcol_ok = sem("vcol_ok")
        bv_wide_ok = sem("bv_wide_ok")
        bv_used = sem("bv_used")
        wT_in_psum = sem("wT_in_psum")
        wT_ok = sem("wT_ok")
        ab_in_psum = sem("ab_in_psum")
        ab_ok = sem("ab_ok")
        a_now_ok = sem("a_now_ok")
        bias0_ok = sem("bias0_ok")
        x_biased = sem("x_biased")
        q_in_psum = sem("q_in_psum")
        q_ok = sem("q_ok")
        scores_ok = sem("scores_ok")
        max_ok = sem("max_ok")
        prob_ok = sem("prob_ok")
        pT_in_psum = sem("pT_in_psum")
        pT_act_ok = sem("pT_act_ok")
        pT_dve_ok = sem("pT_dve_ok")
        u_in_psum = sem("u_in_psum")
        u_ok = sem("u_ok")
        o_in_psum = sem("o_in_psum")
        inv_ok = sem("inv_ok")
        o_added = sem("o_added")
        in_moe = sem("in_moe")
        in_l1 = sem("in_l1")
        rank_ok = sem("rank_ok")
        w1_now_ok = sem("w1_now_ok")
        logit_in_psum = sem("logit_in_psum")
        diff_ok = sem("diff_ok")
        top_exp_ok = sem("top_exp_ok")
        gate_ok = sem("gate_ok")
        gT_in_psum = sem("gT_in_psum")
        gT_ok = sem("gT_ok")
        b2_in_psum = sem("b2_in_psum")
        b2_added = sem("b2_added")
        h_in_psum = sem("h_in_psum")
        h_ok = sem("h_ok")
        y_in_psum = sem("y_in_psum")
        y_added = sem("y_added")
        l1_in_psum = sem("l1_in_psum")
        l1_ok = sem("l1_ok")
        s1_in_psum = sem("s1_in_psum")
        s1_ok = sem("s1_ok")
        p1_ok = sem("p1_ok")
        p1T_in_psum = sem("p1T_in_psum")
        p1T_ok = sem("p1T_ok")
        o1_in_psum = sem("o1_in_psum")
        turned_ok = sem("turned_ok")
        res_in_psum = sem("res_in_psum")
        tanh_in_ok = sem("tanh_in_ok")
        tanh_ok = sem("tanh_ok")
        x_done = sem("x_done")
        in_mask = sem("in_mask")
        in_l16 = [sem("in_l2_attention"), sem("in_l3_attention")]
        in_f2 = sem("in_f2")
        in_f3 = sem("in_f3")
        mask_neg_ok = sem("mask_neg_ok")
        vcol_used = sem("vcol_used")
        ctx_spread = sem("ctx_spread")
        kv16_in_psum = sem("kv16_in_psum")
        kv16_ok = sem("kv16_ok")
        kv16_spread = sem("kv16_spread")
        q16_in_psum = sem("q16_in_psum")
        q16_ok = sem("q16_ok")
        s16_in_psum = sem("s16_in_psum")
        s16_taken = sem("s16_taken")
        s16_ok = sem("s16_ok")
        max16_ok = sem("max16_ok")
        spoil16_ok = sem("spoil16_ok")
        p16_ok = sem("p16_ok")
        p16T_in_psum = sem("p16T_in_psum")
        p16T_ok = sem("p16T_ok")
        o16_in_psum = sem("o16_in_psum")
        o16_ok = sem("o16_ok")
        o16T_in_psum = sem("o16T_in_psum")
        o16T_ok = sem("o16T_ok")
        rne_made = sem("rne_made")
        clip_tanh_ok = sem("clip_tanh_ok")
        wmax_ok = sem("wmax_ok")
        wq2_ok = sem("wq2_ok")
        wq3_ok = sem("wq3_ok")
        w2T_in_psum = sem("w2T_in_psum")
        w2T_ok = sem("w2T_ok")
        w3T_in_psum = sem("w3T_in_psum")
        w3T_ok = sem("w3T_ok")
        xq_ok = sem("xq_ok")
        pmax_ok = sem("pmax_ok")
        pmaxT_in_psum = sem("pmaxT_in_psum")
        gmax_ok = sem("gmax_ok")
        gmax_in_psum = sem("gmax_in_psum")
        c_ok = sem("c_ok")
        gu_in_psum = sem("gu_in_psum")
        gu_tanh_ok = sem("gu_tanh_ok")
        gu_taken = sem("gu_taken")
        hscale_ok = sem("hscale_ok")
        h_rounded = sem("h_rounded")
        hq_ok = sem("hq_ok")
        ug_in_psum = sem("ug_in_psum")
        ug_copied = sem("ug_copied")
        ug_maxed = sem("ug_maxed")
        ug_scale_ok = sem("ug_scale_ok")
        gate_int_ok = sem("gate_int_ok")
        up_int_ok = sem("up_int_ok")
        tanh3_ok = sem("tanh3_ok")
        o3_ok = sem("o3_ok")
        x_final = sem("x_final")
        out_done = sem("out_done")

        block = ctx.enter_context(nc.Block())

        ACT_CHUNKS = (1, 3)
        DVE_CHUNKS = (0, 2, 4)
        PT_BANK = (4, 5, 4, 5, 4)

        def chunk_keys(c):
            return P if c < TPB else NC

        def ready_chunk(eng, u, c):
            if c in ACT_CHUNKS:
                eng.wait_ge(pT_act_ok, len(ACT_CHUNKS) * u + ACT_CHUNKS.index(c) + 1)
            else:
                eng.wait_ge(pT_dve_ok, len(DVE_CHUNKS) * u + DVE_CHUNKS.index(c) + 1)

        @block.sync
        def _(sp):
            xs = a["x"].rearrange("b (t p) d -> b p t d", p=P)
            sp.dma_start(ctx_tok[:], a["ctx_1024"].rearrange("b k d -> k b d")).then_inc(in_ctx, 16)
            for b in range(B):
                sp.dma_start(x[:, TPB * b:TPB * (b + 1), :], xs[b]).then_inc(in_x[b], 16)
            for h in range(H0):
                c = slice(h * D, (h + 1) * D)
                v = slice((H0 + h) * D, (H0 + h + 1) * D)
                sp.dma_start(wq0[:, c], a["L0_xattn_Wq"][:, c]).then_inc(in_w0[h], 16)
                sp.dma_start(wkv0[:, c], a["L0_xattn_Wkv"][:, c]).then_inc(in_w0[h], 16)
                sp.dma_start(wkv0[:, v], a["L0_xattn_Wkv"][:, v]).then_inc(in_w0[h], 16)
                sp.dma_start(wo0[:, h, :], a["L0_xattn_Wo"][c, :]).then_inc(in_w0[h], 16)
            sp.dma_start(w1[:], a["L0_ffn_W1"].rearrange("e h f -> h e f")).then_inc(in_moe, 16)
            sp.dma_start(w2[:], a["L0_ffn_W2"].rearrange("e (j p) o -> p e j o", p=P)).then_inc(in_moe, 16)
            sp.dma_start(wr[:], a["L0_ffn_Wr"]).then_inc(in_moe, 16)
            sp.dma_start(br[:], a["L0_ffn_br"].partition_broadcast(P)).then_inc(in_moe, 16)
            sp.dma_start(b2[:], a["L0_ffn_b2"]).then_inc(in_moe, 16)
            for n, name in ((L1Q, "xattn_Wq"), (L1K, "xattn_Wk"), (L1V, "xattn_Wv"), (L1P, "xattn_Wp"),
                            (L1F, "ffn_weight"), (L1A, "ffn_aux_weight1"), (L1B, "ffn_aux_weight2")):
                sp.dma_start(l1w[:, n, :], a["L1_" + name]).then_inc(in_l1, 16)
            sp.dma_start(bp1[:], a["L1_xattn_bp"].partition_broadcast(P)).then_inc(in_l1, 16)
            sp.dma_start(fbias1[:], a["L1_ffn_bias"].partition_broadcast(P)).then_inc(in_l1, 16)
            for n in range(2):
                for m, name in enumerate(("Wq", "Wk", "Wv", "Wo")):
                    sp.dma_start(w16[:, n, m, :], a[f"L{n + 2}_xattn_{name}"]).then_inc(in_l16[n], 16)
                sp.dma_start(bo16[:, n, :], a[f"L{n + 2}_xattn_bo"].partition_broadcast(P)).then_inc(in_l16[n], 16)
            for m, name in enumerate(("gate", "up")):
                w = a["L2_ffn_w_" + name]
                sp.dma_start(wn2[:, m, 0:2 * P].rearrange("p (i d) -> p i d", i=2),
                             w[0:2 * P, :].rearrange("(i p) d -> p i d", p=P)).then_inc(in_f2, 16)
                sp.dma_start(wn2[0:rows2[2], m, 2 * P:3 * P], w[2 * P:I2, :]).then_inc(in_f2, 16)
                sp.dma_start(wn3[:, 4 * IT * m:4 * IT * (m + 1), :].rearrange("p (i b) k -> p i (b k)", i=IT),
                             a["L3_ffn_w_" + name].rearrange("(i p) d -> p i d", p=P)).then_inc(in_f3, 16)
            sp.dma_start(wn2[:, 2, 0:I2], a["L2_ffn_w_down"]).then_inc(in_f2, 16)
            sp.dma_start(wn3[:, 8 * IT:12 * IT, :].rearrange("p b k -> p (b k)"), a["L3_ffn_w_down"]).then_inc(in_f3, 16)
            sp.dma_start(clip[:, 0:1], a["L2_ffn_clip_x"].partition_broadcast(P)).then_inc(in_f2, 16)
            sp.dma_start(clip[:, 1:2], a["L2_ffn_clip_down"].partition_broadcast(P)).then_inc(in_f2, 16)
            for t in range(NT):
                b, i = t // TPB, t % TPB
                sp.dma_start(maskb[:, t, :].rearrange("p (h k) -> p h k", h=HM),
                             a["mask_Bx16xSxS2_bk1"][b, :, i * P:(i + 1) * P, :].rearrange("h p k -> p h k"))\
                    .then_inc(in_mask, 16)
            sp.wait_ge(x_final, 1)
            sp.dma_start(out.rearrange("b (t p) d -> p b t d", p=P),
                         x[:].rearrange("p (b t) d -> p b t d", b=B)).then_inc(out_done, 16)
            sp.wait_ge(out_done, 16)

        @block.gpsimd
        def _(pool):
            own = Steps(pool, pool_step)
            nc.gpsimd.memset(ones[:], 1.0).then_inc(const_made, 1)
            nc.gpsimd.memset(minus_half[:], -0.5).then_inc(const_made, 1)
            own.add(nc.gpsimd.memset(ident[:], 0.0))
            own.settle()
            nc.gpsimd.affine_select(out=ident[:], in_=ident[:], compare_op=ALU.not_equal, fill=1.0, base=0,
                                    pattern=[[-1, P]], channel_multiplier=1).then_inc(ident_made, 1)
            pool.wait_ge(const_made, 2)
            pool.wait_ge(ctx_var_ok, 1)
            nc.gpsimd.tensor_tensor(ctx_rstd[:], ctx_var_eps[:], minus_half[0:NC, 0:B], ALU.pow).then_inc(ctx_rstd_ok, 1)
            pool.wait_ge(var_ok, 1)
            own.add(nc.gpsimd.tensor_tensor(rstd[:], var_eps[:], minus_half[:, 0:NT], ALU.pow))
            own.settle()
            own.add(nc.gpsimd.tensor_tensor(rstd_again[:], rstd[:], rstd[:], ALU.mult))
            own.settle()
            own.add(nc.gpsimd.tensor_tensor(rstd_again[:], rstd_again[:], meanvar[:, :, 1], ALU.mult))
            own.settle()
            own.add(nc.gpsimd.tensor_scalar(rstd_again[:], rstd_again[:], EPS, None, ALU.add))
            own.settle()
            own.add(nc.gpsimd.tensor_tensor(rstd_again[:], rstd_again[:], minus_half[:, 0:NT], ALU.pow))
            own.settle()
            nc.gpsimd.tensor_tensor(rstd[:], rstd[:], rstd_again[:], ALU.mult).then_inc(rstd_ok, 1)
            pool.wait_ge(vcol_ok, 1)
            col = vrow["bv0"][0]
            for h in range(H0):
                if h >= 2:
                    pool.wait_ge(bv_used, h - 1)
                nc.gpsimd.tensor_scalar(bv0_wide[:, h % 2, :], ones[:], vec_cols[:, col + h:col + h + 1], None,
                                        ALU.mult).then_inc(bv_wide_ok, 1)
            pool.wait_ge(bias0_ok, 1)
            pool.wait_ge(xn_ok, NT)
            nc.gpsimd.tensor_tensor(x[:], x[:], out_bias0[:].unsqueeze(1).to_broadcast([P, NT, D]), ALU.add)\
                .then_inc(x_biased, 1)
            nc.gpsimd.memset(plus_rne[:], RNE).then_inc(rne_made, 1)
            nc.gpsimd.memset(minus_rne[:], -RNE).then_inc(rne_made, 1)
            for tile, width, count in ((head_of_row, DH, HM), (half_of_row, PK, 2), (left_of_row, LK, LH)):
                own.add(nc.gpsimd.memset(tile[:], 1.0))
                own.settle()
                own.add(nc.gpsimd.affine_select(out=tile[:], in_=tile[:], compare_op=ALU.is_ge, fill=0.0, base=0,
                                                pattern=[[-width, count]], channel_multiplier=1))
                own.settle()
                own.add(nc.gpsimd.affine_select(out=tile[:], in_=tile[:], compare_op=ALU.is_ge, fill=0.0,
                                                base=width - 1, pattern=[[width, count]], channel_multiplier=-1))
                own.settle()
            pool.wait_ge(cT_ok, 2)
            nc.gpsimd.tensor_copy(ctx_pair[:], ctxT[:, :, 0:PK].unsqueeze(2).to_broadcast([P, B, 2, PK]))\
                .then_inc(ctx_spread, 1)
            nc.gpsimd.tensor_copy(ctx_left[:], ctxT[:, :, PK:NC].unsqueeze(2).to_broadcast([P, B, LH, LK]))\
                .then_inc(ctx_spread, 1)
            for e in range(E):
                nc.gpsimd.memset(rank[:, :, e:e + 1], float(E - e)).then_inc(rank_ok, 1)

            def inverse_root(k):
                pool.wait_ge(var_ok, k + 1)
                nc.gpsimd.tensor_tensor(rstd[:], var_eps[:], minus_half[:, 0:NT], ALU.pow).then_inc(rstd_ok, 1)

            def add_bias(k, bias):
                pool.wait_ge(xn_ok, NT * (k + 1))
                nc.gpsimd.tensor_tensor(x[:], x[:], bias.unsqueeze(1).to_broadcast([P, NT, D]), ALU.add)\
                    .then_inc(x_biased, 1)

            def whole_weights2():
                pool.wait_ge(wmax_ok, 1)
                for m in range(2):
                    for i in range(IT):
                        w, r = wn2[0:rows2[i], m, i * P:(i + 1) * P], rows2[i]
                        own.add(nc.gpsimd.tensor_scalar(w, w, winv2[0:r, IT * m + i:IT * m + i + 1], RNE, ALU.mult, ALU.add))
                w = wn2[:, 2, 0:I2]
                own.add(nc.gpsimd.tensor_scalar(w, w, winv2[:, 6:7], RNE, ALU.mult, ALU.add))
                own.settle()
                for m in range(2):
                    for i in range(IT):
                        w = wn2[0:rows2[i], m, i * P:(i + 1) * P]
                        nc.gpsimd.tensor_scalar(w, w, -RNE, None, ALU.add).then_inc(wq2_ok, 1)
                w = wn2[:, 2, 0:I2]
                nc.gpsimd.tensor_scalar(w, w, -RNE, None, ALU.add).then_inc(wq2_ok, 1)
                nc.gpsimd.tensor_scalar(diag_down[:], ident[:], wscale2[:, 6:7], None, ALU.mult).then_inc(wq2_ok, 1)

            def whole_weights3(m):
                pool.wait_ge(wmax_ok, 2)
                w, c = wn3[:, 4 * IT * m:4 * IT * (m + 1), :], slice(4 * IT * m, 4 * IT * (m + 1))
                own.add(nc.gpsimd.tensor_tensor(w, w, winv3[:, c].unsqueeze(2).to_broadcast([P, 4 * IT, 32]), ALU.mult))
                own.settle()
                own.add(nc.gpsimd.tensor_scalar(w, w, RNE, None, ALU.add))
                own.settle()
                own.add(nc.gpsimd.tensor_scalar(w, w, -RNE, None, ALU.add))
                own.settle()
                nc.gpsimd.tensor_tensor(w, w, wscale3[:, c].unsqueeze(2).to_broadcast([P, 4 * IT, 32]), ALU.mult)\
                    .then_inc(wq3_ok, 1)

            for h in range(H0):
                pool.wait_ge(ab_ok, h + 1)
                if h >= 1:
                    pool.wait_ge(q_in_psum, B * h)
                nc.gpsimd.tensor_copy(a_now[:], ab0[:, h, 0:P]).then_inc(a_now_ok, 1)
                if h == 3:
                    whole_weights2()
                if h in (4, 5, 6):
                    whole_weights3(h - 4)
            def spread_kv(n):
                pool.wait_ge(kv16_ok, 3 * (n + 1))
                for b in range(B):
                    nc.gpsimd.tensor_tensor(k_blocks[:, n, b], k16T[:, n, b, :].unsqueeze(1).to_broadcast([P, HM, NC]),
                                            head_of_row[:].unsqueeze(2).to_broadcast([P, HM, NC]), ALU.mult)\
                        .then_inc(kv16_spread, 1)
                    half = half_of_row[:].unsqueeze(1)
                    for hd in range(2):
                        nc.gpsimd.tensor_scalar(va_pair[:, n, b, :, hd, 0:DH],
                                                v_pair[:, n, b, :].rearrange("p (c h d) -> p c h d", c=NPAIR, h=2)[:, :, hd, :],
                                                half_of_row[:, hd:hd + 1], None, ALU.mult).then_inc(kv16_spread, 1)
                    nc.gpsimd.tensor_copy(va_pair[:, n, b, :, :, DH], half.to_broadcast([P, NPAIR, 2]))\
                        .then_inc(kv16_spread, 1)
                    for g in range(2):
                        nc.gpsimd.tensor_tensor(va_left[:, n, b, LH * g:LH * (g + 1), 0:DH],
                                                v_left[:, n, b, LH * DH * g:LH * DH * (g + 1)].rearrange("p (h d) -> p h d", h=LH),
                                                left_of_row[:].unsqueeze(2).to_broadcast([LP, LH, DH]), ALU.mult)\
                            .then_inc(kv16_spread, 1)
                        nc.gpsimd.tensor_copy(va_left[:, n, b, LH * g:LH * (g + 1), DH], left_of_row[:])\
                            .then_inc(kv16_spread, 1)

            pool.wait_ge(in_moe, 16 * 5)
            inverse_root(1)
            for e in range(E):
                if e >= 2:
                    pool.wait_ge(h_in_psum, FT * B * (e - 1))
                nc.gpsimd.tensor_copy(w1_now[:, e % 2, :], w1[:, e, :]).then_inc(w1_now_ok, 1)
                pool.wait_ge(in_mask, 16 * NT)
                pool.wait_ge(o_in_psum, U0)
                nc.gpsimd.tensor_scalar(mask_neg[:, e, :], maskb[:, e, :], MASKED, None, ALU.mult)\
                    .then_inc(mask_neg_ok, 1)
            inverse_root(2)
            pool.wait_ge(in_l1, 16 * 9)
            add_bias(2, bp1[:])
            spread_kv(0)
            inverse_root(3)
            spread_kv(1)
            inverse_root(4)
            add_bias(4, bo16[:, 0, :])
            for t in range(NT):
                spoil = spoil16[:, t % 2, :]
                pool.wait_ge(max16_ok, t + 1)
                if t >= 2:
                    pool.wait_ge(o16_ok, t - 1)
                own.add(nc.gpsimd.tensor_scalar(keep16[:, t % 2, :], neg_max16[:, t % 2, :], 1e37, None, ALU.is_lt))
                own.settle()
                own.add(nc.gpsimd.tensor_scalar(spoil, keep16[:, t % 2, :], -1.0, 3e38, ALU.add, ALU.mult))
                own.settle()
                own.add(nc.gpsimd.tensor_scalar(spoil, spoil, 3e38, None, ALU.mult))
                own.settle()
                nc.gpsimd.tensor_tensor(spoil, spoil, keep16[:, t % 2, :], ALU.mult).then_inc(spoil16_ok, 1)
            inverse_root(5)
            inverse_root(6)
            add_bias(6, bo16[:, 1, :])
            inverse_root(7)
            pool.wait_ge(ug_scale_ok, 1)
            pool.wait_ge(ug_copied, 2 * IT * B)
            for b in range(B):
                own.add(nc.gpsimd.tensor_scalar(val[:, :, b, :], val[:, :, b, :], ug_inv[:, 1:2], RNE, ALU.mult, ALU.add))
                own.settle()
                nc.gpsimd.tensor_scalar(val[:, :, b, :], val[:, :, b, :], -RNE, None, ALU.add).then_inc(up_int_ok, 1)

        @block.tensor
        def _(pe):
            pe.wait_ge(in_vec, 16 * len(VROWS))
            pe.wait_ge(ident_made, 1)
            nc.tensor.transpose(bank[:, 6, 0:nrow], vec_rows[:], ident[0:nrow, 0:nrow]).then_inc(vcol_in_psum, 1)
            pe.wait_ge(vcol_ok, 4)
            for h in range(H0):
                c = slice(h * D, (h + 1) * D)
                v = slice((H0 + h) * D, (H0 + h + 1) * D)
                tb, rb = h % 2, 2 + h % 2
                pe.wait_ge(in_w0[h], 64)
                if h >= 2:
                    pe.wait_ge(wT_ok, h - 1)
                for n, w in enumerate((wq0[:, c], wkv0[:, c], wkv0[:, v])):
                    last = nc.tensor.transpose(bank[:, tb, n * P:(n + 1) * P], w, ident[:])
                last.then_inc(wT_in_psum, 1)
                pe.wait_ge(wT_ok, h + 1)
                if h >= 2:
                    pe.wait_ge(ab_ok, h - 1)
                nc.tensor.matmul(bank[:, rb, 0:P], wT0[:, h % 2, 0, :], wT0[:, h % 2, 1, :], start=True, stop=True)
                nc.tensor.matmul(bank[:, rb, P:2 * P], wT0[:, h % 2, 2, :], wo0[:, h, :], start=True, stop=True)
                nc.tensor.matmul(bank[:, rb, 2 * P:2 * P + 1], wT0[:, h % 2, 1, :], bq0_scaled[:, h:h + 1],
                                 start=True, stop=True).then_inc(ab_in_psum, 1)
                pe.wait_ge(bv_wide_ok, h + 1)
                nc.tensor.matmul(bank[:, 7, 0:D], bv0_wide[:, h % 2, :], wo0[:, h, :],
                                 start=(h == 0), stop=(h == H0 - 1)).then_inc(bv_used, 1)
            pe.wait_ge(ctx_norm_ok, 1)
            for b in range(B):
                nc.tensor.transpose(bank[:, 6, b * P:b * P + NC], ctx_norm[:, b, :], ident[0:NC, 0:NC])
            for b in range(B):
                last = nc.tensor.transpose(bank[:, 6, (B + b) * P:(B + b) * P + NC], ctx_tok[:, b, :], ident[0:NC, 0:NC])
            last.then_inc(cT_in_psum, 1)
            for t in range(NT):
                pe.wait_ge(xn_ok, t + 1)
                nc.tensor.transpose(bank[:, 4 + t // TPB, (t % TPB) * P:(t % TPB + 1) * P], xn[:, t, :], ident[:])\
                    .then_inc(xT_in_psum, 1)

            def query(u):
                h, b = u // B, u % B
                pe.wait_ge(a_now_ok, h + 1)
                if u >= 3:
                    pe.wait_ge(o_added, u - 2)
                else:
                    pe.wait_ge(bias0_ok, 1)
                if u >= 1:
                    pe.wait_ge(q_ok, u)
                pe.wait_ge(xnT_b_ok[b], 1)
                nc.tensor.matmul(bank[:, 7, :], a_now[:], kvT[:, b, 0:S], start=True, stop=True).then_inc(q_in_psum, 1)

            def scores(u, i):
                b, first = u % B, 2 * (i % 2)
                if i == 0:
                    pe.wait_ge(q_ok, u + 1)
                    pe.wait_ge(cT_ok, B)
                n = TPB * u + i
                if n >= 2:
                    pe.wait_ge(prob_ok, n - 1)
                else:
                    pe.wait_ge(ab_ok, H0)
                q = qT[b][:, i * P:(i + 1) * P]
                nc.tensor.matmul(bank[:, first, :], q, kvT[:, b, 0:S], start=True, stop=True)
                nc.tensor.matmul(bank[:, first + 1, 0:NC], q, kvT[:, b, S:NK], start=True, stop=True)\
                    .then_inc(scores_ok, 1)

            def transpose_chunk(u, c):
                b, n = u % B, chunk_keys(c)
                pe.wait_ge(prob_ok, TPB * (u + 1))
                if c >= 2:
                    ready_chunk(pe, u, c - 2)
                elif u >= 1:
                    ready_chunk(pe, u - 1, (4, 3)[c])
                for i in range(TPB):
                    last = nc.tensor.transpose(bank[0:n, PT_BANK[c], i * P:(i + 1) * P],
                                               prob[b][:, i, c * P:c * P + n], ident[:])
                last.then_inc(pT_in_psum, 1)

            def attend(u, c):
                b, n = u % B, chunk_keys(c)
                ready_chunk(pe, u, c)
                if c == 0:
                    if u:
                        pe.wait_ge(u_ok, u)
                    else:
                        pe.wait_ge(cT_ok, B)
                kv = xn[:, TPB * b + c, :] if c < TPB else ctx_norm[:, b, :]
                mm = nc.tensor.matmul(bank[:, 6, :], kv, probT[0:n, c, :], start=(c == 0), stop=(c == NCH - 1))
                if c == NCH - 1:
                    mm.then_inc(u_in_psum, 1)

            def output(u):
                h = u // B
                pe.wait_ge(u_ok, u + 1)
                pe.wait_ge(q_ok, min(u + 3, U0))
                if u >= 1:
                    pe.wait_ge(o_added, u)
                for i in range(TPB):
                    last = nc.tensor.matmul(bank[:, 7, i * P:(i + 1) * P], uT[:, i * P:(i + 1) * P], ab0[:, h, P:2 * P],
                                            start=True, stop=True)
                last.then_inc(o_in_psum, 1)

            query(0)
            for u in range(U0 + 2):
                s, p, o = u < U0, 1 <= u <= U0, u >= 2
                if s:
                    scores(u, 0)
                if o:
                    output(u - 2)
                if p:
                    transpose_chunk(u - 1, 0)
                    transpose_chunk(u - 1, 1)
                if s:
                    scores(u, 1)
                if p:
                    attend(u - 1, 0)
                    transpose_chunk(u - 1, 2)
                if s:
                    scores(u, 2)
                    if u + 1 < U0:
                        query(u + 1)
                if p:
                    attend(u - 1, 1)
                    transpose_chunk(u - 1, 3)
                    attend(u - 1, 2)
                if s:
                    scores(u, 3)
                if p:
                    transpose_chunk(u - 1, 4)
                    attend(u - 1, 3)
                    attend(u - 1, 4)

            def norm_transposes(k, quantised=None):
                for t in range(NT):
                    if quantised is None:
                        pe.wait_ge(xn_ok, NT * k + t + 1)
                    else:
                        pe.wait_ge(xq_ok, B * quantised + t // TPB + 1)
                    nc.tensor.transpose(bank[:, 4 + t // TPB, (t % TPB) * P:(t % TPB + 1) * P], xn[:, t, :], ident[:])\
                        .then_inc(xT_in_psum, 1)

            def tile_T(t):
                return xnT[:, t // TPB, (t % TPB) * P:(t % TPB + 1) * P]

            def normed(k):
                for b in range(B):
                    pe.wait_ge(xnT_b_ok[b], k + 1)

            pe.wait_ge(in_l1, 16 * 9)
            pe.wait_ge(o_added, U0)
            pe.wait_ge(prob_ok, TPB * U0)
            both = ctxT[:].rearrange("p b k -> p (b k)")
            nc.tensor.transpose(bank[:, 0, 0:P], l1w[:, L1Q, :], ident[:])
            nc.tensor.transpose(bank[:, 0, P:2 * P], l1w[:, L1F, :], ident[:])
            nc.tensor.matmul(bank[:, 1, 0:B * NC], l1w[:, L1K, :], both, start=True, stop=True)
            for b in range(B):
                last = nc.tensor.matmul(bank[0:NC, 2, b * D:(b + 1) * D], ctxT[:, b, :], l1w[:, L1V, :],
                                        start=True, stop=True)
            last.then_inc(l1_in_psum, 1)
            pe.wait_ge(l1_ok, 3)
            nc.tensor.matmul(bank[:, 3, 0:B * NC], l1T[:, 0, :], k1T[:].rearrange("p b k -> p (b k)"),
                             start=True, stop=True)
            nc.tensor.matmul(bank[:, 3, 256:256 + P], l1w[:, L1A, :], l1T[:, 1, :], start=True, stop=True)\
                .then_inc(l1_in_psum, 1)
            pe.wait_ge(l1_ok, 5)
            nc.tensor.matmul(bank[:, 0, 0:D], wa1T[:], l1w[:, L1B, :], start=True, stop=True).then_inc(l1_in_psum, 1)
            pe.wait_ge(l1_ok, 6)

            norm_transposes(1)
            normed(1)
            pe.wait_ge(in_moe, 16 * 5)
            for t in range(NT):
                last = nc.tensor.matmul(bank[:, 6, t * E:(t + 1) * E], tile_T(t), wr[:], start=True, stop=True)
            last.then_inc(logit_in_psum, 1)

            def hidden(e):
                pe.wait_ge(w1_now_ok, e + 1)
                for j in range(FT):
                    for b in range(B):
                        n = j * B + b
                        if e >= 1:
                            pe.wait_ge(h_ok, FT * B * (e - 1) + n + 1)
                        nc.tensor.matmul(bank[:, n, :], w1_now[:, e % 2, j * P:(j + 1) * P], xnT[:, b, :],
                                         start=True, stop=True).then_inc(h_in_psum, 1)

            def expert_out(e):
                pe.wait_ge(h_ok, FT * B * (e + 1))
                for b in range(B):
                    if e >= 1:
                        pe.wait_ge(y_added, B * (e - 1) + b + 1)
                    else:
                        pe.wait_ge(b2_added, b + 1)
                    for i in range(TPB):
                        for j in range(FT):
                            last = nc.tensor.matmul(bank[:, 6 + b, i * P:(i + 1) * P],
                                                    hT[:, e % 2, j, b, i * P:(i + 1) * P], w2[:, e, j, :],
                                                    start=(j == 0), stop=(j == FT - 1))
                    last.then_inc(y_in_psum, 1)

            hidden(0)
            pe.wait_ge(gate_ok, 1)
            for t in range(NT):
                last = nc.tensor.transpose(bank[0:E, 4 + t // TPB, (t % TPB) * P:(t % TPB + 1) * P],
                                           gate[:, t, :], ident[:])
            last.then_inc(gT_in_psum, 1)
            hidden(1)
            pe.wait_ge(gT_ok, 1)
            for t in range(NT):
                last = nc.tensor.matmul(bank[:, 6 + t // TPB, (t % TPB) * P:(t % TPB + 1) * P], gateT[:, t, :], b2[:],
                                        start=True, stop=True)
            last.then_inc(b2_in_psum, 1)
            expert_out(0)
            for e in range(2, E):
                hidden(e)
                expert_out(e - 1)
            expert_out(E - 1)

            def residual_out(k, weight):
                for b in range(B):
                    for i in range(TPB):
                        last = nc.tensor.matmul(bank[:, 6 + b, i * P:(i + 1) * P], weight[0](TPB * b + i), weight[1],
                                                start=True, stop=True)
                    last.then_inc(res_in_psum, 1)

            def keys_values(n):
                pe.wait_ge(in_l16[n], 80)
                pe.wait_ge(ctx_spread, 2)
                pe.wait_ge(s1_ok, B * n) if n else pe.wait_ge(h_ok, FT * B * E)
                nc.tensor.matmul(bank[:, 0, 0:B * NC], w16[:, n, WK, :], ctxT[:].rearrange("p b k -> p (b k)"),
                                 start=True, stop=True)
                for b in range(B):
                    nc.tensor.matmul(bank[:, 1, b * D:(b + 1) * D], ctx_pair[:, b].rearrange("p n k -> p (n k)"),
                                     w16[:, n, WV, :], start=True, stop=True)
                for b in range(B):
                    last = nc.tensor.matmul(bank[0:LP, 1, (B + b) * D:(B + b + 1) * D],
                                            ctx_left[:, b].rearrange("p n k -> p (n k)"), w16[:, n, WV, :],
                                            start=True, stop=True)
                last.then_inc(kv16_in_psum, 1)

            def global_max(j, count):
                pe.wait_ge(pmax_ok, j + 1)
                for c in range(count):
                    last = nc.tensor.transpose(bank[0:1, 7, c * P:(c + 1) * P], pmax[:, c:c + 1], ident[:])
                last.then_inc(pmaxT_in_psum, 1)
                pe.wait_ge(gmax_ok, j + 1)
                nc.tensor.matmul(bank[:, 7, 2 * P:2 * P + count], ones[0:1, :], gmax_row[:, 0:count],
                                 start=True, stop=True).then_inc(gmax_in_psum, 1)

            def attention16(n, k):
                norm_transposes(k)
                normed(k)
                for b in range(B):
                    nc.tensor.matmul(bank[:, 6 + b, :], w16[:, n, WQ, :], xnT[:, b, :], start=True, stop=True)\
                        .then_inc(q16_in_psum, 1)
                pe.wait_ge(kv16_spread, 14 * (n + 1))
                for t in range(NT + 1):
                    if t < NT:
                        b, m = t // TPB, NT * n + t
                        pe.wait_ge(q16_ok, B * n + b + 1)
                        if t:
                            pe.wait_ge(s16_taken if n == 0 else s16_ok, m)
                        q = q16T[:, b, (t % TPB) * P:(t % TPB + 1) * P]
                        for g in range(4):
                            last = nc.tensor.matmul(bank[:, g, 0:BK * NC], q,
                                                    k_blocks[:, n, b, BK * g:BK * (g + 1), :].rearrange("p h k -> p (h k)"),
                                                    start=True, stop=True)
                        last.then_inc(s16_in_psum, 1)
                    if t:
                        b, m, z = (t - 1) // TPB, NT * n + t - 1, (t - 1) % 2
                        pe.wait_ge(p16_ok, 2 * (m + 1))
                        if t >= 2:
                            pe.wait_ge(p16T_ok, 2 * m)
                        else:
                            pe.wait_ge(q16_ok, B * (n + 1))
                        for c in range(NPAIR):
                            last = nc.tensor.transpose(bank[:, 4 + c // 4, (c % 4) * P:(c % 4 + 1) * P],
                                                       p16[:, z, 2 * PK * c:2 * PK * (c + 1)], ident[:])
                        last.then_inc(p16T_in_psum, 1)
                        for g in range(2):
                            first = HM * PK + LP * g
                            last = nc.tensor.transpose(bank[0:LP, 6, g * P:(g + 1) * P], p16[:, z, first:first + LP],
                                                       ident[:])
                        last.then_inc(p16T_in_psum, 1)
                        pe.wait_ge(p16T_ok, 2 * m + 2)
                        if m >= 1:
                            pe.wait_ge(o16_ok, m)
                        o, w = bank[:, 7, z * 256:z * 256 + HM * (DH + 1)], DH + 1
                        for g in range(2):
                            nc.tensor.matmul(o[:, LH * w * g:LH * w * (g + 1)], p16T[0:LP, NPAIR + g, :],
                                             va_left[:, n, b, LH * g:LH * (g + 1), :].rearrange("p h d -> p (h d)"),
                                             start=(g == 0), stop=False, skip_group_check=True)
                        for c in range(NPAIR):
                            last = nc.tensor.matmul(o[:, 2 * w * c:2 * w * (c + 1)], p16T[:, c, :],
                                                    va_pair[:, n, b, c].rearrange("p h d -> p (h d)"),
                                                    start=False, stop=(c == NPAIR - 1), skip_group_check=True)
                        last.then_inc(o16_in_psum, 1)
                pe.wait_ge(o16_ok, NT * (n + 1))
                for t in range(NT):
                    last = nc.tensor.transpose(bank[:, t // TPB, (t % TPB) * P:(t % TPB + 1) * P], o16[:, t, :], ident[:])
                    if t % TPB == TPB - 1:
                        last.then_inc(o16T_in_psum, 1)
                pe.wait_ge(o16T_ok, B * (n + 1))
                residual_out(2 + 2 * n, (lambda t: q16T[:, t // TPB, (t % TPB) * P:(t % TPB + 1) * P], w16[:, n, WO, :]))

            keys_values(0)
            norm_transposes(2)
            normed(2)
            for t in range(NT):
                b, i = t // TPB, t % TPB
                last = nc.tensor.matmul(bank[:, b, i * NC:(i + 1) * NC], tile_T(t), kq1[:, b, :],
                                        start=True, stop=True)
                if i == TPB - 1:
                    last.then_inc(s1_in_psum, 1)
            for b in range(B):
                pe.wait_ge(p1_ok, b + 1)
                for i in range(TPB):
                    last = nc.tensor.transpose(bank[0:NC, 2 + b, i * P:(i + 1) * P], s1[:, TPB * b + i, :], ident[:])
                last.then_inc(p1T_in_psum, 1)
            for b in range(B):
                pe.wait_ge(p1T_ok, b + 1)
                for i in range(TPB):
                    last = nc.tensor.matmul(bank[:, 4 + b, i * P:(i + 1) * P], p1T[:, TPB * b + i, :], v1[:, b, :],
                                            start=True, stop=True)
                last.then_inc(o1_in_psum, 1)
            pe.wait_ge(y_added, B * E)
            pe.wait_ge(turned_ok, B)
            residual_out(0, (lambda t: turned[:, t // TPB, (t % TPB) * P:(t % TPB + 1) * P], l1w[:, L1P, :]))
            keys_values(1)
            norm_transposes(3)
            normed(3)
            pe.wait_ge(x_done, 2)
            residual_out(1, (tile_T, waa1[:]))
            pe.wait_ge(wq2_ok, 8)
            pe.wait_ge(kv16_ok, 6)
            for m in range(3):
                for i in range(IT):
                    r, to = rows2[i], bank[:, m, i * P:i * P + rows2[i]]
                    if m < 2:
                        nc.tensor.transpose(to, wn2[0:r, m, i * P:(i + 1) * P], ident[0:r, 0:r])
                    else:
                        nc.tensor.transpose(bank[0:r, m, i * P:(i + 1) * P], wn2[:, m, i * P:i * P + r], ident[:])
            nc.tensor.matmul(bank[:, 3, 0:P], ones[:], diag_down[:], start=True, stop=True).then_inc(w2T_in_psum, 1)
            attention16(0, 4)
            pe.wait_ge(wq3_ok, 3)
            pe.wait_ge(o16T_ok, B)
            w3 = wn3[:].rearrange("p (m i b) k -> p m i (b k)", m=3, i=IT)
            for m in range(3):
                for i in range(IT):
                    last = nc.tensor.transpose(bank[:, m, i * P:(i + 1) * P], w3[:, m, i, :], ident[:])
            last.then_inc(w3T_in_psum, 1)
            global_max(0, 1)
            norm_transposes(5, 0)
            normed(5)
            pe.wait_ge(w2T_ok, 5)
            pe.wait_ge(w3T_ok, 1)
            for b in range(B):
                for i in range(IT):
                    n, r = IT * b + i, rows2[i]
                    if n >= 3:
                        pe.wait_ge(gu_taken, n - 2)
                    for m in range(2):
                        last = nc.tensor.matmul(bank[0:r, 2 * (n % 3) + m, :], w2T[:, m, i * P:i * P + r], xqT[:, b, :],
                                                start=True, stop=True)
                    last.then_inc(gu_in_psum, 1)
            global_max(1, 1)
            for b in range(B):
                pe.wait_ge(hq_ok, IT * (b + 1))
                for t in range(TPB):
                    for i in range(IT):
                        r = rows2[i]
                        last = nc.tensor.matmul(bank[:, 6 + b, t * P:(t + 1) * P], hq[0:r, i, b, t * P:(t + 1) * P],
                                                w2T[0:r, 2, i * P:(i + 1) * P], start=(i == 0), stop=(i == IT - 1))
                last.then_inc(res_in_psum, 1)
            attention16(1, 6)
            global_max(2, 1)
            norm_transposes(7, 1)
            normed(7)
            pe.wait_ge(o16T_ok, 2 * B)
            for b in range(B):
                for i in range(IT):
                    n = IT * b + i
                    if n >= 3:
                        pe.wait_ge(ug_copied, 2 * (n - 2))
                    for m in range(2):
                        nc.tensor.matmul(bank[:, 2 * (n % 3) + m, :], w3T[:, m, i * P:(i + 1) * P], xnT[:, b, :],
                                         start=True, stop=True).then_inc(ug_in_psum, 1)
            for j, count in ((3, 2), (4, 1), (5, 1)):
                global_max(j, count)
            for b in range(B):
                pe.wait_ge(o3_ok, b + 1)
                for t in range(TPB):
                    for i in range(IT):
                        last = nc.tensor.matmul(bank[:, 6 + b, t * P:(t + 1) * P], t3[:, i, b, t * P:(t + 1) * P],
                                                w3T[:, 2, i * P:(i + 1) * P], start=(i == 0), stop=(i == IT - 1))
                last.then_inc(res_in_psum, 1)

        @block.scalar
        def _(act):
            for n in VROWS:
                r, k = vrow[n]
                act.dma_start(vec_rows[r:r + k, :], vsrc[n].rearrange("(r d) -> r d", d=D)).then_inc(in_vec, 16)
            for dst, name in ((gamma_ctx, "L0_xattn_gamma_media"), (beta_ctx, "L0_xattn_beta_media"),
                              (gamma_lat, "L0_xattn_gamma_lat"), (beta_lat, "L0_xattn_beta_lat"), (bo0, "L0_xattn_bo")):
                act.dma_start(dst[:], a[name].partition_broadcast(dst.shape[0])).then_inc(in_norm, 16)
            act.wait_ge(vcol_in_psum, 1)
            nc.scalar.activation(vec_cols[:], bank[:, 6, 0:nrow], ACT.Copy).then_inc(vcol_ok, 1)
            nc.scalar.activation(bq0_scaled[:], bank[:, 6, 0:H0], ACT.Copy, scale=SC0).then_inc(vcol_ok, 1)
            for n in range(2):
                row = vrow[f"L{n + 2}_xattn_bq"][0]
                nc.scalar.activation(bq16[:, n:n + 1], bank[:, 6, row:row + 1], ACT.Copy, scale=SC16).then_inc(vcol_ok, 1)
            for h in range(H0):
                act.wait_ge(wT_in_psum, h + 1)
                if h >= 2:
                    act.wait_ge(ab_in_psum, h - 1)
                nc.scalar.activation(wT0[:, h % 2, :, :], bank[:, h % 2, 0:3 * P].rearrange("p (n m) -> p n m", n=3),
                                     ACT.Copy).then_inc(wT_ok, 1)
                act.wait_ge(ab_in_psum, h + 1)
                nc.scalar.activation(ab0[:, h, :], bank[:, 2 + h % 2, 0:2 * P + 1], ACT.Copy).then_inc(ab_ok, 1)
            act.wait_ge(cT_in_psum, 1)
            cT = bank[:, 6, :].rearrange("p (n b k) -> p n b k", n=2, b=B)
            nc.scalar.activation(kvT[:, :, S:NK], cT[:, 0, :, 0:NC], ACT.Copy).then_inc(cT_ok, 1)
            nc.scalar.activation(ctxT[:], cT[:, 1, :, 0:NC], ACT.Copy).then_inc(cT_ok, 1)
            act.wait_ge(xT_in_psum, TPB)
            nc.scalar.activation(kvT[:, 0, 0:S], bank[:, 4, :], ACT.Copy).then_inc(xnT_b_ok[0], 1)

            def query(u):
                h, b = u // B, u % B
                act.wait_ge(q_in_psum, u + 1)
                if u >= 2:
                    act.wait_ge(scores_ok, TPB * (u - 1))
                act.wait_ge(ab_ok, H0)
                nc.scalar.activation(qT[b], bank[:, 7, :], ACT.Identity, bias=ab0[:, h, 2 * P:2 * P + 1],
                                     scale=SC0).then_inc(q_ok, 1)

            def exponent(u, i):
                b, first = u % B, 2 * (i % 2)
                act.wait_ge(max_ok, TPB * u + i + 1)
                act.wait_ge(scores_ok, TPB * u + i + 1)
                if u >= 2:
                    act.wait_ge(pT_in_psum, NCH * (u - 1))
                    act.wait_ge(inv_ok, u - 1)
                nc.scalar.activation(prob[b][:, i, :], bank[:, first:first + 2, :].rearrange("p b n -> p (b n)")[:, 0:NK],
                                     ACT.Exp, bias=neg_max[:, b, i:i + 1], accum_out=row_sum[:, b, i:i + 1])\
                    .then_inc(prob_ok, 1)

            def evacuate(u, c):
                n = chunk_keys(c)
                act.wait_ge(pT_in_psum, NCH * u + c + 1)
                if u:
                    act.wait_ge(u_in_psum, u)
                nc.scalar.activation(probT[0:n, c, :], bank[0:n, PT_BANK[c], :], ACT.Copy).then_inc(pT_act_ok, 1)

            query(0)
            for u in range(U0 + 2):
                s, p, o = u < U0, 1 <= u <= U0, u >= 2
                if s:
                    exponent(u, 0)
                if p:
                    evacuate(u - 1, 1)
                if s:
                    exponent(u, 1)
                    if u + 1 < U0:
                        query(u + 1)
                    exponent(u, 2)
                if p:
                    evacuate(u - 1, 3)
                if s:
                    exponent(u, 3)
                if p:
                    act.wait_ge(u_in_psum, u)
                    if u >= 2:
                        act.wait_ge(o_in_psum, u - 1)
                    nc.scalar.activation(uT[:], bank[:, 6, :], ACT.Copy).then_inc(u_ok, 1)

            def norm_copy(k):
                act.wait_ge(xT_in_psum, NT * k + TPB)
                nc.scalar.activation(xnT[:, 0, :], bank[:, 4, :], ACT.Copy).then_inc(xnT_b_ok[0], 1)

            act.wait_ge(l1_in_psum, 1)
            nc.scalar.activation(l1T[:], bank[:, 0, 0:2 * P].rearrange("p (n m) -> p n m", n=2), ACT.Copy)\
                .then_inc(l1_ok, 1)
            nc.scalar.activation(k1T[:], bank[:, 1, 0:B * NC].rearrange("p (b k) -> p b k", b=B), ACT.Copy)\
                .then_inc(l1_ok, 1)
            nc.scalar.activation(v1[:], bank[0:NC, 2, 0:B * D].rearrange("p (b d) -> p b d", b=B), ACT.Copy)\
                .then_inc(l1_ok, 1)
            act.wait_ge(l1_in_psum, 2)
            nc.scalar.activation(kq1[:], bank[:, 3, 0:B * NC].rearrange("p (b k) -> p b k", b=B), ACT.Copy)\
                .then_inc(l1_ok, 1)
            nc.scalar.activation(wa1T[:], bank[:, 3, 256:256 + P], ACT.Copy).then_inc(l1_ok, 1)
            act.wait_ge(l1_in_psum, 3)
            nc.scalar.activation(waa1[:], bank[:, 0, 0:D], ACT.Copy).then_inc(l1_ok, 1)

            norm_copy(1)

            def relu(e):
                for j in range(FT):
                    for b in range(B):
                        act.wait_ge(h_in_psum, FT * B * e + j * B + b + 1)
                        if e >= 2:
                            act.wait_ge(y_in_psum, B * (e - 1))
                        row = vrow["L0_ffn_b1"][0] + FT * e + j
                        nc.scalar.activation(hT[:, e % 2, j, b, :], bank[:, j * B + b, :], ACT.Relu,
                                             bias=vec_cols[:, row:row + 1]).then_inc(h_ok, 1)

            relu(0)
            act.wait_ge(diff_ok, 1)
            nc.scalar.activation(top_exp[:], top_diff[:], ACT.Exp).then_inc(top_exp_ok, 1)
            act.wait_ge(gT_in_psum, 1)
            nc.scalar.activation(gateT[:].rearrange("e t p -> e (t p)"),
                                 bank[0:E, 4:6, :].rearrange("e b n -> e (b n)"), ACT.Copy).then_inc(gT_ok, 1)
            for e in range(1, E):
                relu(e)
            def keys_values(n):
                act.wait_ge(kv16_in_psum, n + 1)
                row = vrow[f"L{n + 2}_xattn_bk"][0]
                nc.scalar.activation(k16T[:, n], bank[:, 0, 0:B * NC].rearrange("p (b k) -> p b k", b=B), ACT.Identity,
                                     bias=vec_cols[:, row:row + 1]).then_inc(kv16_ok, 1)
                nc.scalar.activation(v_pair[:, n], bank[:, 1, 0:B * D].rearrange("p (b d) -> p b d", b=B), ACT.Copy)\
                    .then_inc(kv16_ok, 1)
                nc.scalar.activation(v_left[:, n], bank[0:LP, 1, B * D:2 * B * D].rearrange("p (b d) -> p b d", b=B),
                                     ACT.Copy).then_inc(kv16_ok, 1)

            def attention16(n, k):
                norm_copy(k)
                for b in range(B):
                    act.wait_ge(q16_in_psum, B * n + b + 1)
                    nc.scalar.activation(q16T[:, b, :], bank[:, 6 + b, :], ACT.Identity, bias=bq16[:, n:n + 1],
                                         scale=SC16).then_inc(q16_ok, 1)
                for t in range(NT + 1):
                    if t:
                        m = NT * n + t - 1
                        act.wait_ge(p16T_in_psum, 2 * m + 1)
                        if m:
                            act.wait_ge(o16_in_psum, m)
                        nc.scalar.activation(p16T[:, 0:NPAIR, :],
                                             bank[:, 4:6, :].rearrange("p b (c q) -> p (b c) q", c=4), ACT.Copy)\
                            .then_inc(p16T_ok, 1)
                        act.wait_ge(p16T_in_psum, 2 * m + 2)
                        nc.scalar.activation(p16T[0:LP, NPAIR:NPAIR + 2, :],
                                             bank[0:LP, 6, 0:2 * P].rearrange("p (c q) -> p c q", c=2), ACT.Copy)\
                            .then_inc(p16T_ok, 1)
                    if t < NT:
                        m = NT * n + t
                        act.wait_ge(s16_ok, m + 1)
                        if t >= 2:
                            act.wait_ge(p16T_in_psum, 2 * (m - 1))
                        pair, left = p16[:, t % 2, 0:HM * PK], p16[:, t % 2, HM * PK:HM * NC]
                        nc.scalar.activation(pair.rearrange("p (h k) -> p h k", h=HM), s16[:, t % 2, :, 0:PK], ACT.Exp)\
                            .then_inc(p16_ok, 1)
                        nc.scalar.activation(left.rearrange("p (h k) -> p h k", h=HM), s16[:, t % 2, :, PK:NC], ACT.Exp)\
                            .then_inc(p16_ok, 1)
                row = vrow[f"L{n + 2}_xattn_bv"][0]
                for b in range(B):
                    act.wait_ge(o16T_in_psum, B * n + b + 1)
                    nc.scalar.activation(q16T[:, b, :], bank[:, b, :], ACT.Identity, bias=vec_cols[:, row:row + 1])\
                        .then_inc(o16T_ok, 1)

            keys_values(0)
            norm_copy(2)
            for b in range(B):
                act.wait_ge(s1_ok, b + 1)
                part = s1[:, TPB * b:TPB * (b + 1), :]
                nc.scalar.activation(part, part, ACT.Exp, scale=SC1).then_inc(p1_ok, 1)
            for b in range(B):
                act.wait_ge(p1T_in_psum, b + 1)
                nc.scalar.activation(p1T[:, TPB * b:TPB * (b + 1), :],
                                     bank[0:NC, 2 + b, :].rearrange("p (i q) -> p i q", i=TPB), ACT.Copy)\
                    .then_inc(p1T_ok, 1)
            keys_values(1)
            norm_copy(3)
            for b in range(B):
                act.wait_ge(tanh_in_ok, b + 1)
                part = tanh_in[:, TPB * b:TPB * (b + 1), :]
                nc.scalar.activation(part, part, ACT.Tanh).then_inc(tanh_ok, 1)
            act.wait_ge(w2T_in_psum, 1)
            act.wait_ge(rne_made, 2)
            for m in range(2):
                nc.scalar.activation(w2T[:, m, 0:I2], bank[:, m, 0:I2], ACT.Copy).then_inc(w2T_ok, 1)
            nc.scalar.activation(w2T[:, 2, 0:2 * P], bank[:, 2, 0:2 * P], ACT.Copy).then_inc(w2T_ok, 1)
            nc.scalar.activation(w2T[0:rows2[2], 2, 2 * P:3 * P], bank[0:rows2[2], 2, 2 * P:3 * P], ACT.Copy)\
                .then_inc(w2T_ok, 1)
            nc.scalar.activation(down_row[:], bank[:, 3, 0:P], ACT.Copy).then_inc(w2T_ok, 1)
            act.wait_ge(in_f2, 16 * 7)
            nc.scalar.activation(clip_sig[:], clip[:], ACT.Tanh, scale=0.5).then_inc(clip_tanh_ok, 1)
            attention16(0, 4)
            act.wait_ge(w3T_in_psum, 1)
            nc.scalar.activation(w3T, bank[:, 0:3, 0:IT * P], ACT.Copy).then_inc(w3T_ok, 1)
            act.wait_ge(xT_in_psum, NT * 5 + TPB)
            nc.scalar.activation(xqT[:, 0, :], bank[:, 4, :], ACT.Identity, bias=minus_rne[:]).then_inc(xnT_b_ok[0], 1)
            act.wait_ge(c_ok, 1)
            for b in range(B):
                for i in range(IT):
                    n, r = IT * b + i, rows2[i]
                    act.wait_ge(gu_in_psum, n + 1)
                    if n >= 2:
                        act.wait_ge(gu_taken, n - 1)
                    nc.scalar.activation(tanh_out[0:r, n % 2, :], bank[0:r, 2 * (n % 3), :], ACT.Tanh,
                                         scale=c_gate[0:r, i:i + 1]).then_inc(gu_tanh_ok, 1)
            act.wait_ge(hscale_ok, 1)
            for b in range(B):
                for i in range(IT):
                    h = val[0:rows2[i], i, b, :]
                    nc.scalar.activation(h, h, ACT.Identity, bias=plus_rne[0:rows2[i], :],
                                         scale=h_inv[0:rows2[i], :]).then_inc(h_rounded, 1)
            attention16(1, 6)
            norm_copy(7)
            for b in range(B):
                for i in range(IT):
                    n = IT * b + i
                    for m, to in enumerate((val2, val)):
                        act.wait_ge(ug_in_psum, 2 * n + m + 1)
                        nc.scalar.activation(to[:, i, b, :], bank[:, 2 * (n % 3) + m, :], ACT.Copy)\
                            .then_inc(ug_copied, 1)
            for b in range(B):
                act.wait_ge(gate_int_ok, b + 1)
                nc.scalar.activation(t3[:, :, b, :], val2[:, :, b, :], ACT.Tanh, scale=half_sg[:]).then_inc(tanh3_ok, 1)

        @block.vector
        def _(dve):
            own = Steps(dve, dve_step)
            dve.wait_ge(in_ctx, 16)
            for b in range(B):
                own.add(nc.vector.bn_stats(ctx_stats[:, b, :], ctx_tok[:, b, :]))
            own.settle()
            for b in range(B):
                own.add(nc.vector.bn_aggr(ctx_meanvar[:, b, :], ctx_stats[:, b, :]))
            own.settle()
            nc.vector.tensor_scalar(ctx_var_eps[:], ctx_meanvar[:, :, 1], EPS, None, ALU.add).then_inc(ctx_var_ok, 1)

            def layer_stats():
                for t in range(NT):
                    own.add(nc.vector.bn_stats(stats[:, t, :], x[:, t, :]))
                own.settle()
                for t in range(NT):
                    own.add(nc.vector.bn_aggr(meanvar[:, t, :], stats[:, t, :]))
                own.settle()
                nc.vector.tensor_scalar(var_eps[:], meanvar[:, :, 1], EPS, None, ALU.add).then_inc(var_ok, 1)

            for b in range(B):
                dve.wait_ge(in_x[b], 16)
            layer_stats()
            dve.wait_ge(ctx_rstd_ok, 1)
            for b in range(B):
                own.add(nc.vector.tensor_scalar(ctx_norm[:, b, :], ctx_tok[:, b, :], ctx_meanvar[:, b, 0:1],
                                                ctx_rstd[:, b:b + 1], ALU.subtract, ALU.mult))
            own.settle()
            dve.wait_ge(in_norm, 16 * 5)
            own.add(nc.vector.tensor_tensor(ctx_norm[:], ctx_norm[:], gamma_ctx[:].unsqueeze(1).to_broadcast([NC, B, D]),
                                            ALU.mult))
            own.settle()
            nc.vector.tensor_tensor(ctx_norm[:], ctx_norm[:], beta_ctx[:].unsqueeze(1).to_broadcast([NC, B, D]),
                                    ALU.add).then_inc(ctx_norm_ok, 1)
            dve.wait_ge(rstd_ok, 1)
            for t in range(NT):
                own.add(nc.vector.tensor_scalar(xn[:, t, :], x[:, t, :], meanvar[:, t, 0:1], rstd[:, t:t + 1],
                                                ALU.subtract, ALU.mult))
            own.settle()
            for b in range(B):
                part = xn[:, TPB * b:TPB * (b + 1), :]
                own.add(nc.vector.tensor_tensor(part, part, gamma_lat[:].unsqueeze(1).to_broadcast([P, TPB, D]), ALU.mult))
                own.settle()
                for t in range(TPB * b, TPB * (b + 1)):
                    nc.vector.tensor_tensor(xn[:, t, :], xn[:, t, :], beta_lat[:], ALU.add).then_inc(xn_ok, 1)
            dve.wait_ge(bv_used, H0)
            nc.vector.tensor_tensor(out_bias0[:], bank[:, 7, 0:D], bo0[:], ALU.add).then_inc(bias0_ok, 1)
            dve.wait_ge(xT_in_psum, NT)
            nc.vector.tensor_copy(kvT[:, 1, 0:S], bank[:, 5, :]).then_inc(xnT_b_ok[1], 1)

            def maximum(u, i):
                b, first = u % B, 2 * (i % 2)
                dve.wait_ge(scores_ok, TPB * u + i + 1)
                if u >= 2:
                    dve.wait_ge(prob_ok, TPB * (u - 1))
                nc.vector.tensor_reduce(neg_max[:, b, i:i + 1], bank[:, first:first + 2, :].rearrange("p b n -> p (b n)")[:, 0:NK],
                                        AX.X, ALU.max, negate=True).then_inc(max_ok, 1)

            def evacuate(u, c):
                n = chunk_keys(c)
                dve.wait_ge(pT_in_psum, NCH * u + c + 1)
                if u:
                    dve.wait_ge(u_in_psum, u)
                nc.vector.tensor_copy(probT[0:n, c, :], bank[0:n, PT_BANK[c], :]).then_inc(pT_dve_ok, 1)

            def add_output(u):
                b = u % B
                dve.wait_ge(o_in_psum, u + 1)
                dve.wait_ge(inv_ok, u + 1)
                if u == 0:
                    dve.wait_ge(x_biased, 1)
                if u >= 2:
                    dve.wait_ge(o_added, u - 1)
                for i in range(TPB):
                    t = TPB * b + i
                    last = nc.vector.scalar_tensor_tensor(out=x[:, t, :], in0=bank[:, 7, i * P:(i + 1) * P],
                                                          scalar=row_inv[:, b, i:i + 1], in1=x[:, t, :],
                                                          op0=ALU.mult, op1=ALU.add)
                last.then_inc(o_added, 1)

            def invert(u):
                b = u % B
                dve.wait_ge(prob_ok, TPB * (u + 1))
                if u >= 2:
                    dve.wait_ge(o_added, u - 1)
                nc.vector.reciprocal(row_inv[:, b, :], row_sum[:, b, :]).then_inc(inv_ok, 1)

            def weight_scales2():
                own.add(nc.vector.memset(wmax2[:], 1.0))
                dve.wait_ge(in_f2, 16 * 7)
                own.settle()
                for m in range(2):
                    own.add(nc.vector.tensor_reduce(wmax2[:, IT * m:IT * m + 2],
                                                    wn2[:, m, 0:2 * P].rearrange("p (i d) -> p i d", i=2), AX.X, ALU.max,
                                                    apply_absolute_value=True))
                    own.add(nc.vector.tensor_reduce(wmax2[0:rows2[2], IT * m + 2:IT * m + 3], wn2[0:rows2[2], m, 2 * P:3 * P],
                                                    AX.X, ALU.max, apply_absolute_value=True))
                own.add(nc.vector.tensor_reduce(wmax2[:, 6:7], wn2[:, 2, 0:I2], AX.X, ALU.max, apply_absolute_value=True))
                own.settle()
                own.add(nc.vector.tensor_scalar(wscale2[:], wmax2[:], 1.0 / 127, None, ALU.mult))
                own.settle()
                nc.vector.reciprocal(winv2[:], wscale2[:]).then_inc(wmax_ok, 1)

            def weight_scales3():
                dve.wait_ge(in_f3, 16 * 3)
                own.add(nc.vector.tensor_reduce(wmax3[:], wn3[:], AX.X, ALU.max, apply_absolute_value=True))
                own.settle()
                own.add(nc.vector.tensor_scalar(wscale3[:], wmax3[:], 1.0 / 7, 1e-12, ALU.mult, ALU.max))
                own.settle()
                nc.vector.reciprocal(winv3[:], wscale3[:]).then_inc(wmax_ok, 1)

            for u in range(U0 + 2):
                s, p, o = u < U0, 1 <= u <= U0, u >= 2
                if s:
                    maximum(u, 0)
                if u == 3:
                    weight_scales2()
                if u == 5:
                    weight_scales3()
                if o:
                    add_output(u - 2)
                if p:
                    invert(u - 1)
                    evacuate(u - 1, 0)
                if s:
                    maximum(u, 1)
                if p:
                    evacuate(u - 1, 2)
                if s:
                    maximum(u, 2)
                    maximum(u, 3)
                if p:
                    evacuate(u - 1, 4)

            def layer_norm(k):
                layer_stats()
                dve.wait_ge(rstd_ok, k + 1)
                for t in range(NT):
                    nc.vector.tensor_scalar(xn[:, t, :], x[:, t, :], meanvar[:, t, 0:1], rstd[:, t:t + 1],
                                            ALU.subtract, ALU.mult).then_inc(xn_ok, 1)

            def norm_copy(k):
                dve.wait_ge(xT_in_psum, NT * (k + 1))
                nc.vector.tensor_copy(xnT[:, 1, :], bank[:, 5, :]).then_inc(xnT_b_ok[1], 1)

            def per_tile(v, n=E):
                return v.unsqueeze(2).to_broadcast([P, NT, n])

            def batch(tile, b):
                return tile[:, TPB * b:TPB * (b + 1), :]

            def add_result(k, done):
                for b in range(B):
                    dve.wait_ge(res_in_psum, B * k + b + 1)
                    nc.vector.tensor_tensor(batch(x, b), bank[:, 6 + b, :].rearrange("p (i d) -> p i d", i=TPB),
                                            batch(x, b), ALU.add).then_inc(x_done, 1)
                dve.wait_ge(x_done, done)

            dve.wait_ge(o_added, U0)
            layer_norm(1)
            norm_copy(1)
            dve.wait_ge(logit_in_psum, 1)
            dve.wait_ge(rank_ok, E)
            dve.wait_ge(in_moe, 16 * 5)
            own.add(nc.vector.tensor_tensor(logit[:], bank[:, 6, 0:NT * E].rearrange("p (t e) -> p t e", t=NT),
                                            br[:].unsqueeze(1).to_broadcast([P, NT, E]), ALU.add))
            own.settle()
            for i, src in ((0, logit), (1, logit2)):
                own.add(nc.vector.tensor_reduce(top[i][:], src[:], AX.X, ALU.max))
                own.settle()
                own.add(nc.vector.tensor_tensor(key[:], src[:], per_tile(top[i][:]), ALU.is_equal))
                own.settle()
                own.add(nc.vector.tensor_tensor(key[:], key[:], rank[:], ALU.mult))
                own.settle()
                own.add(nc.vector.tensor_reduce(top_key[:], key[:], AX.X, ALU.max))
                own.settle()
                own.add(nc.vector.tensor_tensor(pick[i][:], key[:], per_tile(top_key[:]), ALU.is_equal))
                own.settle()
                if i == 0:
                    own.add(nc.vector.scalar_tensor_tensor(out=logit2[:], in0=pick[0][:], scalar=-3e38, in1=logit[:],
                                                           op0=ALU.mult, op1=ALU.add))
                    own.settle()
            nc.vector.tensor_tensor(top_diff[:], top[1][:], top[0][:], ALU.subtract).then_inc(diff_ok, 1)
            dve.wait_ge(top_exp_ok, 1)
            own.add(nc.vector.tensor_scalar(top_den[:], top_exp[:], 1.0, None, ALU.add))
            own.settle()
            own.add(nc.vector.reciprocal(top_w[0][:], top_den[:]))
            own.settle()
            own.add(nc.vector.tensor_tensor(top_w[1][:], top_exp[:], top_w[0][:], ALU.mult))
            own.add(nc.vector.tensor_tensor(pick[0][:], pick[0][:], per_tile(top_w[0][:]), ALU.mult))
            own.settle()
            own.add(nc.vector.tensor_tensor(pick[1][:], pick[1][:], per_tile(top_w[1][:]), ALU.mult))
            own.settle()
            nc.vector.tensor_tensor(gate[:], pick[0][:], pick[1][:], ALU.add).then_inc(gate_ok, 1)
            dve.wait_ge(b2_in_psum, 1)
            for b in range(B):
                nc.vector.tensor_tensor(batch(x, b), bank[:, 6 + b, :].rearrange("p (i d) -> p i d", i=TPB),
                                        batch(x, b), ALU.add).then_inc(b2_added, 1)
            dve.wait_ge(gate_ok, 1)
            dve.wait_ge(b2_added, B)
            for e in range(E):
                for b in range(B):
                    dve.wait_ge(y_in_psum, B * e + b + 1)
                    if e >= 1:
                        dve.wait_ge(y_added, B * (e - 1) + b + 1)
                    for i in range(TPB):
                        t = TPB * b + i
                        last = nc.vector.scalar_tensor_tensor(out=x[:, t, :], in0=bank[:, 6 + b, i * P:(i + 1) * P],
                                                              scalar=gate[:, t, e:e + 1], in1=x[:, t, :],
                                                              op0=ALU.mult, op1=ALU.add)
                    last.then_inc(y_added, 1)
            dve.wait_ge(y_added, B * E)
            layer_norm(2)
            norm_copy(2)
            for b in range(B):
                dve.wait_ge(s1_in_psum, b + 1)
                src = bank[:, b, 0:TPB * NC].rearrange("p (i k) -> p i k", i=TPB)
                own.add(nc.vector.tensor_reduce(neg_max1[:, TPB * b:TPB * (b + 1)], src, AX.X, ALU.max, negate=True))
                own.settle()
                nc.vector.tensor_tensor(batch(s1, b), src,
                                        neg_max1[:, TPB * b:TPB * (b + 1)].unsqueeze(2).to_broadcast([P, TPB, NC]),
                                        ALU.add).then_inc(s1_ok, 1)
            for b in range(B):
                dve.wait_ge(p1_ok, b + 1)
                own.add(nc.vector.tensor_reduce(sum1[:, TPB * b:TPB * (b + 1)], batch(s1, b), AX.X, ALU.add))
            own.settle()
            own.add(nc.vector.reciprocal(inv1[:], sum1[:]))
            own.settle()
            for b in range(B):
                dve.wait_ge(o1_in_psum, b + 1)
                nc.vector.tensor_tensor(turned[:, b, :].rearrange("p (c i) -> p i c", i=TPB),
                                        bank[:, 4 + b, :].rearrange("p (i c) -> p i c", i=TPB),
                                        inv1[:, TPB * b:TPB * (b + 1)].unsqueeze(2).to_broadcast([P, TPB, D]),
                                        ALU.mult).then_inc(turned_ok, 1)
            dve.wait_ge(x_biased, 2)
            add_result(0, 2)
            layer_norm(3)
            norm_copy(3)
            dve.wait_ge(in_l1, 16 * 9)
            for b in range(B):
                dve.wait_ge(res_in_psum, B + b + 1)
                nc.vector.tensor_tensor(batch(tanh_in, b), bank[:, 6 + b, :].rearrange("p (i d) -> p i d", i=TPB),
                                        fbias1[:].unsqueeze(1).to_broadcast([P, TPB, D]), ALU.add)\
                    .then_inc(tanh_in_ok, 1)
            for b in range(B):
                dve.wait_ge(tanh_ok, b + 1)
                nc.vector.tensor_tensor(batch(x, b), batch(tanh_in, b), batch(x, b), ALU.add).then_inc(x_done, 1)
            dve.wait_ge(x_done, 4)

            def attention16(n, k):
                layer_norm(k)
                norm_copy(k)
                if n == 0:
                    dve.wait_ge(mask_neg_ok, NT)
                for t in range(NT + 1):
                    if t < NT:
                        m, z = NT * n + t, t % 2
                        tile, scores = s16[:, z], bank[:, 0:4, 0:BK * NC]
                        flat = tile.rearrange("p (g h) k -> p g (h k)", g=4)
                        by_head = scores.rearrange("p g (h k) -> p g h k", h=BK)
                        nmax = neg_max16[:, z, :]
                        dve.wait_ge(s16_in_psum, m + 1)
                        if m >= 2:
                            dve.wait_ge(p16_ok, 2 * (m - 1))
                        if n == 0:
                            nc.vector.tensor_tensor(flat, scores, mask_neg[:, t, :].rearrange("p (g n) -> p g n", g=4),
                                                    ALU.add).then_inc(s16_taken, 1)
                            dve.wait_ge(s16_taken, m + 1)
                            nc.vector.tensor_reduce(nmax, tile, AX.X, ALU.max, negate=True).then_inc(max16_ok, 1)
                            dve.wait_ge(max16_ok, m + 1)
                            nc.vector.tensor_tensor(tile, tile, nmax.unsqueeze(2).to_broadcast([P, HM, NC]), ALU.add)\
                                .then_inc(s16_ok, 1)
                        else:
                            own.add(nc.vector.tensor_reduce(nmax.rearrange("p (g h) -> p g h", g=4), by_head, AX.X,
                                                            ALU.max, negate=True))
                            own.settle()
                            for g in range(4):
                                part = nmax[:, BK * g:BK * (g + 1)].unsqueeze(2).to_broadcast([P, BK, NC])
                                last = nc.vector.tensor_tensor(tile[:, BK * g:BK * (g + 1), :], by_head[:, g], part, ALU.add)
                                if g < 3:
                                    own.add(last)
                            last.then_inc(s16_ok, 1)
                    if t:
                        m, z = NT * n + t - 1, (t - 1) % 2
                        o = bank[:, 7, z * 256:z * 256 + HM * (DH + 1)].rearrange("p (h d) -> p h d", h=HM)
                        dve.wait_ge(o16_in_psum, m + 1)
                        if m >= 2:
                            dve.wait_ge(o16_ok, m - 1)
                        own.add(nc.vector.reciprocal(inv16[:, z, :], o[:, :, DH]))
                        own.settle()
                        if n == 0:
                            dve.wait_ge(spoil16_ok, m + 1)
                            own.add(nc.vector.tensor_tensor(inv16[:, z, :], inv16[:, z, :], spoil16[:, z, :], ALU.add))
                            own.settle()
                        nc.vector.tensor_tensor(o16[:, t - 1, :].rearrange("p (h d) -> p h d", h=HM), o[:, :, 0:DH],
                                                inv16[:, z, :].unsqueeze(2).to_broadcast([P, HM, DH]), ALU.mult)\
                            .then_inc(o16_ok, 1)
                dve.wait_ge(x_biased, 3 + n)
                add_result(2 + 2 * n, 6 + 4 * n)

            def global_max(j, count):
                dve.wait_ge(pmaxT_in_psum, j + 1)
                nc.vector.tensor_reduce(gmax_row[:, 0:count], bank[0:1, 7, 0:count * P].rearrange("p (c q) -> p c q", c=count),
                                        AX.X, ALU.max).then_inc(gmax_ok, 1)
                dve.wait_ge(gmax_in_psum, j + 1)
                return bank[:, 7, 2 * P:2 * P + count]

            def row_max(to, src, axis=AX.X):
                return nc.vector.tensor_reduce(to, src, axis, ALU.max, apply_absolute_value=True)

            def scalars(to, src, s1, s2, op0, op1):
                own.add(nc.vector.tensor_scalar(to, src, s1, s2, op0, op1))
                own.settle()

            attention16(0, 4)
            dve.wait_ge(clip_tanh_ok, 1)
            scalars(clip_sig[:], clip_sig[:], 0.5, 0.5, ALU.mult, ALU.add)
            layer_norm(5)
            dve.wait_ge(xn_ok, NT * 6)
            row_max(pmax[:, 0:1], xn[:], AX.XY).then_inc(pmax_ok, 1)
            m = global_max(0, 1)
            scalars(x_scale[:], m, clip_sig[:, 0:1], 1.0 / 127, ALU.mult, ALU.mult)
            own.add(nc.vector.reciprocal(x_inv[:], x_scale[:]))
            own.settle()
            for b in range(B):
                scalars(batch(xn, b), batch(xn, b), x_inv[:], RNE, ALU.mult, ALU.add)
                nc.vector.tensor_scalar(batch(xn, b), batch(xn, b), RNE + 127, RNE - 128, ALU.min, ALU.max)\
                    .then_inc(xq_ok, 1)
            scalars(c_gate[:], wscale2[:, 0:IT], x_scale[:], 0.5, ALU.mult, ALU.mult)
            scalars(c_both[:], wscale2[:, IT:2 * IT], x_scale[:], None, ALU.mult, ALU.bypass)
            nc.vector.tensor_tensor(c_both[:], c_both[:], c_gate[:], ALU.mult).then_inc(c_ok, 1)
            own.add(nc.vector.memset(unit_max[:], 0.0))
            dve.wait_ge(c_ok, 1)
            own.settle()
            dve.wait_ge(xT_in_psum, NT * 6)
            nc.vector.tensor_scalar(xqT[:, 1, :], bank[:, 5, :], -RNE, None, ALU.add).then_inc(xnT_b_ok[1], 1)
            for b in range(B):
                for i in range(IT):
                    n, r = IT * b + i, rows2[i]
                    dve.wait_ge(gu_tanh_ok, n + 1)
                    own.add(nc.vector.scalar_tensor_tensor(out=silu_in[0:r, :], in0=tanh_out[0:r, n % 2, :], scalar=1.0,
                                                           in1=bank[0:r, 2 * (n % 3), :], op0=ALU.add, op1=ALU.mult))
                    own.settle()
                    nc.vector.scalar_tensor_tensor(out=val[0:r, i, b, :], in0=silu_in[0:r, :],
                                                   scalar=c_both[0:r, i:i + 1], in1=bank[0:r, 2 * (n % 3) + 1, :],
                                                   op0=ALU.mult, op1=ALU.mult).then_inc(gu_taken, 1)
                    dve.wait_ge(gu_taken, n + 1)
                    own.add(row_max(unit_max[0:r, 0, n:n + 1], val[0:r, i, b, :]))
            own.settle()
            row_max(pmax[:, 0:1], unit_max[:, 0, :]).then_inc(pmax_ok, 1)
            m = global_max(1, 1)
            scalars(h_scale[:], m, clip_sig[:, 1:2], 1.0 / 127, ALU.mult, ALU.mult)
            nc.vector.reciprocal(h_inv[:], h_scale[:]).then_inc(hscale_ok, 1)
            dve.wait_ge(w2T_ok, 5)
            own.add(nc.vector.tensor_scalar(down_scale[:], down_row[:], h_scale[:], None, ALU.mult))
            for b in range(B):
                for i in range(IT):
                    n, r = IT * b + i, rows2[i]
                    dve.wait_ge(h_rounded, n + 1)
                    h = val[0:r, i, b, :]
                    scalars(h, h, RNE + 127, RNE - 128, ALU.min, ALU.max)
                    nc.vector.tensor_scalar(hq[0:r, i, b, :], h, -RNE, None, ALU.add).then_inc(hq_ok, 1)
            for b in range(B):
                dve.wait_ge(res_in_psum, B * 3 + b + 1)
                own.add(nc.vector.tensor_tensor(batch(tanh_in, b), bank[:, 6 + b, :].rearrange("p (i d) -> p i d", i=TPB),
                                                down_scale[:].unsqueeze(1).to_broadcast([P, TPB, D]), ALU.mult))
                own.settle()
                nc.vector.tensor_tensor(batch(x, b), batch(tanh_in, b), batch(x, b), ALU.add).then_inc(x_done, 1)
            dve.wait_ge(x_done, 8)
            attention16(1, 6)
            Q16 = 32767.0
            layer_norm(7)
            dve.wait_ge(xn_ok, NT * 8)
            row_max(pmax[:, 0:1], xn[:], AX.XY).then_inc(pmax_ok, 1)
            m = global_max(2, 1)
            scalars(x_scale[:], m, 1 / Q16, 1e-12, ALU.mult, ALU.max)
            own.add(nc.vector.reciprocal(x_inv[:], x_scale[:]))
            own.settle()
            for b in range(B):
                scalars(batch(xn, b), batch(xn, b), x_inv[:], RNE, ALU.mult, ALU.add)
                nc.vector.tensor_scalar(batch(xn, b), batch(xn, b), -RNE, x_scale[:], ALU.add, ALU.mult)\
                    .then_inc(xq_ok, 1)
            norm_copy(7)
            for b in range(B):
                for i in range(IT):
                    n = IT * b + i
                    for m in range(2):
                        dve.wait_ge(ug_copied, 2 * n + m + 1)
                        row_max(unit_max[:, m, n:n + 1], (val2, val)[m][:, i, b, :]).then_inc(ug_maxed, 1)
            dve.wait_ge(ug_maxed, 2 * IT * B)
            row_max(pmax[:], unit_max[:]).then_inc(pmax_ok, 1)
            m = global_max(3, 2)
            scalars(ug_scale[:], m, 1 / Q16, 1e-12, ALU.mult, ALU.max)
            sg, su = ug_scale[:, 0:1], ug_scale[:, 1:2]
            own.add(nc.vector.tensor_scalar(half_sg[:], sg, 0.5, None, ALU.mult))
            nc.vector.reciprocal(ug_inv[:], ug_scale[:]).then_inc(ug_scale_ok, 1)
            dve.wait_ge(ug_scale_ok, 1)
            own.settle()
            dve.wait_ge(ug_copied, 2 * IT * B)
            for b in range(B):
                g = val2[:, :, b, :]
                scalars(g, g, ug_inv[:, 0:1], RNE, ALU.mult, ALU.add)
                nc.vector.tensor_scalar(g, g, -RNE, None, ALU.add).then_inc(gate_int_ok, 1)
            for b in range(B):
                g, t = val2[:, :, b, :], t3[:, :, b, :]
                dve.wait_ge(tanh3_ok, b + 1)
                scalars(t, t, 32768.0, RNE + 32768, ALU.mult, ALU.add)
                scalars(t, t, RNE + 65535, -RNE, ALU.min, ALU.add)
                own.add(nc.vector.tensor_tensor(t, g, t, ALU.mult))
                own.settle()
                own.add(row_max(unit_max[:, 0, b:b + 1], t, AX.XY))
            own.settle()
            row_max(pmax[:, 0:1], unit_max[:, 0, 0:B]).then_inc(pmax_ok, 1)
            m = global_max(4, 1)
            scalars(amax3[:, 0:1], m, sg, 2.0 ** -16, ALU.mult, ALU.mult)
            scalars(scale3[:, 0:1], amax3[:, 0:1], 1 / Q16, 1e-12, ALU.mult, ALU.max)
            own.add(nc.vector.reciprocal(inv3[:, 0:1], scale3[:, 0:1]))
            own.settle()
            scalars(ratio3[:, 0:1], inv3[:, 0:1], sg, 2.0 ** -16, ALU.mult, ALU.mult)
            for b in range(B):
                dve.wait_ge(up_int_ok, b + 1)
                t, u = t3[:, :, b, :], val[:, :, b, :]
                scalars(t, t, ratio3[:, 0:1], RNE, ALU.mult, ALU.add)
                own.add(nc.vector.scalar_tensor_tensor(out=t, in0=t, scalar=-RNE, in1=u, op0=ALU.add, op1=ALU.mult))
                own.settle()
                own.add(row_max(unit_max[:, 0, b:b + 1], t, AX.XY))
            own.settle()
            row_max(pmax[:, 0:1], unit_max[:, 0, 0:B]).then_inc(pmax_ok, 1)
            m = global_max(5, 1)
            scalars(amax3[:, 1:2], m, scale3[:, 0:1], su, ALU.mult, ALU.mult)
            scalars(scale3[:, 1:2], amax3[:, 1:2], 1 / Q16, 1e-12, ALU.mult, ALU.max)
            own.add(nc.vector.reciprocal(inv3[:, 1:2], scale3[:, 1:2]))
            own.settle()
            scalars(ratio3[:, 1:2], inv3[:, 1:2], scale3[:, 0:1], su, ALU.mult, ALU.mult)
            for b in range(B):
                t = t3[:, :, b, :]
                scalars(t, t, ratio3[:, 1:2], RNE, ALU.mult, ALU.add)
                nc.vector.tensor_scalar(t, t, -RNE, scale3[:, 1:2], ALU.add, ALU.mult).then_inc(o3_ok, 1)
            add_result(5, 12)
            nc.vector.memset(stats[:, 0, 0:1], 0.0).then_inc(x_final, 1)


def kernel(**inputs):
    import numpy as np
    import concourse.bacc as bacc
    from concourse.bass_utils import run_bass_kernel_spmd

    nc = bacc.Bacc("TRN2", target_bir_lowering=False, num_devices=1)
    arrays, handles = {}, {}
    for name, value in inputs.items():
        array = np.ascontiguousarray(value)
        arrays["in_" + name] = array
        handles[name] = nc.dram_tensor("in_" + name, array.shape, mybir.dt.from_np(array.dtype), kind="ExternalInput").ap()
    out = nc.dram_tensor("out_x", inputs["x"].shape, F32, kind="ExternalOutput").ap()
    build(nc, handles, out)
    result = run_bass_kernel_spmd(nc, [arrays], core_ids=[0])
    return result.results[0]["out_x"]
```

```python
from contextlib import ExitStack

import concourse.bass as bass
from concourse import mybir

ALU = mybir.AluOpType
ACT = mybir.ActivationFunctionType
AX = mybir.AxisListType
F32 = mybir.dt.float32
BF16 = mybir.dt.bfloat16
U8 = mybir.dt.uint8
F32R = mybir.dt.float32r

P = 128
B = 2
NT = 8
TPB = NT // B
EPS = 1e-5
RNE = 1.5 * 2.0 ** 23
MASKED = -3e38


class Steps:

    def __init__(self, engine, semaphore):
        self.engine, self.semaphore, self.made = engine, semaphore, 0

    def add(self, instruction):
        instruction.then_inc(self.semaphore, 1)
        self.made += 1

    def settle(self):
        self.engine.wait_ge(self.semaphore, self.made)


def build(nc, a, out):
    S = a["x"].shape[1]
    D = a["x"].shape[2]
    NC = a["ctx_1024"].shape[1]
    H0 = a["L0_xattn_Wq"].shape[1] // D
    NK = S + NC
    NCH = TPB + 1
    U0 = H0 * B
    SC0 = float(D) ** -0.5
    E, _, F1 = a["L0_ffn_W1"].shape
    FT = F1 // P
    SC1 = 16 ** -0.5
    HM = a["mask_Bx16xSxS2_bk1"].shape[1]
    DH = D // HM
    SC16 = float(DH) ** -0.5
    PK = 64
    LK = NC - PK
    NPAIR = HM // 2
    LH = HM // 2
    LP = LH * LK
    BK = HM // 4
    I2 = a["L2_ffn_w_gate"].shape[0]
    I3 = a["L3_ffn_w_gate"].shape[0]
    IT = 3
    rows2 = [P, P, I2 - 2 * P]
    assert LP <= P and I3 == IT * P
    assert D == P and S == TPB * P

    with ExitStack() as ctx:
        def sb(name, shape, dt=F32):
            return ctx.enter_context(nc.sbuf_tensor(name, shape, dt))

        def sem(name):
            return ctx.enter_context(nc.semaphore(name))

        bank = ctx.enter_context(nc.psum_tensor("bank", [P, 8, 512], F32))

        x = sb("x_residual", [P, NT, D])
        ident = sb("ident", [P, P])
        ones = sb("ones", [P, P])
        minus_half = sb("minus_half", [P, 16])
        xn = sb("xn", [P, NT, D])
        xnT = sb("xnT", [P, B, S])
        stats = sb("stats", [P, NT, 6])
        meanvar = sb("meanvar", [P, NT, 2])
        var_eps = sb("var_eps", [P, NT])
        rstd = sb("rstd", [P, NT])
        rstd_again = sb("rstd_again", [P, NT])

        ctx_tok = sb("ctx_tok", [NC, B, D])
        ctxT = sb("ctxT", [P, B, NC])
        ctx_stats = sb("ctx_stats", [NC, B, 6])
        ctx_meanvar = sb("ctx_meanvar", [NC, B, 2])
        ctx_var_eps = sb("ctx_var_eps", [NC, B])
        ctx_rstd = sb("ctx_rstd", [NC, B])
        ctx_norm = sb("ctx_norm", [NC, B, D])
        gamma_ctx = sb("gamma_ctx", [NC, D])
        beta_ctx = sb("beta_ctx", [NC, D])
        gamma_lat = sb("gamma_lat", [P, D])
        beta_lat = sb("beta_lat", [P, D])
        bo0 = sb("bo0", [P, D])
        out_bias0 = sb("out_bias0", [P, D])
        HI, LO = range(2)
        kvT = [sb(f"kvT_{n}", [P, B, NK + NK % 2], F32R) for n in ("hi", "lo")]
        kv_lat = [sb(f"kv_lat_{n}", [P, NT, D], F32R) for n in ("hi", "lo")]
        kv_ctx = [sb(f"kv_ctx_{n}", [NC, B, D], F32R) for n in ("hi", "lo")]

        VROWS = ["L0_xattn_bq", "bv0", "L0_ffn_b1", "L2_xattn_bq", "L2_xattn_bk", "L3_xattn_bq", "L3_xattn_bk",
                 "L2_xattn_bv", "L3_xattn_bv"]
        vsrc = {n: a[n] for n in VROWS if n != "bv0"}
        vsrc["bv0"] = a["L0_xattn_bkv"][H0 * D:]
        vsrc["L0_ffn_b1"] = a["L0_ffn_b1"].rearrange("e f -> (e f)")
        vrow, nrow = {}, 0
        for n in VROWS:
            k = vsrc[n].shape[0] // D
            vrow[n] = (nrow, k)
            nrow += k
        vec_rows = sb("vec_rows", [nrow, D])
        vec_cols = sb("vec_cols", [P, nrow])
        bq0_scaled = sb("bq0_scaled", [P, H0])
        bv0_wide = sb("bv0_wide", [P, 2, P])

        shared = sb("shared", [P, 4 * H0 * D + B * TPB * NK])
        wq0 = shared[:, 0:H0 * D]
        wkv0 = shared[:, H0 * D:3 * H0 * D]
        wo0 = shared[:, 3 * H0 * D:4 * H0 * D].rearrange("p (h d) -> p h d", h=H0)
        wT0 = sb("wT0", [P, 2, 3, P])
        ab0 = sb("ab0", [P, H0, 2 * P + 1])
        a_now = [sb(f"a_now_{n}", [P, P], F32R) for n in ("hi", "lo")]
        qT = [sb(f"qT_{n}", [P, B, S], F32R) for n in ("hi", "lo")]
        at = 4 * H0 * D
        prob = [shared[:, at + b * TPB * NK:at + (b + 1) * TPB * NK].rearrange("p (i k) -> p i k", i=TPB)
                for b in range(B)]
        SLOT = (0, 1, 2, 0, 1)
        probT = [sb(f"probT_{n}", [P, 3, S], F32R) for n in ("hi", "lo")]
        queries = sb("queries", [P, B, S])
        uT, q_full = queries[:, 0, :], queries[:, 1, :]
        neg_max = sb("neg_max", [P, B, TPB])
        row_sum = sb("row_sum", [P, B, TPB])
        row_inv = sb("row_inv", [P, B, TPB])

        w1 = sb("w1", [P, E, F1])
        w2 = sb("w2", [P, E, FT, D])
        w1_now = [part[:].rearrange("p c s -> p (c s)")[:, 0:2 * F1].rearrange("p (n f) -> p n f", n=2) for part in probT]
        wr = sb("wr", [P, E])
        br = sb("br", [P, E])
        b2 = sb("b2", [E, D])
        rank = sb("rank", [P, NT, E])
        logit = sb("logit", [P, NT, E])
        logit2 = sb("logit2", [P, NT, E])
        key = sb("key", [P, NT, E])
        pick = [sb(f"pick{i}", [P, NT, E]) for i in range(2)]
        top = [sb(f"top{i}", [P, NT]) for i in range(2)]
        top_key = sb("top_key", [P, NT])
        top_diff = sb("top_diff", [P, NT])
        top_exp = sb("top_exp", [P, NT])
        top_den = sb("top_den", [P, NT])
        top_w = [sb(f"top_w{i}", [P, NT]) for i in range(2)]
        gate = sb("gate", [P, NT, E])
        scratch = sb("scratch", [P, 2 * HM * NC])
        gateT = scratch[0:E, 0:NT * P].rearrange("e (t p) -> e t p", t=NT)
        hT = sb("hT", [P, 2, FT, B, S])

        l1w = sb("l1w", [P, 7, D])
        L1Q, L1K, L1V, L1P, L1F, L1A, L1B = range(7)
        bp1 = sb("bp1", [P, D])
        fbias1 = sb("fbias1", [P, D])
        l1T = sb("l1T", [P, 2, P])
        k1T = sb("k1T", [P, B, NC])
        kq1 = sb("kq1", [P, B, NC])
        v1 = sb("v1", [NC, B, D])
        wa1T = sb("wa1T", [P, P])
        waa1 = sb("waa1", [P, D])
        s1 = sb("s1", [P, NT, NC])
        neg_max1 = sb("neg_max1", [P, NT])
        sum1 = sb("sum1", [P, NT])
        inv1 = sb("inv1", [P, NT])
        p1T = scratch[0:NC, 0:NT * P].rearrange("k (t p) -> k t p", t=NT)
        turned = hT[:].rearrange("p a j b s -> p (a j b s)")[:, 0:B * S].rearrange("p (b s) -> p b s", b=B)
        tanh_in = scratch[:, 0:NT * D].rearrange("p (t d) -> p t d", t=NT)

        mask_at = NT * HM * NC // 2
        maskb = shared[:, mask_at:mask_at + NT * HM * NC // 4].bitcast(U8).rearrange("p (t n) -> p t n", t=NT)
        mask_neg = shared[:, 0:NT * HM * NC // 2].bitcast(BF16).rearrange("p (t n) -> p t n", t=NT)
        w16 = sb("w16", [P, 2, 4, D])
        WQ, WK, WV, WO = range(4)
        bo16 = sb("bo16", [P, 2, D])
        bq16 = sb("bq16", [P, 2])
        head_of_row = sb("head_of_row", [P, HM])
        half_of_row = sb("half_of_row", [P, 2])
        left_of_row = sb("left_of_row", [LP, LH])
        ctx_pair = sb("ctx_pair", [P, B, 2, PK])
        ctx_left = sb("ctx_left", [P, B, LH, LK])
        k16T = sb("k16T", [P, 2, B, NC])
        k_blocks = sb("k_blocks", [P, B, HM, NC])
        v_pair = sb("v_pair", [P, 2, B, D])
        v_left = sb("v_left", [LP, 2, B, D])
        va_pair = sb("va_pair", [P, 2, B, NPAIR, 2, DH + 1])
        va_left = sb("va_left", [LP, 2, B, HM, DH + 1])
        q16T = queries
        s16 = scratch[:].rearrange("p (z h k) -> p z h k", z=2, h=HM)
        neg_max16 = sb("neg_max16", [P, 2, HM])
        keep16 = sb("keep16", [P, HM])
        spoil16 = sb("spoil16", [P, 4, HM])
        inv16 = sb("inv16", [P, 2, HM])
        p16 = hT[:].rearrange("p a j b s -> p (a j b s)")[:, 0:2 * HM * NC].rearrange("p (z n) -> p z n", z=2)
        p16T = w2[:].rearrange("p e j d -> p (e j) d")[:, 0:NPAIR + 2, :]
        o16 = shared[:, 3 * mask_at // 2:3 * mask_at // 2 + NT * D].rearrange("p (t d) -> p t d", t=NT)

        def late(at, *dims):
            n = 1
            for d in dims:
                n *= d
            v = shared[:, at:at + n]
            return v.rearrange("p (i b s) -> p i b s", i=dims[0], b=dims[1]), at + n

        val, at = late(0, IT, B, S)
        val2, at = late(at, IT, B, S)
        tanh_out = shared[:, at:at + 2 * S].rearrange("p (n s) -> p n s", n=2)
        silu_in = shared[:, at + 2 * S:at + 3 * S]
        t3 = hT[:].rearrange("p a j b s -> p (a j b s)")[:, 0:IT * B * S].rearrange("p (i b s) -> p i b s", i=IT, b=B)
        w1_half = w1[:].rearrange("p e f -> p (e f)").bitcast(BF16)
        xqT = w1_half[:, 0:B * S].rearrange("p (b s) -> p b s", b=B)
        hq = w1_half[:, B * S:(1 + IT) * B * S].rearrange("p (i b s) -> p i b s", i=IT, b=B)
        wn2 = sb("wn2", [P, 3, IT * P])
        wmax2 = sb("wmax2", [P, 7])
        wscale2 = sb("wscale2", [P, 7])
        winv2 = sb("winv2", [P, 7])
        ab0_flat = ab0[:].rearrange("p h n -> p (h n)")
        w3T = ab0_flat[:, 0:3 * IT * P].rearrange("p (m n) -> p m n", m=3)
        w2T = ab0_flat[:, 3 * IT * P:3 * IT * P + 3 * IT * P // 2].bitcast(BF16).rearrange("p (m n) -> p m n", m=3)
        diag_down = sb("diag_down", [P, P])
        down_row = sb("down_row", [P, D])
        down_scale = sb("down_scale", [P, D])
        clip = sb("clip", [P, 2])
        clip_sig = sb("clip_sig", [P, 2])
        minus_rne = sb("minus_rne", [P, 1])
        plus_rne = sb("plus_rne", [P, 1])
        wn3 = sb("wn3", [P, 3 * IT * 4, 32])
        wmax3 = sb("wmax3", [P, 3 * IT * 4])
        wscale3 = sb("wscale3", [P, 3 * IT * 4])
        winv3 = sb("winv3", [P, 3 * IT * 4])
        pmax = sb("pmax", [P, 2])
        gmax_row = sb("gmax_row", [1, 2])
        unit_max = sb("unit_max", [P, 2, IT * B])
        x_scale = sb("x_scale", [P, 1])
        x_inv = sb("x_inv", [P, 1])
        h_scale = sb("h_scale", [P, 1])
        h_inv = sb("h_inv", [P, 1])
        c_gate = sb("c_gate", [P, IT])
        c_both = sb("c_both", [P, IT])
        ug_scale = sb("ug_scale", [P, 2])
        ug_inv = sb("ug_inv", [P, 2])
        half_sg = sb("half_sg", [P, 1])
        amax3 = sb("amax3", [P, 2])
        scale3 = sb("scale3", [P, 2])
        inv3 = sb("inv3", [P, 2])
        ratio3 = sb("ratio3", [P, 2])

        in_x = [sem("in_x0"), sem("in_x1")]
        in_ctx = sem("in_ctx")
        in_vec = sem("in_vec")
        in_norm = sem("in_norm")
        in_w0 = [sem(f"in_w0_{n}") for n in range(2)]
        const_made = sem("const_made")
        ident_made = sem("ident_made")
        dve_step = sem("dve_step")
        act_step = sem("act_step")
        pool_step = sem("pool_step")
        ctx_var_ok = sem("ctx_var_ok")
        ctx_rstd_ok = sem("ctx_rstd_ok")
        ctx_norm_ok = sem("ctx_norm_ok")
        var_ok = sem("var_ok")
        rstd_ok = sem("rstd_ok")
        xn_ok = sem("xn_ok")
        xT_in_psum = sem("xT_in_psum")
        xnT_b_ok = [sem("xnT0_ok"), sem("xnT1_ok")]
        cT_in_psum = sem("cT_in_psum")
        cT_ok = sem("cT_ok")
        vcol_in_psum = sem("vcol_in_psum")
        vcol_ok = sem("vcol_ok")
        bv_wide_ok = sem("bv_wide_ok")
        bv_used = sem("bv_used")
        wT_in_psum = sem("wT_in_psum")
        wT_ok = sem("wT_ok")
        ab_in_psum = sem("ab_in_psum")
        ab_ok = sem("ab_ok")
        a_now_ok = sem("a_now_ok")
        bias0_ok = sem("bias0_ok")
        x_biased = sem("x_biased")
        q_in_psum = sem("q_in_psum")
        q_full_ok = sem("q_full_ok")
        cT_lo_ok = sem("cT_lo_ok")
        q_ok = sem("q_ok")
        scores_ok = sem("scores_ok")
        max_ok = sem("max_ok")
        prob_ok = sem("prob_ok")
        pT_in_psum = sem("pT_in_psum")
        kv_lat_ok = sem("kv_lat_ok")
        xn_hi_ok = sem("xn_hi_ok")
        xn_lo_ok = sem("xn_lo_ok")
        kvT_hi_ok = [sem("kvT_hi_ok0"), sem("kvT_hi_ok1")]
        kvT_lo_ok = [sem("kvT_lo_ok0"), sem("kvT_lo_ok1")]
        pad_ok = sem("pad_ok")
        q_hi_ok = sem("q_hi_ok")
        pT_hi_ok = sem("pT_hi_ok")
        pT_lo_ok = sem("pT_lo_ok")
        pv_done = sem("pv_done")
        u_ok = sem("u_ok")
        o_in_psum = sem("o_in_psum")
        inv_ok = sem("inv_ok")
        o_added = sem("o_added")
        in_moe = sem("in_moe")
        in_l1 = sem("in_l1")
        rank_ok = sem("rank_ok")
        w1_now_ok = sem("w1_now_ok")
        logit_in_psum = sem("logit_in_psum")
        diff_ok = sem("diff_ok")
        top_exp_ok = sem("top_exp_ok")
        gate_ok = sem("gate_ok")
        gT_in_psum = sem("gT_in_psum")
        gT_ok = sem("gT_ok")
        b2_in_psum = sem("b2_in_psum")
        b2_added = sem("b2_added")
        h_in_psum = sem("h_in_psum")
        h_ok = sem("h_ok")
        y_in_psum = sem("y_in_psum")
        y_added = sem("y_added")
        l1_in_psum = sem("l1_in_psum")
        l1_ok = sem("l1_ok")
        s1_in_psum = sem("s1_in_psum")
        s1_ok = sem("s1_ok")
        p1_ok = sem("p1_ok")
        p1T_in_psum = sem("p1T_in_psum")
        p1T_ok = sem("p1T_ok")
        o1_in_psum = sem("o1_in_psum")
        turned_ok = sem("turned_ok")
        res_in_psum = sem("res_in_psum")
        tanh_in_ok = sem("tanh_in_ok")
        tanh_ok = sem("tanh_ok")
        x_done = sem("x_done")
        in_mask = sem("in_mask")
        in_l16 = [sem("in_l2_attention"), sem("in_l3_attention")]
        in_f2 = sem("in_f2")
        in_f3 = sem("in_f3")
        mask_neg_ok = sem("mask_neg_ok")
        vcol_used = sem("vcol_used")
        ctx_spread = sem("ctx_spread")
        kv16_in_psum = sem("kv16_in_psum")
        kv16_ok = sem("kv16_ok")
        kv16_spread = sem("kv16_spread")
        q16_in_psum = sem("q16_in_psum")
        q16_ok = sem("q16_ok")
        s16_in_psum = sem("s16_in_psum")
        s16_taken = sem("s16_taken")
        s16_ok = sem("s16_ok")
        max16_ok = sem("max16_ok")
        spoil16_ok = sem("spoil16_ok")
        p16_ok = sem("p16_ok")
        p16T_in_psum = sem("p16T_in_psum")
        p16T_ok = sem("p16T_ok")
        o16_in_psum = sem("o16_in_psum")
        o16_ok = sem("o16_ok")
        o16T_in_psum = sem("o16T_in_psum")
        o16T_ok = sem("o16T_ok")
        rne_made = sem("rne_made")
        clip_tanh_ok = sem("clip_tanh_ok")
        wmax_ok = sem("wmax_ok")
        wq2_ok = sem("wq2_ok")
        wq3_ok = sem("wq3_ok")
        w2T_in_psum = sem("w2T_in_psum")
        w2T_ok = sem("w2T_ok")
        w3T_in_psum = sem("w3T_in_psum")
        w3T_ok = sem("w3T_ok")
        xq_ok = sem("xq_ok")
        pmax_ok = sem("pmax_ok")
        pmaxT_in_psum = sem("pmaxT_in_psum")
        gmax_ok = sem("gmax_ok")
        gmax_in_psum = sem("gmax_in_psum")
        c_ok = sem("c_ok")
        gu_in_psum = sem("gu_in_psum")
        gu_tanh_ok = sem("gu_tanh_ok")
        gu_taken = sem("gu_taken")
        hscale_ok = sem("hscale_ok")
        h_rounded = sem("h_rounded")
        hq_ok = sem("hq_ok")
        ug_in_psum = sem("ug_in_psum")
        ug_copied = sem("ug_copied")
        ug_maxed = sem("ug_maxed")
        ug_scale_ok = sem("ug_scale_ok")
        gate_int_ok = sem("gate_int_ok")
        up_int_ok = sem("up_int_ok")
        tanh3_ok = sem("tanh3_ok")
        o3_ok = sem("o3_ok")
        x_final = sem("x_final")
        out_done = sem("out_done")

        block = ctx.enter_context(nc.Block())

        def chunk_keys(c):
            return P if c < TPB else NC

        PT_BANK = ((4, 5, 4, 5, 4), (5, 4, 5, 4, 5))

        def wait_from(eng, semaphore, count):
            if not isinstance(count, int) or count > 0:
                eng.wait_ge(semaphore, count)

        def slot_free(eng, u, c):
            wait_from(eng, pv_done, NCH * u + c + 1 - (2, 2, NCH, 3, 3)[c])

        def run_heads(eng, step):
            def head(h, first, last):
                for b in range(B):
                    for c in range(NCH):
                        step(h, b, c, first, last)
            head(0, True, False)
            head(1, False, False)
            with eng.Fori(2, H0 - 1) as h:
                head(h, False, False)
            head(H0 - 1, False, True)

        def split_matmul(out, lhsT, rhs, first=True, last=True):
            nc.tensor.matmul(out, lhsT[HI], rhs[HI], start=first, stop=False)
            nc.tensor.matmul(out, lhsT[HI], rhs[LO], start=False, stop=False)
            return nc.tensor.matmul(out, lhsT[LO], rhs[HI], start=False, stop=last)

        @block.sync
        def _(sp):
            half = H0 // 2
            for n in range(2):
                c = slice(n * half * D, (n + 1) * half * D)
                v = slice((H0 + n * half) * D, (H0 + (n + 1) * half) * D)
                sp.dma_start(wq0[:, c], a["L0_xattn_Wq"][:, c]).then_inc(in_w0[n], 16)
                sp.dma_start(wkv0[:, c], a["L0_xattn_Wkv"][:, c]).then_inc(in_w0[n], 16)
                sp.dma_start(wkv0[:, v], a["L0_xattn_Wkv"][:, v]).then_inc(in_w0[n], 16)
                sp.dma_start(wo0[:, n * half:(n + 1) * half, :],
                             a["L0_xattn_Wo"][c, :].rearrange("(h d) n -> d h n", d=D)).then_inc(in_w0[n], 16)
            sp.dma_start(w1[:], a["L0_ffn_W1"].rearrange("e h f -> h e f")).then_inc(in_moe, 16)
            sp.dma_start(w2[:], a["L0_ffn_W2"].rearrange("e (j p) o -> p e j o", p=P)).then_inc(in_moe, 16)
            sp.dma_start(wr[:], a["L0_ffn_Wr"]).then_inc(in_moe, 16)
            sp.dma_start(br[:], a["L0_ffn_br"].partition_broadcast(P)).then_inc(in_moe, 16)
            sp.dma_start(b2[:], a["L0_ffn_b2"]).then_inc(in_moe, 16)
            for n, name in ((L1Q, "xattn_Wq"), (L1K, "xattn_Wk"), (L1V, "xattn_Wv"), (L1P, "xattn_Wp"),
                            (L1F, "ffn_weight"), (L1A, "ffn_aux_weight1"), (L1B, "ffn_aux_weight2")):
                sp.dma_start(l1w[:, n, :], a["L1_" + name]).then_inc(in_l1, 16)
            sp.dma_start(bp1[:], a["L1_xattn_bp"].partition_broadcast(P)).then_inc(in_l1, 16)
            sp.dma_start(fbias1[:], a["L1_ffn_bias"].partition_broadcast(P)).then_inc(in_l1, 16)
            for n in range(2):
                for m, name in enumerate(("Wq", "Wk", "Wv", "Wo")):
                    sp.dma_start(w16[:, n, m, :], a[f"L{n + 2}_xattn_{name}"]).then_inc(in_l16[n], 16)
                sp.dma_start(bo16[:, n, :], a[f"L{n + 2}_xattn_bo"].partition_broadcast(P)).then_inc(in_l16[n], 16)
            for m, name in enumerate(("gate", "up")):
                w = a["L2_ffn_w_" + name]
                sp.dma_start(wn2[:, m, 0:2 * P].rearrange("p (i d) -> p i d", i=2),
                             w[0:2 * P, :].rearrange("(i p) d -> p i d", p=P)).then_inc(in_f2, 16)
                sp.dma_start(wn2[0:rows2[2], m, 2 * P:3 * P], w[2 * P:I2, :]).then_inc(in_f2, 16)
                sp.dma_start(wn3[:, 4 * IT * m:4 * IT * (m + 1), :].rearrange("p (i b) k -> p i (b k)", i=IT),
                             a["L3_ffn_w_" + name].rearrange("(i p) d -> p i d", p=P)).then_inc(in_f3, 16)
            sp.dma_start(wn2[:, 2, 0:I2], a["L2_ffn_w_down"]).then_inc(in_f2, 16)
            sp.dma_start(wn3[:, 8 * IT:12 * IT, :].rearrange("p b k -> p (b k)"), a["L3_ffn_w_down"]).then_inc(in_f3, 16)
            sp.dma_start(clip[:, 0:1], a["L2_ffn_clip_x"].partition_broadcast(P)).then_inc(in_f2, 16)
            sp.dma_start(clip[:, 1:2], a["L2_ffn_clip_down"].partition_broadcast(P)).then_inc(in_f2, 16)
            sp.wait_ge(o_in_psum, U0)
            for t in range(NT):
                b, i = t // TPB, t % TPB
                sp.dma_start(maskb[:, t, :].rearrange("p (h k) -> p h k", h=HM),
                             a["mask_Bx16xSxS2_bk1"][b, :, i * P:(i + 1) * P, :].rearrange("h p k -> p h k"))\
                    .then_inc(in_mask, 16)
            sp.wait_ge(x_final, 1)
            sp.dma_start(out.rearrange("b (t p) d -> p b t d", p=P),
                         x[:].rearrange("p (b t) d -> p b t d", b=B)).then_inc(out_done, 16)
            sp.wait_ge(out_done, 16)

        @block.gpsimd
        def _(pool):
            own = Steps(pool, pool_step)
            nc.gpsimd.memset(ones[:], 1.0).then_inc(const_made, 1)
            nc.gpsimd.memset(minus_half[:], -0.5).then_inc(const_made, 1)
            own.add(nc.gpsimd.memset(ident[:], 0.0))
            own.settle()
            nc.gpsimd.affine_select(out=ident[:], in_=ident[:], compare_op=ALU.not_equal, fill=1.0, base=0,
                                    pattern=[[-1, P]], channel_multiplier=1).then_inc(ident_made, 1)
            pool.wait_ge(const_made, 2)
            pool.wait_ge(ctx_var_ok, 1)
            nc.gpsimd.tensor_tensor(ctx_rstd[:], ctx_var_eps[:], minus_half[0:NC, 0:B], ALU.pow).then_inc(ctx_rstd_ok, 1)
            for b in range(B):
                c = slice(TPB * b, TPB * (b + 1))
                pool.wait_ge(var_ok, b + 1)
                own.add(nc.gpsimd.tensor_tensor(rstd[:, c], var_eps[:, c], minus_half[:, 0:TPB], ALU.pow))
                own.settle()
                own.add(nc.gpsimd.tensor_tensor(rstd_again[:, c], rstd[:, c], rstd[:, c], ALU.mult))
                own.settle()
                own.add(nc.gpsimd.tensor_tensor(rstd_again[:, c], rstd_again[:, c], meanvar[:, c, 1], ALU.mult))
                own.settle()
                own.add(nc.gpsimd.tensor_scalar(rstd_again[:, c], rstd_again[:, c], EPS, None, ALU.add))
                own.settle()
                own.add(nc.gpsimd.tensor_tensor(rstd_again[:, c], rstd_again[:, c], minus_half[:, 0:TPB], ALU.pow))
                own.settle()
                nc.gpsimd.tensor_tensor(rstd[:, c], rstd[:, c], rstd_again[:, c], ALU.mult).then_inc(rstd_ok, 1)
            if NK % 2:
                for part in kvT:
                    nc.gpsimd.memset(part[:, :, NK:NK + 1].bitcast(F32), 0.0).then_inc(pad_ok, 1)
            pool.wait_ge(vcol_ok, 1)
            col = vrow["bv0"][0]
            for h in range(H0):
                if h >= 2:
                    pool.wait_ge(bv_used, h - 1)
                nc.gpsimd.tensor_scalar(bv0_wide[:, h % 2, :], ones[:], vec_cols[:, col + h:col + h + 1], None,
                                        ALU.mult).then_inc(bv_wide_ok, 1)
            def stationary(h):
                pool.wait_ge(ab_ok, h + 1)
                if h >= 1:
                    pool.wait_ge(q_in_psum, B * h)
                own.add(nc.gpsimd.tensor_copy(a_now[HI][:], ab0[:, h, 0:P]))
                own.settle()
                nc.gpsimd.tensor_tensor(a_now[LO][:], ab0[:, h, 0:P], a_now[HI][:].bitcast(F32), ALU.subtract)\
                    .then_inc(a_now_ok, 1)

            stationary(0)
            pool.wait_ge(bias0_ok, 1)
            pool.wait_ge(xn_ok, NT)
            nc.gpsimd.tensor_tensor(x[:], x[:], out_bias0[:].unsqueeze(1).to_broadcast([P, NT, D]), ALU.add)\
                .then_inc(x_biased, 1)
            nc.gpsimd.memset(plus_rne[:], RNE).then_inc(rne_made, 1)
            nc.gpsimd.memset(minus_rne[:], -RNE).then_inc(rne_made, 1)
            for tile, width, count in ((head_of_row, DH, HM), (half_of_row, PK, 2), (left_of_row, LK, LH)):
                own.add(nc.gpsimd.memset(tile[:], 1.0))
                own.settle()
                own.add(nc.gpsimd.affine_select(out=tile[:], in_=tile[:], compare_op=ALU.is_ge, fill=0.0, base=0,
                                                pattern=[[-width, count]], channel_multiplier=1))
                own.settle()
                own.add(nc.gpsimd.affine_select(out=tile[:], in_=tile[:], compare_op=ALU.is_ge, fill=0.0,
                                                base=width - 1, pattern=[[width, count]], channel_multiplier=-1))
                own.settle()
            pool.wait_ge(cT_ok, 2)
            nc.gpsimd.tensor_copy(ctx_pair[:], ctxT[:, :, 0:PK].unsqueeze(2).to_broadcast([P, B, 2, PK]))\
                .then_inc(ctx_spread, 1)
            nc.gpsimd.tensor_copy(ctx_left[:], ctxT[:, :, PK:NC].unsqueeze(2).to_broadcast([P, B, LH, LK]))\
                .then_inc(ctx_spread, 1)
            for e in range(E):
                nc.gpsimd.memset(rank[:, :, e:e + 1], float(E - e)).then_inc(rank_ok, 1)

            def inverse_root(k):
                for b in range(B):
                    c = slice(TPB * b, TPB * (b + 1))
                    pool.wait_ge(var_ok, B * k + b + 1)
                    nc.gpsimd.tensor_tensor(rstd[:, c], var_eps[:, c], minus_half[:, 0:TPB], ALU.pow)\
                        .then_inc(rstd_ok, 1)

            def add_bias(k, bias):
                pool.wait_ge(xn_ok, NT * (k + 1))
                nc.gpsimd.tensor_tensor(x[:], x[:], bias.unsqueeze(1).to_broadcast([P, NT, D]), ALU.add)\
                    .then_inc(x_biased, 1)

            def whole_weights2():
                pool.wait_ge(wmax_ok, 1)
                for m in range(2):
                    for i in range(IT):
                        w, r = wn2[0:rows2[i], m, i * P:(i + 1) * P], rows2[i]
                        own.add(nc.gpsimd.tensor_scalar(w, w, winv2[0:r, IT * m + i:IT * m + i + 1], RNE, ALU.mult, ALU.add))
                w = wn2[:, 2, 0:I2]
                own.add(nc.gpsimd.tensor_scalar(w, w, winv2[:, 6:7], RNE, ALU.mult, ALU.add))
                own.settle()
                for m in range(2):
                    for i in range(IT):
                        w = wn2[0:rows2[i], m, i * P:(i + 1) * P]
                        nc.gpsimd.tensor_scalar(w, w, -RNE, None, ALU.add).then_inc(wq2_ok, 1)
                w = wn2[:, 2, 0:I2]
                nc.gpsimd.tensor_scalar(w, w, -RNE, None, ALU.add).then_inc(wq2_ok, 1)
                nc.gpsimd.tensor_scalar(diag_down[:], ident[:], wscale2[:, 6:7], None, ALU.mult).then_inc(wq2_ok, 1)

            def whole_weights3(m):
                pool.wait_ge(wmax_ok, 2)
                w, c = wn3[:, 4 * IT * m:4 * IT * (m + 1), :], slice(4 * IT * m, 4 * IT * (m + 1))
                own.add(nc.gpsimd.tensor_tensor(w, w, winv3[:, c].unsqueeze(2).to_broadcast([P, 4 * IT, 32]), ALU.mult))
                own.settle()
                own.add(nc.gpsimd.tensor_scalar(w, w, RNE, None, ALU.add))
                own.settle()
                own.add(nc.gpsimd.tensor_scalar(w, w, -RNE, None, ALU.add))
                own.settle()
                nc.gpsimd.tensor_tensor(w, w, wscale3[:, c].unsqueeze(2).to_broadcast([P, 4 * IT, 32]), ALU.mult)\
                    .then_inc(wq3_ok, 1)

            for h in range(1, H0):
                stationary(h)
                if h == 3:
                    whole_weights2()
                if h in (4, 5, 6):
                    whole_weights3(h - 4)

            def spread_kv(n):
                pool.wait_ge(kv16_ok, 3 * (n + 1))
                if n:
                    pool.wait_ge(s16_in_psum, NT)
                for b in range(B):
                    nc.gpsimd.tensor_tensor(k_blocks[:, b], k16T[:, n, b, :].unsqueeze(1).to_broadcast([P, HM, NC]),
                                            head_of_row[:].unsqueeze(2).to_broadcast([P, HM, NC]), ALU.mult)\
                        .then_inc(kv16_spread, 1)
                    half = half_of_row[:].unsqueeze(1)
                    for hd in range(2):
                        nc.gpsimd.tensor_scalar(va_pair[:, n, b, :, hd, 0:DH],
                                                v_pair[:, n, b, :].rearrange("p (c h d) -> p c h d", c=NPAIR, h=2)[:, :, hd, :],
                                                half_of_row[:, hd:hd + 1], None, ALU.mult).then_inc(kv16_spread, 1)
                    nc.gpsimd.tensor_copy(va_pair[:, n, b, :, :, DH], half.to_broadcast([P, NPAIR, 2]))\
                        .then_inc(kv16_spread, 1)
                    for g in range(2):
                        nc.gpsimd.tensor_tensor(va_left[:, n, b, LH * g:LH * (g + 1), 0:DH],
                                                v_left[:, n, b, LH * DH * g:LH * DH * (g + 1)].rearrange("p (h d) -> p h d", h=LH),
                                                left_of_row[:].unsqueeze(2).to_broadcast([LP, LH, DH]), ALU.mult)\
                            .then_inc(kv16_spread, 1)
                        nc.gpsimd.tensor_copy(va_left[:, n, b, LH * g:LH * (g + 1), DH], left_of_row[:])\
                            .then_inc(kv16_spread, 1)

            def less_maximum(t, n):
                pool.wait_ge(max16_ok, NT * n + t + 1)
                nc.gpsimd.tensor_tensor(s16[:, t % 2], s16[:, t % 2],
                                        neg_max16[:, t % 2, :].unsqueeze(2).to_broadcast([P, HM, NC]), ALU.add)\
                    .then_inc(s16_ok, 1)

            pool.wait_ge(in_moe, 16 * 5)
            inverse_root(1)
            pool.wait_ge(pv_done, NCH * U0)
            for e in range(E):
                if e >= 2:
                    pool.wait_ge(h_in_psum, FT * B * (e - 1))
                own.add(nc.gpsimd.tensor_copy(w1_now[HI][:, e % 2, :], w1[:, e, :]))
                own.settle()
                nc.gpsimd.tensor_tensor(w1_now[LO][:, e % 2, :], w1[:, e, :], w1_now[HI][:, e % 2, :].bitcast(F32),
                                        ALU.subtract).then_inc(w1_now_ok, 1)
                pool.wait_ge(in_mask, 16 * NT)
                pool.wait_ge(o_in_psum, U0)
                nc.gpsimd.tensor_scalar(mask_neg[:, e, :], maskb[:, e, :], MASKED, None, ALU.mult)\
                    .then_inc(mask_neg_ok, 1)
            inverse_root(2)
            pool.wait_ge(in_l1, 16 * 9)
            add_bias(2, bp1[:])
            spread_kv(0)
            inverse_root(3)
            inverse_root(4)
            add_bias(4, bo16[:, 0, :])
            for t in range(NT):
                less_maximum(t, 0)
                spoil = spoil16[:, t % 4, :]
                if t:
                    pool.wait_ge(spoil16_ok, t)
                if t >= 4:
                    pool.wait_ge(o16_ok, t - 3)
                own.add(nc.gpsimd.tensor_scalar(keep16[:], neg_max16[:, t % 2, :], 1e37, None, ALU.is_lt))
                own.settle()
                own.add(nc.gpsimd.tensor_scalar(spoil, keep16[:], -1.0, 3e38, ALU.add, ALU.mult))
                own.settle()
                own.add(nc.gpsimd.tensor_scalar(spoil, spoil, 3e38, None, ALU.mult))
                own.settle()
                nc.gpsimd.tensor_tensor(spoil, spoil, keep16[:], ALU.mult).then_inc(spoil16_ok, 1)
            inverse_root(5)
            spread_kv(1)
            inverse_root(6)
            add_bias(6, bo16[:, 1, :])
            for t in range(NT):
                less_maximum(t, 1)
            inverse_root(7)
            pool.wait_ge(ug_scale_ok, 1)
            pool.wait_ge(ug_copied, 2 * IT * B)
            for b in range(B):
                own.add(nc.gpsimd.tensor_scalar(val[:, :, b, :], val[:, :, b, :], ug_inv[:, 1:2], RNE, ALU.mult, ALU.add))
                own.settle()
                nc.gpsimd.tensor_scalar(val[:, :, b, :], val[:, :, b, :], -RNE, None, ALU.add).then_inc(up_int_ok, 1)

        @block.tensor
        def _(pe):
            pe.wait_ge(ident_made, 1)

            def keys_transposes():
                pe.wait_ge(ctx_norm_ok, 1)
                for b in range(B):
                    nc.tensor.transpose(bank[:, 6, b * P:b * P + NC], ctx_norm[:, b, :], ident[0:NC, 0:NC])
                for b in range(B):
                    last = nc.tensor.transpose(bank[:, 6, (B + b) * P:(B + b) * P + NC], ctx_tok[:, b, :], ident[0:NC, 0:NC])
                last.then_inc(cT_in_psum, 1)
                for t in range(NT):
                    pe.wait_ge(xn_ok, t + 1)
                    nc.tensor.transpose(bank[:, 4 + t // TPB, (t % TPB) * P:(t % TPB + 1) * P], xn[:, t, :], ident[:])\
                        .then_inc(xT_in_psum, 1)

            for h in range(H0 + 1):
                if h < H0:
                    c = slice(h * D, (h + 1) * D)
                    v = slice((H0 + h) * D, (H0 + h + 1) * D)
                    pe.wait_ge(in_w0[2 * h // H0], 64)
                    if h >= 2:
                        pe.wait_ge(wT_ok, h - 1)
                    for n, w in enumerate((wq0[:, c], wkv0[:, c], wkv0[:, v])):
                        last = nc.tensor.transpose(bank[:, h % 2, n * P:(n + 1) * P], w, ident[:])
                    last.then_inc(wT_in_psum, 1)
                if h == 1:
                    pe.wait_ge(in_vec, 16 * len(VROWS))
                    nc.tensor.transpose(bank[:, 6, 0:nrow], vec_rows[:], ident[0:nrow, 0:nrow]).then_inc(vcol_in_psum, 1)
                    pe.wait_ge(vcol_ok, 4)
                if h == H0 // 2:
                    keys_transposes()
                if h:
                    g = h - 1
                    rb = 2 + g % 2
                    pe.wait_ge(wT_ok, g + 1)
                    if g >= 2:
                        pe.wait_ge(ab_ok, g - 1)
                    nc.tensor.matmul(bank[:, rb, 0:P], wT0[:, g % 2, 0, :], wT0[:, g % 2, 1, :], start=True, stop=True)
                    nc.tensor.matmul(bank[:, rb, P:2 * P], wT0[:, g % 2, 2, :], wo0[:, g, :], start=True, stop=True)
                    nc.tensor.matmul(bank[:, rb, 2 * P:2 * P + 1], wT0[:, g % 2, 1, :], bq0_scaled[:, g:g + 1],
                                     start=True, stop=True).then_inc(ab_in_psum, 1)
                    pe.wait_ge(bv_wide_ok, g + 1)
                    nc.tensor.matmul(bank[:, 7, 0:D], bv0_wide[:, g % 2, :], wo0[:, g, :],
                                     start=(g == 0), stop=(g == H0 - 1)).then_inc(bv_used, 1)
            def query(h, b):
                u = B * h + b
                pe.wait_ge(a_now_ok, h + 1)
                wait_from(pe, o_added, u - 3)
                wait_from(pe, q_full_ok, u)
                split_matmul(bank[:, 7, :], [part[:] for part in a_now], [part[:, b, 0:S] for part in kvT])\
                    .then_inc(q_in_psum, 1)

            def scores(u, b, i):
                first = 2 * (i % 2)
                if i == 0:
                    pe.wait_ge(q_ok, u + 1)
                wait_from(pe, prob_ok, TPB * u + i - 1)
                q = [part[:, b, i * P:(i + 1) * P] for part in qT]
                lat, late = bank[:, first, :], bank[:, first + 1, 0:NC + NC % 2]
                wide = NK + NK % 2
                for stationary, moving in ((HI, HI), (HI, LO), (LO, HI)):
                    begin, end = stationary == moving, stationary == LO
                    nc.tensor.matmul(lat, q[stationary], kvT[moving][:, b, 0:S], start=begin, stop=end)
                    last = nc.tensor.matmul(late, q[stationary], kvT[moving][:, b, S:wide], start=begin, stop=end)
                last.then_inc(scores_ok, 1)

            def transpose_chunk(u, b, c):
                n = chunk_keys(c)
                if c == 0:
                    pe.wait_ge(prob_ok, TPB * (u + 1))
                wait_from(pe, pT_lo_ok, NCH * u + c - 1)
                for i in range(TPB):
                    last = nc.tensor.transpose(bank[0:n, PT_BANK[b][c], i * P:(i + 1) * P],
                                               prob[b][:, i, c * P:c * P + n], ident[:])
                last.then_inc(pT_in_psum, 1)

            def attend(u, b, c):
                n = chunk_keys(c)
                pe.wait_ge(pT_lo_ok, NCH * u + c + 1)
                if c == 0:
                    wait_from(pe, u_ok, u)
                kv = [kv_lat[m][:, TPB * b + c, :] if c < TPB else kv_ctx[m][:, b, :] for m in (HI, LO)]
                split_matmul(bank[:, 6, :], kv, [part[0:n, SLOT[c], :] for part in probT], c == 0, c == NCH - 1)\
                    .then_inc(pv_done, 1)

            def output(h, b, asked):
                u = B * h + b
                pe.wait_ge(u_ok, u + 1)
                pe.wait_ge(q_full_ok, asked)
                wait_from(pe, o_added, u)
                for i in range(TPB):
                    last = nc.tensor.matmul(bank[:, 7, i * P:(i + 1) * P], uT[:, i * P:(i + 1) * P],
                                            ab0[:, bass.ds(h, 1), P:2 * P].rearrange("p n m -> p (n m)"),
                                            start=True, stop=True)
                last.then_inc(o_in_psum, 1)

            def step(h, b, c, first, last):
                u = B * h + b
                if c == 2 and not (last and b):
                    query(h + b, 1 - b)
                if c < TPB:
                    scores(u, b, c)
                if not first or b:
                    transpose_chunk(u - 1, 1 - b, c)
                if c == TPB and not first:
                    output(h - 1, b, U0 if last and b else u + 2)
                if c == 0 and not first:
                    attend(u - 2, b, NCH - 1)
                if c and (not first or b):
                    attend(u - 1, 1 - b, c - 1)

            pe.wait_ge(bias0_ok, 1)
            pe.wait_ge(ab_ok, H0)
            for b in range(B):
                pe.wait_ge(kvT_lo_ok[b], 1)
            query(0, 0)
            pe.wait_ge(cT_lo_ok, 1)
            pe.wait_ge(kv_lat_ok, 2 * (B + 1))
            pe.wait_ge(pad_ok, 2)
            run_heads(pe, step)
            for c in range(NCH):
                transpose_chunk(U0 - 1, B - 1, c)
                attend(U0 - 1 if c else U0 - 2, B - 1 if c else 0, (c - 1) % NCH)
            output(H0 - 1, 0, U0)
            attend(U0 - 1, B - 1, NCH - 1)
            output(H0 - 1, B - 1, U0)

            def norm_transposes(k, quantised=None):
                for t in range(NT):
                    if quantised is None:
                        pe.wait_ge(xn_ok, NT * k + t + 1)
                    else:
                        pe.wait_ge(xq_ok, B * quantised + t // TPB + 1)
                    nc.tensor.transpose(bank[:, 4 + t // TPB, (t % TPB) * P:(t % TPB + 1) * P], xn[:, t, :], ident[:])\
                        .then_inc(xT_in_psum, 1)

            def tile_T(t):
                return xnT[:, t // TPB, (t % TPB) * P:(t % TPB + 1) * P]

            def normed(k):
                for b in range(B):
                    pe.wait_ge(xnT_b_ok[b], k)

            pe.wait_ge(in_l1, 16 * 9)
            pe.wait_ge(o_added, U0)
            pe.wait_ge(prob_ok, TPB * U0)
            both = ctxT[:].rearrange("p b k -> p (b k)")
            nc.tensor.transpose(bank[:, 0, 0:P], l1w[:, L1Q, :], ident[:])
            nc.tensor.transpose(bank[:, 0, P:2 * P], l1w[:, L1F, :], ident[:])
            nc.tensor.matmul(bank[:, 1, 0:B * NC], l1w[:, L1K, :], both, start=True, stop=True)
            for b in range(B):
                last = nc.tensor.matmul(bank[0:NC, 2, b * D:(b + 1) * D], ctxT[:, b, :], l1w[:, L1V, :],
                                        start=True, stop=True)
            last.then_inc(l1_in_psum, 1)
            pe.wait_ge(l1_ok, 3)
            nc.tensor.matmul(bank[:, 3, 0:B * NC], l1T[:, 0, :], k1T[:].rearrange("p b k -> p (b k)"),
                             start=True, stop=True)
            nc.tensor.matmul(bank[:, 3, 256:256 + P], l1w[:, L1A, :], l1T[:, 1, :], start=True, stop=True)\
                .then_inc(l1_in_psum, 1)
            pe.wait_ge(l1_ok, 5)
            nc.tensor.matmul(bank[:, 0, 0:D], wa1T[:], l1w[:, L1B, :], start=True, stop=True).then_inc(l1_in_psum, 1)
            pe.wait_ge(l1_ok, 6)

            norm_transposes(1)
            normed(1)
            pe.wait_ge(in_moe, 16 * 5)
            for t in range(NT):
                last = nc.tensor.matmul(bank[:, 6, t * E:(t + 1) * E], tile_T(t), wr[:], start=True, stop=True)
            last.then_inc(logit_in_psum, 1)

            def hidden(e):
                pe.wait_ge(w1_now_ok, e + 1)
                for j in range(FT):
                    for b in range(B):
                        n = j * B + b
                        if e >= 1:
                            pe.wait_ge(h_ok, FT * B * (e - 1) + n + 1)
                        if e == 0:
                            pe.wait_ge(xn_lo_ok, b + 1)
                        split_matmul(bank[:, n, :], [part[:, e % 2, j * P:(j + 1) * P] for part in w1_now],
                                     [part[:, b, :] for part in qT]).then_inc(h_in_psum, 1)

            def expert_out(e):
                pe.wait_ge(h_ok, FT * B * (e + 1))
                for b in range(B):
                    if e >= 1:
                        pe.wait_ge(y_added, B * (e - 1) + b + 1)
                    else:
                        pe.wait_ge(b2_added, b + 1)
                    for i in range(TPB):
                        for j in range(FT):
                            last = nc.tensor.matmul(bank[:, 6 + b, i * P:(i + 1) * P],
                                                    hT[:, e % 2, j, b, i * P:(i + 1) * P], w2[:, e, j, :],
                                                    start=(j == 0), stop=(j == FT - 1))
                    last.then_inc(y_in_psum, 1)

            hidden(0)
            pe.wait_ge(gate_ok, 1)
            for t in range(NT):
                last = nc.tensor.transpose(bank[0:E, 4 + t // TPB, (t % TPB) * P:(t % TPB + 1) * P],
                                           gate[:, t, :], ident[:])
            last.then_inc(gT_in_psum, 1)
            hidden(1)
            pe.wait_ge(gT_ok, 1)
            for t in range(NT):
                last = nc.tensor.matmul(bank[:, 6 + t // TPB, (t % TPB) * P:(t % TPB + 1) * P], gateT[:, t, :], b2[:],
                                        start=True, stop=True)
            last.then_inc(b2_in_psum, 1)
            expert_out(0)
            for e in range(2, E):
                hidden(e)
                expert_out(e - 1)
            expert_out(E - 1)

            def residual_out(k, weight):
                for b in range(B):
                    for i in range(TPB):
                        last = nc.tensor.matmul(bank[:, 6 + b, i * P:(i + 1) * P], weight[0](TPB * b + i), weight[1],
                                                start=True, stop=True)
                    last.then_inc(res_in_psum, 1)

            def keys_values(n):
                pe.wait_ge(in_l16[n], 80)
                pe.wait_ge(ctx_spread, 2)
                pe.wait_ge(s1_ok, B * n) if n else pe.wait_ge(h_ok, FT * B * E)
                nc.tensor.matmul(bank[:, 0, 0:B * NC], w16[:, n, WK, :], ctxT[:].rearrange("p b k -> p (b k)"),
                                 start=True, stop=True)
                for b in range(B):
                    nc.tensor.matmul(bank[:, 1, b * D:(b + 1) * D], ctx_pair[:, b].rearrange("p n k -> p (n k)"),
                                     w16[:, n, WV, :], start=True, stop=True)
                for b in range(B):
                    last = nc.tensor.matmul(bank[0:LP, 1, (B + b) * D:(B + b + 1) * D],
                                            ctx_left[:, b].rearrange("p n k -> p (n k)"), w16[:, n, WV, :],
                                            start=True, stop=True)
                last.then_inc(kv16_in_psum, 1)

            def global_max(j, count):
                pe.wait_ge(pmax_ok, j + 1)
                for c in range(count):
                    last = nc.tensor.transpose(bank[0:1, 7, c * P:(c + 1) * P], pmax[:, c:c + 1], ident[:])
                last.then_inc(pmaxT_in_psum, 1)
                pe.wait_ge(gmax_ok, j + 1)
                nc.tensor.matmul(bank[:, 7, 2 * P:2 * P + count], ones[0:1, :], gmax_row[:, 0:count],
                                 start=True, stop=True).then_inc(gmax_in_psum, 1)

            def attention16(n, k):
                norm_transposes(k)
                normed(k)
                for b in range(B):
                    nc.tensor.matmul(bank[:, 6 + b, :], w16[:, n, WQ, :], xnT[:, b, :], start=True, stop=True)\
                        .then_inc(q16_in_psum, 1)
                pe.wait_ge(kv16_spread, 8 * B * (n + 1))

                def scores(t):
                    b, m = t // TPB, NT * n + t
                    pe.wait_ge(q16_ok, B * n + b + 1)
                    q = q16T[:, b, (t % TPB) * P:(t % TPB + 1) * P]
                    if t:
                        pe.wait_ge(s16_taken, m)
                    for g in range(4):
                        last = nc.tensor.matmul(bank[:, g, 0:BK * NC], q,
                                                k_blocks[:, b, BK * g:BK * (g + 1), :].rearrange("p h k -> p (h k)"),
                                                start=True, stop=True)
                    last.then_inc(s16_in_psum, 1)

                def transposes(t):
                    m, z = NT * n + t, t % 2
                    pe.wait_ge(p16_ok, 2 * (m + 1))
                    pe.wait_ge(p16T_ok, 2 * m) if t else pe.wait_ge(q16_ok, B * (n + 1))
                    for c in range(NPAIR):
                        last = nc.tensor.transpose(bank[:, 4 + c // 4, (c % 4) * P:(c % 4 + 1) * P],
                                                   p16[:, z, 2 * PK * c:2 * PK * (c + 1)], ident[:])
                    last.then_inc(p16T_in_psum, 1)
                    for g in range(2):
                        first = HM * PK + LP * g
                        last = nc.tensor.transpose(bank[0:LP, 6, g * P:(g + 1) * P], p16[:, z, first:first + LP],
                                                   ident[:])
                    last.then_inc(p16T_in_psum, 1)

                def averages(t):
                    b, m = t // TPB, NT * n + t
                    pe.wait_ge(p16T_ok, 2 * m + 2)
                    if m >= 1:
                        pe.wait_ge(o16_ok, m)
                    o, w = bank[:, 7, 0:HM * (DH + 1)], DH + 1
                    for g in range(2):
                        nc.tensor.matmul(o[:, LH * w * g:LH * w * (g + 1)], p16T[0:LP, NPAIR + g, :],
                                         va_left[:, n, b, LH * g:LH * (g + 1), :].rearrange("p h d -> p (h d)"),
                                         start=(g == 0), stop=False, skip_group_check=True)
                    for c in range(NPAIR):
                        last = nc.tensor.matmul(o[:, 2 * w * c:2 * w * (c + 1)], p16T[:, c, :],
                                                va_pair[:, n, b, c].rearrange("p h d -> p (h d)"),
                                                start=False, stop=(c == NPAIR - 1), skip_group_check=True)
                    last.then_inc(o16_in_psum, 1)

                scores(0)
                scores(1)
                for t in range(NT + 1):
                    if t + 2 < NT:
                        scores(t + 2)
                    if t:
                        averages(t - 1)
                    if t < NT:
                        transposes(t)
                pe.wait_ge(o16_ok, NT * (n + 1))
                for t in range(NT):
                    last = nc.tensor.transpose(bank[:, t // TPB, (t % TPB) * P:(t % TPB + 1) * P], o16[:, t, :], ident[:])
                    if t % TPB == TPB - 1:
                        last.then_inc(o16T_in_psum, 1)
                pe.wait_ge(o16T_ok, B * (n + 1))
                residual_out(2 + 2 * n, (lambda t: q16T[:, t // TPB, (t % TPB) * P:(t % TPB + 1) * P], w16[:, n, WO, :]))

            keys_values(0)
            norm_transposes(2)
            normed(2)
            for t in range(NT):
                b, i = t // TPB, t % TPB
                last = nc.tensor.matmul(bank[:, b, i * NC:(i + 1) * NC], tile_T(t), kq1[:, b, :],
                                        start=True, stop=True)
                if i == TPB - 1:
                    last.then_inc(s1_in_psum, 1)
            for b in range(B):
                pe.wait_ge(p1_ok, b + 1)
                for i in range(TPB):
                    last = nc.tensor.transpose(bank[0:NC, 2 + b, i * P:(i + 1) * P], s1[:, TPB * b + i, :], ident[:])
                last.then_inc(p1T_in_psum, 1)
            for b in range(B):
                pe.wait_ge(p1T_ok, b + 1)
                for i in range(TPB):
                    last = nc.tensor.matmul(bank[:, 4 + b, i * P:(i + 1) * P], p1T[:, TPB * b + i, :], v1[:, b, :],
                                            start=True, stop=True)
                last.then_inc(o1_in_psum, 1)
            pe.wait_ge(y_added, B * E)
            pe.wait_ge(turned_ok, B)
            residual_out(0, (lambda t: turned[:, t // TPB, (t % TPB) * P:(t % TPB + 1) * P], l1w[:, L1P, :]))
            keys_values(1)
            norm_transposes(3)
            normed(3)
            pe.wait_ge(x_done, 2)
            residual_out(1, (tile_T, waa1[:]))
            pe.wait_ge(wq2_ok, 8)
            pe.wait_ge(kv16_ok, 6)
            for m in range(3):
                for i in range(IT):
                    r, to = rows2[i], bank[:, m, i * P:i * P + rows2[i]]
                    if m < 2:
                        nc.tensor.transpose(to, wn2[0:r, m, i * P:(i + 1) * P], ident[0:r, 0:r])
                    else:
                        nc.tensor.transpose(bank[0:r, m, i * P:(i + 1) * P], wn2[:, m, i * P:i * P + r], ident[:])
            nc.tensor.matmul(bank[:, 3, 0:P], ones[:], diag_down[:], start=True, stop=True).then_inc(w2T_in_psum, 1)
            attention16(0, 4)
            pe.wait_ge(wq3_ok, 3)
            pe.wait_ge(o16T_ok, B)
            w3 = wn3[:].rearrange("p (m i b) k -> p m i (b k)", m=3, i=IT)
            for m in range(3):
                for i in range(IT):
                    last = nc.tensor.transpose(bank[:, m, i * P:(i + 1) * P], w3[:, m, i, :], ident[:])
            last.then_inc(w3T_in_psum, 1)
            global_max(0, 1)
            norm_transposes(5, 0)
            normed(5)
            pe.wait_ge(w2T_ok, 5)
            pe.wait_ge(w3T_ok, 1)
            for b in range(B):
                for i in range(IT):
                    n, r = IT * b + i, rows2[i]
                    if n >= 3:
                        pe.wait_ge(gu_taken, n - 2)
                    for m in range(2):
                        last = nc.tensor.matmul(bank[0:r, 2 * (n % 3) + m, :], w2T[:, m, i * P:i * P + r], xqT[:, b, :],
                                                start=True, stop=True)
                    last.then_inc(gu_in_psum, 1)
            global_max(1, 1)
            for b in range(B):
                pe.wait_ge(hq_ok, IT * (b + 1))
                for t in range(TPB):
                    for i in range(IT):
                        r = rows2[i]
                        last = nc.tensor.matmul(bank[:, 6 + b, t * P:(t + 1) * P], hq[0:r, i, b, t * P:(t + 1) * P],
                                                w2T[0:r, 2, i * P:(i + 1) * P], start=(i == 0), stop=(i == IT - 1))
                last.then_inc(res_in_psum, 1)
            attention16(1, 6)
            global_max(2, 1)
            norm_transposes(7, 1)
            normed(7)
            pe.wait_ge(o16T_ok, 2 * B)
            for b in range(B):
                for i in range(IT):
                    n = IT * b + i
                    if n >= 3:
                        pe.wait_ge(ug_copied, 2 * (n - 2))
                    for m in range(2):
                        nc.tensor.matmul(bank[:, 2 * (n % 3) + m, :], w3T[:, m, i * P:(i + 1) * P], xnT[:, b, :],
                                         start=True, stop=True).then_inc(ug_in_psum, 1)
            for j, count in ((3, 2), (4, 1), (5, 1)):
                global_max(j, count)
            for b in range(B):
                pe.wait_ge(o3_ok, b + 1)
                for t in range(TPB):
                    for i in range(IT):
                        last = nc.tensor.matmul(bank[:, 6 + b, t * P:(t + 1) * P], t3[:, i, b, t * P:(t + 1) * P],
                                                w3T[:, 2, i * P:(i + 1) * P], start=(i == 0), stop=(i == IT - 1))
                last.then_inc(res_in_psum, 1)

        @block.scalar
        def _(act):
            xs = a["x"].rearrange("b (t p) d -> b p t d", p=P)
            act.dma_start(ctx_tok[:], a["ctx_1024"].rearrange("b k d -> k b d")).then_inc(in_ctx, 16)
            for b in range(B):
                act.dma_start(x[:, TPB * b:TPB * (b + 1), :], xs[b]).then_inc(in_x[b], 16)
            for n in VROWS:
                r, k = vrow[n]
                act.dma_start(vec_rows[r:r + k, :], vsrc[n].rearrange("(r d) -> r d", d=D)).then_inc(in_vec, 16)
            for dst, name in ((gamma_ctx, "L0_xattn_gamma_media"), (beta_ctx, "L0_xattn_beta_media"),
                              (gamma_lat, "L0_xattn_gamma_lat"), (beta_lat, "L0_xattn_beta_lat"), (bo0, "L0_xattn_bo")):
                act.dma_start(dst[:], a[name].partition_broadcast(dst.shape[0])).then_inc(in_norm, 16)
            for h in range(H0 + 1):
                if h < H0:
                    act.wait_ge(wT_in_psum, h + 1)
                    if h >= 2:
                        act.wait_ge(ab_in_psum, h - 1)
                    nc.scalar.activation(wT0[:, h % 2, :, :], bank[:, h % 2, 0:3 * P].rearrange("p (n m) -> p n m", n=3),
                                         ACT.Copy).then_inc(wT_ok, 1)
                if h == 0:
                    act.wait_ge(vcol_in_psum, 1)
                    nc.scalar.activation(vec_cols[:], bank[:, 6, 0:nrow], ACT.Copy).then_inc(vcol_ok, 1)
                    nc.scalar.activation(bq0_scaled[:], bank[:, 6, 0:H0], ACT.Copy, scale=SC0).then_inc(vcol_ok, 1)
                    for n in range(2):
                        row = vrow[f"L{n + 2}_xattn_bq"][0]
                        nc.scalar.activation(bq16[:, n:n + 1], bank[:, 6, row:row + 1], ACT.Copy, scale=SC16).then_inc(vcol_ok, 1)
                if h:
                    act.wait_ge(ab_in_psum, h)
                    nc.scalar.activation(ab0[:, h - 1, :], bank[:, 2 + (h - 1) % 2, 0:2 * P + 1], ACT.Copy).then_inc(ab_ok, 1)
                if h == H0 // 2:
                    act.wait_ge(cT_in_psum, 1)
                    cT = bank[:, 6, :].rearrange("p (n b k) -> p n b k", n=2, b=B)
                    nc.scalar.activation(kvT[HI][:, :, S:NK], cT[:, 0, :, 0:NC], ACT.Copy).then_inc(cT_ok, 1)
                    nc.scalar.activation(ctxT[:], cT[:, 1, :, 0:NC], ACT.Copy).then_inc(cT_ok, 1)
                    for b in range(B):
                        act.wait_ge(xT_in_psum, TPB * (b + 1))
                        nc.scalar.activation(kvT[HI][:, b, 0:S], bank[:, 4 + b, :], ACT.Copy).then_inc(kvT_hi_ok[b], 1)

            def query(h, b):
                u = B * h + b
                act.wait_ge(q_in_psum, u + 1)
                wait_from(act, scores_ok, TPB * (u - 1))
                wait_from(act, q_ok, u)
                nc.scalar.activation(q_full, bank[:, 7, :], ACT.Identity,
                                     bias=ab0[:, bass.ds(h, 1), 2 * P:2 * P + 1].rearrange("p n m -> p (n m)"),
                                     scale=SC0).then_inc(q_full_ok, 1)
                act.wait_ge(q_full_ok, u + 1)
                nc.scalar.activation(qT[HI][:, b, :], q_full, ACT.Copy).then_inc(q_hi_ok, 1)

            def exponent(u, b, i):
                first = 2 * (i % 2)
                act.wait_ge(max_ok, TPB * u + i + 1)
                wait_from(act, pT_in_psum, NCH * (u - 1))
                wait_from(act, inv_ok, u - 1)
                nc.scalar.activation(prob[b][:, i, :], bank[:, first:first + 2, :].rearrange("p b n -> p (b n)")[:, 0:NK],
                                     ACT.Exp, bias=neg_max[:, b, i:i + 1], accum_out=row_sum[:, b, i:i + 1])\
                    .then_inc(prob_ok, 1)

            def evacuate(u, b, c):
                n = chunk_keys(c)
                act.wait_ge(pT_in_psum, NCH * u + c + 1)
                slot_free(act, u, c)
                nc.scalar.activation(probT[HI][0:n, SLOT[c], :], bank[0:n, PT_BANK[b][c], :], ACT.Copy)\
                    .then_inc(pT_hi_ok, 1)

            def copy_u(u):
                act.wait_ge(pv_done, NCH * (u + 1))
                wait_from(act, o_in_psum, u)
                nc.scalar.activation(uT, bank[:, 6, :], ACT.Copy).then_inc(u_ok, 1)

            def step(h, b, c, first, last):
                u = B * h + b
                if c == 1 and not first:
                    copy_u(u - 2)
                if c == 2 and not (last and b):
                    query(h + b, 1 - b)
                if not first or b:
                    evacuate(u - 1, 1 - b, c)
                if c < TPB:
                    exponent(u, b, c)

            act.wait_ge(ab_ok, H0)
            query(0, 0)
            run_heads(act, step)
            for c in range(NCH):
                if c == 1:
                    copy_u(U0 - 2)
                evacuate(U0 - 1, B - 1, c)
            copy_u(U0 - 1)

            def norm_copy(k):
                act.wait_ge(xT_in_psum, NT * k + TPB)
                nc.scalar.activation(xnT[:, 0, :], bank[:, 4, :], ACT.Copy).then_inc(xnT_b_ok[0], 1)

            act.wait_ge(l1_in_psum, 1)
            nc.scalar.activation(l1T[:], bank[:, 0, 0:2 * P].rearrange("p (n m) -> p n m", n=2), ACT.Copy)\
                .then_inc(l1_ok, 1)
            nc.scalar.activation(k1T[:], bank[:, 1, 0:B * NC].rearrange("p (b k) -> p b k", b=B), ACT.Copy)\
                .then_inc(l1_ok, 1)
            nc.scalar.activation(v1[:], bank[0:NC, 2, 0:B * D].rearrange("p (b d) -> p b d", b=B), ACT.Copy)\
                .then_inc(l1_ok, 1)
            act.wait_ge(l1_in_psum, 2)
            nc.scalar.activation(kq1[:], bank[:, 3, 0:B * NC].rearrange("p (b k) -> p b k", b=B), ACT.Copy)\
                .then_inc(l1_ok, 1)
            nc.scalar.activation(wa1T[:], bank[:, 3, 256:256 + P], ACT.Copy).then_inc(l1_ok, 1)
            act.wait_ge(l1_in_psum, 3)
            nc.scalar.activation(waa1[:], bank[:, 0, 0:D], ACT.Copy).then_inc(l1_ok, 1)

            norm_copy(1)
            for b in range(B):
                act.wait_ge(xnT_b_ok[b], 1)
                nc.scalar.activation(qT[HI][:, b, :], xnT[:, b, :], ACT.Copy).then_inc(xn_hi_ok, 1)

            def relu(e):
                for j in range(FT):
                    for b in range(B):
                        act.wait_ge(h_in_psum, FT * B * e + j * B + b + 1)
                        if e >= 2:
                            act.wait_ge(y_in_psum, B * (e - 1))
                        row = vrow["L0_ffn_b1"][0] + FT * e + j
                        nc.scalar.activation(hT[:, e % 2, j, b, :], bank[:, j * B + b, :], ACT.Relu,
                                             bias=vec_cols[:, row:row + 1]).then_inc(h_ok, 1)

            relu(0)
            act.wait_ge(diff_ok, 1)
            nc.scalar.activation(top_exp[:], top_diff[:], ACT.Exp).then_inc(top_exp_ok, 1)
            act.wait_ge(gT_in_psum, 1)
            nc.scalar.activation(gateT[:].rearrange("e t p -> e (t p)"),
                                 bank[0:E, 4:6, :].rearrange("e b n -> e (b n)"), ACT.Copy).then_inc(gT_ok, 1)
            for e in range(1, E):
                relu(e)
            def keys_values(n):
                act.wait_ge(kv16_in_psum, n + 1)
                row = vrow[f"L{n + 2}_xattn_bk"][0]
                nc.scalar.activation(k16T[:, n], bank[:, 0, 0:B * NC].rearrange("p (b k) -> p b k", b=B), ACT.Identity,
                                     bias=vec_cols[:, row:row + 1]).then_inc(kv16_ok, 1)
                nc.scalar.activation(v_pair[:, n], bank[:, 1, 0:B * D].rearrange("p (b d) -> p b d", b=B), ACT.Copy)\
                    .then_inc(kv16_ok, 1)
                nc.scalar.activation(v_left[:, n], bank[0:LP, 1, B * D:2 * B * D].rearrange("p (b d) -> p b d", b=B),
                                     ACT.Copy).then_inc(kv16_ok, 1)

            def attention16(n, k):
                norm_copy(k)
                for b in range(B):
                    act.wait_ge(q16_in_psum, B * n + b + 1)
                    nc.scalar.activation(q16T[:, b, :], bank[:, 6 + b, :], ACT.Identity, bias=bq16[:, n:n + 1],
                                         scale=SC16).then_inc(q16_ok, 1)
                for t in range(NT + 1):
                    if t < NT:
                        m = NT * n + t
                        act.wait_ge(s16_ok, m + 1)
                        if t >= 2:
                            act.wait_ge(p16T_in_psum, 2 * (m - 1))
                        pair, left = p16[:, t % 2, 0:HM * PK], p16[:, t % 2, HM * PK:HM * NC]
                        nc.scalar.activation(pair.rearrange("p (h k) -> p h k", h=HM), s16[:, t % 2, :, 0:PK], ACT.Exp)\
                            .then_inc(p16_ok, 1)
                        nc.scalar.activation(left.rearrange("p (h k) -> p h k", h=HM), s16[:, t % 2, :, PK:NC], ACT.Exp)\
                            .then_inc(p16_ok, 1)
                    if t:
                        m = NT * n + t - 1
                        act.wait_ge(p16T_in_psum, 2 * m + 1)
                        if m:
                            act.wait_ge(o16_in_psum, m)
                        nc.scalar.activation(p16T[:, 0:NPAIR, :],
                                             bank[:, 4:6, :].rearrange("p b (c q) -> p (b c) q", c=4), ACT.Copy)\
                            .then_inc(p16T_ok, 1)
                        act.wait_ge(p16T_in_psum, 2 * m + 2)
                        nc.scalar.activation(p16T[0:LP, NPAIR:NPAIR + 2, :],
                                             bank[0:LP, 6, 0:2 * P].rearrange("p (c q) -> p c q", c=2), ACT.Copy)\
                            .then_inc(p16T_ok, 1)
                row = vrow[f"L{n + 2}_xattn_bv"][0]
                for b in range(B):
                    act.wait_ge(o16T_in_psum, B * n + b + 1)
                    nc.scalar.activation(q16T[:, b, :], bank[:, b, :], ACT.Identity, bias=vec_cols[:, row:row + 1])\
                        .then_inc(o16T_ok, 1)

            keys_values(0)
            norm_copy(2)
            for b in range(B):
                act.wait_ge(s1_ok, b + 1)
                part = s1[:, TPB * b:TPB * (b + 1), :]
                nc.scalar.activation(part, part, ACT.Exp, scale=SC1).then_inc(p1_ok, 1)
            for b in range(B):
                act.wait_ge(p1T_in_psum, b + 1)
                nc.scalar.activation(p1T[:, TPB * b:TPB * (b + 1), :],
                                     bank[0:NC, 2 + b, :].rearrange("p (i q) -> p i q", i=TPB), ACT.Copy)\
                    .then_inc(p1T_ok, 1)
            keys_values(1)
            norm_copy(3)
            for b in range(B):
                act.wait_ge(tanh_in_ok, b + 1)
                part = tanh_in[:, TPB * b:TPB * (b + 1), :]
                nc.scalar.activation(part, part, ACT.Tanh).then_inc(tanh_ok, 1)
            act.wait_ge(w2T_in_psum, 1)
            act.wait_ge(rne_made, 2)
            for m in range(2):
                nc.scalar.activation(w2T[:, m, 0:I2], bank[:, m, 0:I2], ACT.Copy).then_inc(w2T_ok, 1)
            nc.scalar.activation(w2T[:, 2, 0:2 * P], bank[:, 2, 0:2 * P], ACT.Copy).then_inc(w2T_ok, 1)
            nc.scalar.activation(w2T[0:rows2[2], 2, 2 * P:3 * P], bank[0:rows2[2], 2, 2 * P:3 * P], ACT.Copy)\
                .then_inc(w2T_ok, 1)
            nc.scalar.activation(down_row[:], bank[:, 3, 0:P], ACT.Copy).then_inc(w2T_ok, 1)
            act.wait_ge(in_f2, 16 * 7)
            nc.scalar.activation(clip_sig[:], clip[:], ACT.Tanh, scale=0.5).then_inc(clip_tanh_ok, 1)
            attention16(0, 4)
            act.wait_ge(w3T_in_psum, 1)
            nc.scalar.activation(w3T, bank[:, 0:3, 0:IT * P], ACT.Copy).then_inc(w3T_ok, 1)
            act.wait_ge(xT_in_psum, NT * 5 + TPB)
            nc.scalar.activation(xqT[:, 0, :], bank[:, 4, :], ACT.Identity, bias=minus_rne[:]).then_inc(xnT_b_ok[0], 1)
            act.wait_ge(c_ok, 1)
            for b in range(B):
                for i in range(IT):
                    n, r = IT * b + i, rows2[i]
                    act.wait_ge(gu_in_psum, n + 1)
                    if n >= 2:
                        act.wait_ge(gu_taken, n - 1)
                    nc.scalar.activation(tanh_out[0:r, n % 2, :], bank[0:r, 2 * (n % 3), :], ACT.Tanh,
                                         scale=c_gate[0:r, i:i + 1]).then_inc(gu_tanh_ok, 1)
            act.wait_ge(hscale_ok, 1)
            for b in range(B):
                for i in range(IT):
                    h = val[0:rows2[i], i, b, :]
                    nc.scalar.activation(h, h, ACT.Identity, bias=plus_rne[0:rows2[i], :],
                                         scale=h_inv[0:rows2[i], :]).then_inc(h_rounded, 1)
            attention16(1, 6)
            norm_copy(7)
            for b in range(B):
                for i in range(IT):
                    n = IT * b + i
                    for m, to in enumerate((val2, val)):
                        act.wait_ge(ug_in_psum, 2 * n + m + 1)
                        nc.scalar.activation(to[:, i, b, :], bank[:, 2 * (n % 3) + m, :], ACT.Copy)\
                            .then_inc(ug_copied, 1)
            for b in range(B):
                act.wait_ge(gate_int_ok, b + 1)
                nc.scalar.activation(t3[:, :, b, :], val2[:, :, b, :], ACT.Tanh, scale=half_sg[:]).then_inc(tanh3_ok, 1)

        @block.vector
        def _(dve):
            own = Steps(dve, dve_step)
            dve.wait_ge(in_ctx, 16)
            for b in range(B):
                own.add(nc.vector.bn_stats(ctx_stats[:, b, :], ctx_tok[:, b, :]))
            own.settle()
            for b in range(B):
                own.add(nc.vector.bn_aggr(ctx_meanvar[:, b, :], ctx_stats[:, b, :]))
            own.settle()
            nc.vector.tensor_scalar(ctx_var_eps[:], ctx_meanvar[:, :, 1], EPS, None, ALU.add).then_inc(ctx_var_ok, 1)

            def layer_stats(b):
                tiles = range(TPB * b, TPB * (b + 1))
                for t in tiles:
                    own.add(nc.vector.bn_stats(stats[:, t, :], x[:, t, :]))
                own.settle()
                for t in tiles:
                    own.add(nc.vector.bn_aggr(meanvar[:, t, :], stats[:, t, :]))
                own.settle()
                c = slice(TPB * b, TPB * (b + 1))
                nc.vector.tensor_scalar(var_eps[:, c], meanvar[:, c, 1], EPS, None, ALU.add).then_inc(var_ok, 1)

            for b in range(B):
                dve.wait_ge(in_x[b], 16)
                layer_stats(b)
            dve.wait_ge(ctx_rstd_ok, 1)
            for b in range(B):
                own.add(nc.vector.tensor_scalar(ctx_norm[:, b, :], ctx_tok[:, b, :], ctx_meanvar[:, b, 0:1],
                                                ctx_rstd[:, b:b + 1], ALU.subtract, ALU.mult))
            own.settle()
            dve.wait_ge(in_norm, 16 * 5)
            own.add(nc.vector.tensor_tensor(ctx_norm[:], ctx_norm[:], gamma_ctx[:].unsqueeze(1).to_broadcast([NC, B, D]),
                                            ALU.mult))
            own.settle()
            nc.vector.tensor_tensor(ctx_norm[:], ctx_norm[:], beta_ctx[:].unsqueeze(1).to_broadcast([NC, B, D]),
                                    ALU.add).then_inc(ctx_norm_ok, 1)
            for b in range(B):
                dve.wait_ge(rstd_ok, b + 1)
                for t in range(TPB * b, TPB * (b + 1)):
                    own.add(nc.vector.tensor_scalar(xn[:, t, :], x[:, t, :], meanvar[:, t, 0:1], rstd[:, t:t + 1],
                                                    ALU.subtract, ALU.mult))
                own.settle()
                part = xn[:, TPB * b:TPB * (b + 1), :]
                own.add(nc.vector.tensor_tensor(part, part, gamma_lat[:].unsqueeze(1).to_broadcast([P, TPB, D]), ALU.mult))
                own.settle()
                for t in range(TPB * b, TPB * (b + 1)):
                    nc.vector.tensor_tensor(xn[:, t, :], xn[:, t, :], beta_lat[:], ALU.add).then_inc(xn_ok, 1)
            dve.wait_ge(cT_ok, 2)
            nc.vector.tensor_tensor(kvT[LO][:, :, S:NK], bank[:, 6, :].rearrange("p (n b k) -> p n b k", n=2, b=B)[:, 0, :, 0:NC],
                                    kvT[HI][:, :, S:NK].bitcast(F32), ALU.subtract).then_inc(cT_lo_ok, 1)
            for b in range(B):
                dve.wait_ge(kvT_hi_ok[b], 1)
                nc.vector.tensor_tensor(kvT[LO][:, b, 0:S], bank[:, 4 + b, :], kvT[HI][:, b, 0:S].bitcast(F32),
                                        ALU.subtract).then_inc(kvT_lo_ok[b], 1)
            dve.wait_ge(xn_ok, NT)
            for b in range(B):
                c = slice(TPB * b, TPB * (b + 1))
                nc.vector.tensor_copy(kv_lat[HI][:, c, :], xn[:, c, :]).then_inc(kv_lat_ok, 1)
                dve.wait_ge(kv_lat_ok, 2 * b + 1)
                nc.vector.tensor_tensor(kv_lat[LO][:, c, :], xn[:, c, :], kv_lat[HI][:, c, :].bitcast(F32), ALU.subtract)\
                    .then_inc(kv_lat_ok, 1)
            dve.wait_ge(ctx_norm_ok, 1)
            nc.vector.tensor_copy(kv_ctx[HI][:], ctx_norm[:]).then_inc(kv_lat_ok, 1)
            dve.wait_ge(kv_lat_ok, 2 * B + 1)
            nc.vector.tensor_tensor(kv_ctx[LO][:], ctx_norm[:], kv_ctx[HI][:].bitcast(F32), ALU.subtract)\
                .then_inc(kv_lat_ok, 1)
            dve.wait_ge(bv_used, H0)
            nc.vector.tensor_tensor(out_bias0[:], bank[:, 7, 0:D], bo0[:], ALU.add).then_inc(bias0_ok, 1)

            def maximum(u, b, i):
                first = 2 * (i % 2)
                dve.wait_ge(scores_ok, TPB * u + i + 1)
                wait_from(dve, prob_ok, TPB * (u - 1))
                nc.vector.tensor_reduce(neg_max[:, b, i:i + 1], bank[:, first:first + 2, :].rearrange("p b n -> p (b n)")[:, 0:NK],
                                        AX.X, ALU.max, negate=True).then_inc(max_ok, 1)

            def evacuate(u, b, c):
                n = chunk_keys(c)
                dve.wait_ge(pT_hi_ok, NCH * u + c + 1)
                nc.vector.tensor_tensor(probT[LO][0:n, SLOT[c], :], bank[0:n, PT_BANK[b][c], :],
                                        probT[HI][0:n, SLOT[c], :].bitcast(F32), ALU.subtract).then_inc(pT_lo_ok, 1)

            def query(u, b):
                dve.wait_ge(q_hi_ok, u + 1)
                nc.vector.tensor_tensor(qT[LO][:, b, :], q_full, qT[HI][:, b, :].bitcast(F32), ALU.subtract)\
                    .then_inc(q_ok, 1)

            def add_output(u, b):
                dve.wait_ge(o_in_psum, u + 1)
                dve.wait_ge(inv_ok, u + 1)
                if u is 0:
                    dve.wait_ge(x_biased, 1)
                wait_from(dve, o_added, u - 1)
                for i in range(TPB):
                    t = TPB * b + i
                    last = nc.vector.scalar_tensor_tensor(out=x[:, t, :], in0=bank[:, 7, i * P:(i + 1) * P],
                                                          scalar=row_inv[:, b, i:i + 1], in1=x[:, t, :],
                                                          op0=ALU.mult, op1=ALU.add)
                last.then_inc(o_added, 1)

            def invert(u, b):
                dve.wait_ge(prob_ok, TPB * (u + 1))
                wait_from(dve, o_added, u - 1)
                nc.vector.reciprocal(row_inv[:, b, :], row_sum[:, b, :]).then_inc(inv_ok, 1)

            def weight_scales2():
                own.add(nc.vector.memset(wmax2[:], 1.0))
                dve.wait_ge(in_f2, 16 * 7)
                own.settle()
                for m in range(2):
                    own.add(nc.vector.tensor_reduce(wmax2[:, IT * m:IT * m + 2],
                                                    wn2[:, m, 0:2 * P].rearrange("p (i d) -> p i d", i=2), AX.X, ALU.max,
                                                    apply_absolute_value=True))
                    own.add(nc.vector.tensor_reduce(wmax2[0:rows2[2], IT * m + 2:IT * m + 3], wn2[0:rows2[2], m, 2 * P:3 * P],
                                                    AX.X, ALU.max, apply_absolute_value=True))
                own.add(nc.vector.tensor_reduce(wmax2[:, 6:7], wn2[:, 2, 0:I2], AX.X, ALU.max, apply_absolute_value=True))
                own.settle()
                own.add(nc.vector.tensor_scalar(wscale2[:], wmax2[:], 1.0 / 127, None, ALU.mult))
                own.settle()
                nc.vector.reciprocal(winv2[:], wscale2[:]).then_inc(wmax_ok, 1)

            def weight_scales3():
                dve.wait_ge(in_f3, 16 * 3)
                own.add(nc.vector.tensor_reduce(wmax3[:], wn3[:], AX.X, ALU.max, apply_absolute_value=True))
                own.settle()
                own.add(nc.vector.tensor_scalar(wscale3[:], wmax3[:], 1.0 / 7, 1e-12, ALU.mult, ALU.max))
                own.settle()
                nc.vector.reciprocal(winv3[:], wscale3[:]).then_inc(wmax_ok, 1)

            def step(h, b, c, first, last):
                u = B * h + b
                if c < TPB:
                    maximum(u, b, c)
                if c == 2 and not (last and b):
                    query(u + 1, 1 - b)
                if not first or b:
                    if c == 0:
                        invert(u - 1, 1 - b)
                    evacuate(u - 1, 1 - b, c)
                if c == TPB and not first:
                    add_output(u - 2, b)
                if c == 4 and first and b:
                    weight_scales2()
                    weight_scales3()

            query(0, 0)
            run_heads(dve, step)
            invert(U0 - 1, B - 1)
            for c in range(NCH):
                evacuate(U0 - 1, B - 1, c)
            add_output(U0 - 2, 0)

            def layer_norm(k, result=None):
                for b in range(B):
                    result(b)
                    layer_stats(b)
                for t in range(NT):
                    if t % TPB == 0:
                        dve.wait_ge(rstd_ok, B * k + t // TPB + 1)
                    nc.vector.tensor_scalar(xn[:, t, :], x[:, t, :], meanvar[:, t, 0:1], rstd[:, t:t + 1],
                                            ALU.subtract, ALU.mult).then_inc(xn_ok, 1)

            def norm_copy(k):
                dve.wait_ge(xT_in_psum, NT * (k + 1))
                nc.vector.tensor_copy(xnT[:, 1, :], bank[:, 5, :]).then_inc(xnT_b_ok[1], 1)

            def moe_norm_copy():
                norm_copy(1)
                for b in range(B):
                    dve.wait_ge(xn_hi_ok, b + 1)
                    nc.vector.tensor_tensor(qT[LO][:, b, :], xnT[:, b, :], qT[HI][:, b, :].bitcast(F32), ALU.subtract)\
                        .then_inc(xn_lo_ok, 1)

            def per_tile(v, n=E):
                return v.unsqueeze(2).to_broadcast([P, NT, n])

            def batch(tile, b):
                return tile[:, TPB * b:TPB * (b + 1), :]

            def add_result(k, b):
                dve.wait_ge(res_in_psum, B * k + b + 1)
                nc.vector.tensor_tensor(batch(x, b), bank[:, 6 + b, :].rearrange("p (i d) -> p i d", i=TPB),
                                        batch(x, b), ALU.add).then_inc(x_done, 1)
                dve.wait_ge(x_done, B * k + b + 1)

            def result0(b):
                if b:
                    add_output(U0 - 1, B - 1)
                dve.wait_ge(o_added, U0 - 1 + b)

            layer_norm(1, result0)
            moe_norm_copy()
            dve.wait_ge(logit_in_psum, 1)
            dve.wait_ge(rank_ok, E)
            dve.wait_ge(in_moe, 16 * 5)
            own.add(nc.vector.tensor_tensor(logit[:], bank[:, 6, 0:NT * E].rearrange("p (t e) -> p t e", t=NT),
                                            br[:].unsqueeze(1).to_broadcast([P, NT, E]), ALU.add))
            own.settle()
            for i, src in ((0, logit), (1, logit2)):
                own.add(nc.vector.tensor_reduce(top[i][:], src[:], AX.X, ALU.max))
                own.settle()
                own.add(nc.vector.tensor_tensor(key[:], src[:], per_tile(top[i][:]), ALU.is_equal))
                own.settle()
                own.add(nc.vector.tensor_tensor(key[:], key[:], rank[:], ALU.mult))
                own.settle()
                own.add(nc.vector.tensor_reduce(top_key[:], key[:], AX.X, ALU.max))
                own.settle()
                own.add(nc.vector.tensor_tensor(pick[i][:], key[:], per_tile(top_key[:]), ALU.is_equal))
                own.settle()
                if i == 0:
                    own.add(nc.vector.scalar_tensor_tensor(out=logit2[:], in0=pick[0][:], scalar=-3e38, in1=logit[:],
                                                           op0=ALU.mult, op1=ALU.add))
                    own.settle()
            nc.vector.tensor_tensor(top_diff[:], top[1][:], top[0][:], ALU.subtract).then_inc(diff_ok, 1)
            dve.wait_ge(top_exp_ok, 1)
            own.add(nc.vector.tensor_scalar(top_den[:], top_exp[:], 1.0, None, ALU.add))
            own.settle()
            own.add(nc.vector.reciprocal(top_w[0][:], top_den[:]))
            own.settle()
            own.add(nc.vector.tensor_tensor(top_w[1][:], top_exp[:], top_w[0][:], ALU.mult))
            own.add(nc.vector.tensor_tensor(pick[0][:], pick[0][:], per_tile(top_w[0][:]), ALU.mult))
            own.settle()
            own.add(nc.vector.tensor_tensor(pick[1][:], pick[1][:], per_tile(top_w[1][:]), ALU.mult))
            own.settle()
            nc.vector.tensor_tensor(gate[:], pick[0][:], pick[1][:], ALU.add).then_inc(gate_ok, 1)
            dve.wait_ge(b2_in_psum, 1)
            for b in range(B):
                nc.vector.tensor_tensor(batch(x, b), bank[:, 6 + b, :].rearrange("p (i d) -> p i d", i=TPB),
                                        batch(x, b), ALU.add).then_inc(b2_added, 1)
            dve.wait_ge(gate_ok, 1)
            dve.wait_ge(b2_added, B)
            def add_expert(e, b):
                dve.wait_ge(y_in_psum, B * e + b + 1)
                if e >= 1:
                    dve.wait_ge(y_added, B * (e - 1) + b + 1)
                for i in range(TPB):
                    t = TPB * b + i
                    last = nc.vector.scalar_tensor_tensor(out=x[:, t, :], in0=bank[:, 6 + b, i * P:(i + 1) * P],
                                                          scalar=gate[:, t, e:e + 1], in1=x[:, t, :],
                                                          op0=ALU.mult, op1=ALU.add)
                last.then_inc(y_added, 1)

            for e in range(E - 1):
                for b in range(B):
                    add_expert(e, b)

            def result1(b):
                add_expert(E - 1, b)
                dve.wait_ge(y_added, B * (E - 1) + b + 1)

            layer_norm(2, result1)
            norm_copy(2)
            for b in range(B):
                dve.wait_ge(s1_in_psum, b + 1)
                src = bank[:, b, 0:TPB * NC].rearrange("p (i k) -> p i k", i=TPB)
                own.add(nc.vector.tensor_reduce(neg_max1[:, TPB * b:TPB * (b + 1)], src, AX.X, ALU.max, negate=True))
                own.settle()
                nc.vector.tensor_tensor(batch(s1, b), src,
                                        neg_max1[:, TPB * b:TPB * (b + 1)].unsqueeze(2).to_broadcast([P, TPB, NC]),
                                        ALU.add).then_inc(s1_ok, 1)
            for b in range(B):
                dve.wait_ge(p1_ok, b + 1)
                own.add(nc.vector.tensor_reduce(sum1[:, TPB * b:TPB * (b + 1)], batch(s1, b), AX.X, ALU.add))
            own.settle()
            own.add(nc.vector.reciprocal(inv1[:], sum1[:]))
            own.settle()
            for b in range(B):
                dve.wait_ge(o1_in_psum, b + 1)
                nc.vector.tensor_tensor(turned[:, b, :].rearrange("p (c i) -> p i c", i=TPB),
                                        bank[:, 4 + b, :].rearrange("p (i c) -> p i c", i=TPB),
                                        inv1[:, TPB * b:TPB * (b + 1)].unsqueeze(2).to_broadcast([P, TPB, D]),
                                        ALU.mult).then_inc(turned_ok, 1)
            dve.wait_ge(x_biased, 2)
            layer_norm(3, lambda b: add_result(0, b))
            norm_copy(3)
            dve.wait_ge(in_l1, 16 * 9)
            for b in range(B):
                dve.wait_ge(res_in_psum, B + b + 1)
                nc.vector.tensor_tensor(batch(tanh_in, b), bank[:, 6 + b, :].rearrange("p (i d) -> p i d", i=TPB),
                                        fbias1[:].unsqueeze(1).to_broadcast([P, TPB, D]), ALU.add)\
                    .then_inc(tanh_in_ok, 1)

            def result3(b):
                dve.wait_ge(tanh_ok, b + 1)
                nc.vector.tensor_tensor(batch(x, b), batch(tanh_in, b), batch(x, b), ALU.add).then_inc(x_done, 1)
                dve.wait_ge(x_done, B + b + 1)


            def attention16(n, k, result):
                layer_norm(k, result)
                norm_copy(k)
                if n == 0:
                    dve.wait_ge(mask_neg_ok, NT)
                LAG = 3
                for t in range(NT + LAG):
                    m, z = NT * n + t, t % 2
                    if t < NT:
                        scores, to = bank[:, 0:4, 0:BK * NC], s16[:, z].rearrange("p (g h) k -> p g (h k)", g=4)
                        dve.wait_ge(s16_in_psum, m + 1)
                        if m >= 2:
                            dve.wait_ge(p16_ok, 2 * (m - 1))
                        if n == 0:
                            nc.vector.tensor_tensor(to, scores, mask_neg[:, t, :].rearrange("p (g n) -> p g n", g=4),
                                                    ALU.add).then_inc(s16_taken, 1)
                        else:
                            nc.vector.tensor_copy(to, scores).then_inc(s16_taken, 1)
                    if t >= LAG:
                        d, y = NT * n + t - LAG, (t - LAG) % 2
                        o = bank[:, 7, 0:HM * (DH + 1)].rearrange("p (h d) -> p h d", h=HM)
                        dve.wait_ge(o16_in_psum, d + 1)
                        if d >= 2:
                            dve.wait_ge(o16_ok, d - 1)
                        own.add(nc.vector.reciprocal(inv16[:, y, :], o[:, :, DH]))
                        own.settle()
                        if n == 0:
                            dve.wait_ge(spoil16_ok, d + 1)
                            own.add(nc.vector.tensor_tensor(inv16[:, y, :], inv16[:, y, :], spoil16[:, d % 4, :], ALU.add))
                            own.settle()
                        nc.vector.tensor_tensor(o16[:, t - LAG, :].rearrange("p (h d) -> p h d", h=HM), o[:, :, 0:DH],
                                                inv16[:, y, :].unsqueeze(2).to_broadcast([P, HM, DH]), ALU.mult)\
                            .then_inc(o16_ok, 1)
                    if t < NT:
                        dve.wait_ge(s16_taken, m + 1)
                        if m >= 2 and n == 0:
                            dve.wait_ge(spoil16_ok, m - 1)
                        nc.vector.tensor_reduce(neg_max16[:, z, :], s16[:, z], AX.X, ALU.max, negate=True)\
                            .then_inc(max16_ok, 1)
                dve.wait_ge(x_biased, 3 + n)

            def global_max(j, count):
                dve.wait_ge(pmaxT_in_psum, j + 1)
                nc.vector.tensor_reduce(gmax_row[:, 0:count], bank[0:1, 7, 0:count * P].rearrange("p (c q) -> p c q", c=count),
                                        AX.X, ALU.max).then_inc(gmax_ok, 1)
                dve.wait_ge(gmax_in_psum, j + 1)
                return bank[:, 7, 2 * P:2 * P + count]

            def row_max(to, src, axis=AX.X):
                return nc.vector.tensor_reduce(to, src, axis, ALU.max, apply_absolute_value=True)

            def scalars(to, src, s1, s2, op0, op1):
                own.add(nc.vector.tensor_scalar(to, src, s1, s2, op0, op1))
                own.settle()

            attention16(0, 4, result3)
            dve.wait_ge(clip_tanh_ok, 1)
            scalars(clip_sig[:], clip_sig[:], 0.5, 0.5, ALU.mult, ALU.add)
            layer_norm(5, lambda b: add_result(2, b))
            dve.wait_ge(xn_ok, NT * 6)
            row_max(pmax[:, 0:1], xn[:], AX.XY).then_inc(pmax_ok, 1)
            m = global_max(0, 1)
            scalars(x_scale[:], m, clip_sig[:, 0:1], 1.0 / 127, ALU.mult, ALU.mult)
            own.add(nc.vector.reciprocal(x_inv[:], x_scale[:]))
            own.settle()
            for b in range(B):
                scalars(batch(xn, b), batch(xn, b), x_inv[:], RNE, ALU.mult, ALU.add)
                nc.vector.tensor_scalar(batch(xn, b), batch(xn, b), RNE + 127, RNE - 128, ALU.min, ALU.max)\
                    .then_inc(xq_ok, 1)
            scalars(c_gate[:], wscale2[:, 0:IT], x_scale[:], 0.5, ALU.mult, ALU.mult)
            scalars(c_both[:], wscale2[:, IT:2 * IT], x_scale[:], None, ALU.mult, ALU.bypass)
            nc.vector.tensor_tensor(c_both[:], c_both[:], c_gate[:], ALU.mult).then_inc(c_ok, 1)
            own.add(nc.vector.memset(unit_max[:], 0.0))
            dve.wait_ge(c_ok, 1)
            own.settle()
            dve.wait_ge(xT_in_psum, NT * 6)
            nc.vector.tensor_scalar(xqT[:, 1, :], bank[:, 5, :], -RNE, None, ALU.add).then_inc(xnT_b_ok[1], 1)
            for b in range(B):
                for i in range(IT):
                    n, r = IT * b + i, rows2[i]
                    dve.wait_ge(gu_tanh_ok, n + 1)
                    own.add(nc.vector.scalar_tensor_tensor(out=silu_in[0:r, :], in0=tanh_out[0:r, n % 2, :], scalar=1.0,
                                                           in1=bank[0:r, 2 * (n % 3), :], op0=ALU.add, op1=ALU.mult))
                    own.settle()
                    nc.vector.scalar_tensor_tensor(out=val[0:r, i, b, :], in0=silu_in[0:r, :],
                                                   scalar=c_both[0:r, i:i + 1], in1=bank[0:r, 2 * (n % 3) + 1, :],
                                                   op0=ALU.mult, op1=ALU.mult).then_inc(gu_taken, 1)
                    dve.wait_ge(gu_taken, n + 1)
                    own.add(row_max(unit_max[0:r, 0, n:n + 1], val[0:r, i, b, :]))
            own.settle()
            row_max(pmax[:, 0:1], unit_max[:, 0, :]).then_inc(pmax_ok, 1)
            m = global_max(1, 1)
            scalars(h_scale[:], m, clip_sig[:, 1:2], 1.0 / 127, ALU.mult, ALU.mult)
            nc.vector.reciprocal(h_inv[:], h_scale[:]).then_inc(hscale_ok, 1)
            dve.wait_ge(w2T_ok, 5)
            own.add(nc.vector.tensor_scalar(down_scale[:], down_row[:], h_scale[:], None, ALU.mult))
            for b in range(B):
                for i in range(IT):
                    n, r = IT * b + i, rows2[i]
                    dve.wait_ge(h_rounded, n + 1)
                    h = val[0:r, i, b, :]
                    scalars(h, h, RNE + 127, RNE - 128, ALU.min, ALU.max)
                    nc.vector.tensor_scalar(hq[0:r, i, b, :], h, -RNE, None, ALU.add).then_inc(hq_ok, 1)

            def result5(b):
                dve.wait_ge(res_in_psum, B * 3 + b + 1)
                own.add(nc.vector.tensor_tensor(batch(tanh_in, b), bank[:, 6 + b, :].rearrange("p (i d) -> p i d", i=TPB),
                                                down_scale[:].unsqueeze(1).to_broadcast([P, TPB, D]), ALU.mult))
                own.settle()
                nc.vector.tensor_tensor(batch(x, b), batch(tanh_in, b), batch(x, b), ALU.add).then_inc(x_done, 1)
                dve.wait_ge(x_done, B * 3 + b + 1)

            attention16(1, 6, result5)
            Q16 = 32767.0
            layer_norm(7, lambda b: add_result(4, b))
            dve.wait_ge(xn_ok, NT * 8)
            row_max(pmax[:, 0:1], xn[:], AX.XY).then_inc(pmax_ok, 1)
            m = global_max(2, 1)
            scalars(x_scale[:], m, 1 / Q16, 1e-12, ALU.mult, ALU.max)
            own.add(nc.vector.reciprocal(x_inv[:], x_scale[:]))
            own.settle()
            for b in range(B):
                scalars(batch(xn, b), batch(xn, b), x_inv[:], RNE, ALU.mult, ALU.add)
                nc.vector.tensor_scalar(batch(xn, b), batch(xn, b), -RNE, x_scale[:], ALU.add, ALU.mult)\
                    .then_inc(xq_ok, 1)
            norm_copy(7)
            for b in range(B):
                for i in range(IT):
                    n = IT * b + i
                    for m in range(2):
                        dve.wait_ge(ug_copied, 2 * n + m + 1)
                        row_max(unit_max[:, m, n:n + 1], (val2, val)[m][:, i, b, :]).then_inc(ug_maxed, 1)
            dve.wait_ge(ug_maxed, 2 * IT * B)
            row_max(pmax[:], unit_max[:]).then_inc(pmax_ok, 1)
            m = global_max(3, 2)
            scalars(ug_scale[:], m, 1 / Q16, 1e-12, ALU.mult, ALU.max)
            sg, su = ug_scale[:, 0:1], ug_scale[:, 1:2]
            own.add(nc.vector.tensor_scalar(half_sg[:], sg, 0.5, None, ALU.mult))
            nc.vector.reciprocal(ug_inv[:], ug_scale[:]).then_inc(ug_scale_ok, 1)
            dve.wait_ge(ug_scale_ok, 1)
            own.settle()
            dve.wait_ge(ug_copied, 2 * IT * B)
            for b in range(B):
                g = val2[:, :, b, :]
                scalars(g, g, ug_inv[:, 0:1], RNE, ALU.mult, ALU.add)
                nc.vector.tensor_scalar(g, g, -RNE, None, ALU.add).then_inc(gate_int_ok, 1)
            for b in range(B):
                g, t = val2[:, :, b, :], t3[:, :, b, :]
                dve.wait_ge(tanh3_ok, b + 1)
                scalars(t, t, 32768.0, RNE + 32768, ALU.mult, ALU.add)
                scalars(t, t, RNE + 65535, -RNE, ALU.min, ALU.add)
                own.add(nc.vector.tensor_tensor(t, g, t, ALU.mult))
                own.settle()
                own.add(row_max(unit_max[:, 0, b:b + 1], t, AX.XY))
            own.settle()
            row_max(pmax[:, 0:1], unit_max[:, 0, 0:B]).then_inc(pmax_ok, 1)
            m = global_max(4, 1)
            scalars(amax3[:, 0:1], m, sg, 2.0 ** -16, ALU.mult, ALU.mult)
            scalars(scale3[:, 0:1], amax3[:, 0:1], 1 / Q16, 1e-12, ALU.mult, ALU.max)
            own.add(nc.vector.reciprocal(inv3[:, 0:1], scale3[:, 0:1]))
            own.settle()
            scalars(ratio3[:, 0:1], inv3[:, 0:1], sg, 2.0 ** -16, ALU.mult, ALU.mult)
            for b in range(B):
                dve.wait_ge(up_int_ok, b + 1)
                t, u = t3[:, :, b, :], val[:, :, b, :]
                scalars(t, t, ratio3[:, 0:1], RNE, ALU.mult, ALU.add)
                own.add(nc.vector.scalar_tensor_tensor(out=t, in0=t, scalar=-RNE, in1=u, op0=ALU.add, op1=ALU.mult))
                own.settle()
                own.add(row_max(unit_max[:, 0, b:b + 1], t, AX.XY))
            own.settle()
            row_max(pmax[:, 0:1], unit_max[:, 0, 0:B]).then_inc(pmax_ok, 1)
            m = global_max(5, 1)
            scalars(amax3[:, 1:2], m, scale3[:, 0:1], su, ALU.mult, ALU.mult)
            scalars(scale3[:, 1:2], amax3[:, 1:2], 1 / Q16, 1e-12, ALU.mult, ALU.max)
            own.add(nc.vector.reciprocal(inv3[:, 1:2], scale3[:, 1:2]))
            own.settle()
            scalars(ratio3[:, 1:2], inv3[:, 1:2], scale3[:, 0:1], su, ALU.mult, ALU.mult)
            for b in range(B):
                t = t3[:, :, b, :]
                scalars(t, t, ratio3[:, 1:2], RNE, ALU.mult, ALU.add)
                nc.vector.tensor_scalar(t, t, -RNE, scale3[:, 1:2], ALU.add, ALU.mult).then_inc(o3_ok, 1)
            for b in range(B):
                add_result(5, b)
            nc.vector.memset(stats[:, 0, 0:1], 0.0).then_inc(x_final, 1)


def kernel(**inputs):
    import numpy as np
    import concourse.bacc as bacc
    from concourse.bass_utils import run_bass_kernel_spmd

    nc = bacc.Bacc("TRN2", target_bir_lowering=False, num_devices=1)
    arrays, handles = {}, {}
    for name, value in inputs.items():
        array = np.ascontiguousarray(value)
        arrays["in_" + name] = array
        handles[name] = nc.dram_tensor("in_" + name, array.shape, mybir.dt.from_np(array.dtype), kind="ExternalInput").ap()
    out = nc.dram_tensor("out_x", inputs["x"].shape, F32, kind="ExternalOutput").ap()
    build(nc, handles, out)
    result = run_bass_kernel_spmd(nc, [arrays], core_ids=[0])
    return result.results[0]["out_x"]
```

```python
from contextlib import ExitStack

import concourse.bass as bass
from concourse import mybir

ALU = mybir.AluOpType
ACT = mybir.ActivationFunctionType
AX = mybir.AxisListType
F32 = mybir.dt.float32
BF16 = mybir.dt.bfloat16
U8 = mybir.dt.uint8
F32R = mybir.dt.float32r

P = 128
B = 2
NT = 8
TPB = NT // B
EPS = 1e-5
RNE = 1.5 * 2.0 ** 23
MASKED = -3e38


class Steps:

    def __init__(self, engine, semaphore):
        self.engine, self.semaphore, self.made = engine, semaphore, 0

    def add(self, instruction):
        instruction.then_inc(self.semaphore, 1)
        self.made += 1

    def settle(self):
        self.engine.wait_ge(self.semaphore, self.made)


def build(nc, a, out):
    S = a["x"].shape[1]
    D = a["x"].shape[2]
    NC = a["ctx_1024"].shape[1]
    H0 = a["L0_xattn_Wq"].shape[1] // D
    NK = S + NC
    NCH = TPB + 1
    U0 = H0 * B
    SC0 = float(D) ** -0.5
    E, _, F1 = a["L0_ffn_W1"].shape
    FT = F1 // P
    SC1 = 16 ** -0.5
    HM = a["mask_Bx16xSxS2_bk1"].shape[1]
    DH = D // HM
    SC16 = float(DH) ** -0.5
    PK = 64
    LK = NC - PK
    NPAIR = HM // 2
    LH = HM // 2
    LP = LH * LK
    BK = HM // 4
    I2 = a["L2_ffn_w_gate"].shape[0]
    I3 = a["L3_ffn_w_gate"].shape[0]
    IT = 3
    rows2 = [P, P, I2 - 2 * P]
    assert LP <= P and I3 == IT * P
    assert D == P and S == TPB * P

    with ExitStack() as ctx:
        def sb(name, shape, dt=F32):
            return ctx.enter_context(nc.sbuf_tensor(name, shape, dt))

        def sem(name):
            return ctx.enter_context(nc.semaphore(name))

        bank = ctx.enter_context(nc.psum_tensor("bank", [P, 8, 512], F32))

        x = sb("x_residual", [P, NT, D])
        ident = sb("ident", [P, P])
        ones = sb("ones", [P, P])
        minus_half = sb("minus_half", [P, 16])
        xn = sb("xn", [P, NT, D])
        xnT = sb("xnT", [P, B, S])
        stats = sb("stats", [P, NT, 6])
        meanvar = sb("meanvar", [P, NT, 2])
        var_eps = sb("var_eps", [P, NT])
        rstd = sb("rstd", [P, NT])
        rstd_again = sb("rstd_again", [P, NT])

        ctx_tok = sb("ctx_tok", [NC, B, D])
        ctxT = sb("ctxT", [P, B, NC])
        ctx_stats = sb("ctx_stats", [NC, B, 6])
        ctx_meanvar = sb("ctx_meanvar", [NC, B, 2])
        ctx_var_eps = sb("ctx_var_eps", [NC, B])
        ctx_rstd = sb("ctx_rstd", [NC, B])
        ctx_norm = sb("ctx_norm", [NC, B, D])
        gamma_ctx = sb("gamma_ctx", [NC, D])
        beta_ctx = sb("beta_ctx", [NC, D])
        gamma_lat = sb("gamma_lat", [P, D])
        beta_lat = sb("beta_lat", [P, D])
        bo0 = sb("bo0", [P, D])
        out_bias0 = sb("out_bias0", [P, D])
        HI, LO = range(2)
        kvT = [sb(f"kvT_{n}", [P, B, NK + NK % 2], F32R) for n in ("hi", "lo")]
        kv_lat = [sb(f"kv_lat_{n}", [P, NT, D], F32R) for n in ("hi", "lo")]
        kv_ctx = [sb(f"kv_ctx_{n}", [NC, B, D], F32R) for n in ("hi", "lo")]

        VROWS = ["L0_xattn_bq", "bv0", "L0_ffn_b1", "L2_xattn_bq", "L2_xattn_bk", "L3_xattn_bq", "L3_xattn_bk",
                 "L2_xattn_bv", "L3_xattn_bv"]
        vsrc = {n: a[n] for n in VROWS if n != "bv0"}
        vsrc["bv0"] = a["L0_xattn_bkv"][H0 * D:]
        vsrc["L0_ffn_b1"] = a["L0_ffn_b1"].rearrange("e f -> (e f)")
        vrow, nrow = {}, 0
        for n in VROWS:
            k = vsrc[n].shape[0] // D
            vrow[n] = (nrow, k)
            nrow += k
        FIRST = 2 * H0
        vec_rows0 = sb("vec_rows0", [FIRST, D])
        vec_rows = sb("vec_rows", [nrow - FIRST, D])
        vec_cols = sb("vec_cols", [P, nrow])
        bq0_scaled = sb("bq0_scaled", [P, H0])
        bv0_wide = sb("bv0_wide", [P, 2, P])

        shared = sb("shared", [P, 4 * H0 * D + B * TPB * NK])
        wq0 = shared[:, 0:H0 * D]
        wkv0 = shared[:, H0 * D:3 * H0 * D]
        wo0 = shared[:, 3 * H0 * D:4 * H0 * D].rearrange("p (h d) -> p h d", h=H0)
        wT0 = sb("wT0", [P, 2, 3, P])
        ab0 = sb("ab0", [P, H0, 2 * P + 1])
        a_now = [sb(f"a_now_{n}", [P, P], F32R) for n in ("hi", "lo")]
        qT = [sb(f"qT_{n}", [P, B, S], F32R) for n in ("hi", "lo")]
        at = 4 * H0 * D
        prob = [shared[:, at + b * TPB * NK:at + (b + 1) * TPB * NK].rearrange("p (i k) -> p i k", i=TPB)
                for b in range(B)]
        SLOT = (0, 1, 2, 0, 1)
        probT = [sb(f"probT_{n}", [P, 3, S], F32R) for n in ("hi", "lo")]
        queries = sb("queries", [P, B, S])
        uT, q_full = queries[:, 0, :], queries[:, 1, :]
        neg_max = sb("neg_max", [P, B, TPB])
        row_sum = sb("row_sum", [P, B, TPB])
        row_inv = sb("row_inv", [P, B, TPB])

        w1 = sb("w1", [P, E, F1])
        w2 = sb("w2", [P, E, FT, D])
        w1_now = [part[:].rearrange("p c s -> p (c s)")[:, 0:2 * F1].rearrange("p (n f) -> p n f", n=2)
                  for part in probT]
        wr = sb("wr", [P, E])
        br = sb("br", [P, E])
        b2 = sb("b2", [E, D])
        rank = sb("rank", [P, NT, E])
        logit = sb("logit", [P, NT, E])
        logit2 = sb("logit2", [P, NT, E])
        key = sb("key", [P, NT, E])
        pick = [sb(f"pick{i}", [P, NT, E]) for i in range(2)]
        top = [sb(f"top{i}", [P, NT]) for i in range(2)]
        top_key = sb("top_key", [P, NT])
        top_diff = sb("top_diff", [P, NT])
        top_exp = sb("top_exp", [P, NT])
        top_den = sb("top_den", [P, NT])
        top_w = [sb(f"top_w{i}", [P, NT]) for i in range(2)]
        gate = sb("gate", [P, NT, E])
        scratch = sb("scratch", [P, 2 * HM * NC])
        gateT = scratch[0:E, 0:NT * P].rearrange("e (t p) -> e t p", t=NT)
        hT = sb("hT", [P, 2, FT, B, S])

        l1w = sb("l1w", [P, 7, D])
        L1Q, L1K, L1V, L1P, L1F, L1A, L1B = range(7)
        bp1 = sb("bp1", [P, D])
        fbias1 = sb("fbias1", [P, D])
        l1T = sb("l1T", [P, 2, P])
        k1T = sb("k1T", [P, B, NC])
        kq1 = sb("kq1", [P, B, NC])
        v1 = sb("v1", [NC, B, D])
        wa1T = sb("wa1T", [P, P])
        waa1 = sb("waa1", [P, D])
        s1 = sb("s1", [P, NT, NC])
        neg_max1 = sb("neg_max1", [P, NT])
        sum1 = sb("sum1", [P, NT])
        inv1 = sb("inv1", [P, NT])
        p1T = scratch[0:NC, 0:NT * P].rearrange("k (t p) -> k t p", t=NT)
        turned = hT[:].rearrange("p a j b s -> p (a j b s)")[:, 0:B * S].rearrange("p (b s) -> p b s", b=B)
        tanh_in = scratch[:, 0:NT * D].rearrange("p (t d) -> p t d", t=NT)

        mask_at = NT * HM * NC // 2
        maskb = shared[:, mask_at:mask_at + NT * HM * NC // 4].bitcast(U8).rearrange("p (t n) -> p t n", t=NT)
        mask_neg = shared[:, 0:NT * HM * NC // 2].bitcast(BF16).rearrange("p (t n) -> p t n", t=NT)
        w16 = sb("w16", [P, 2, 4, D])
        WQ, WK, WV, WO = range(4)
        bo16 = sb("bo16", [P, 2, D])
        bq16 = sb("bq16", [P, 2])
        head_of_row = sb("head_of_row", [P, HM])
        half_of_row = sb("half_of_row", [P, 2])
        left_of_row = sb("left_of_row", [LP, LH])
        ctx_pair = sb("ctx_pair", [P, B, 2, PK])
        ctx_left = sb("ctx_left", [P, B, LH, LK])
        k16T = sb("k16T", [P, 2, B, NC])
        k_blocks = sb("k_blocks", [P, B, HM, NC])
        v_pair = sb("v_pair", [P, 2, B, D])
        v_left = sb("v_left", [LP, 2, B, D])
        va_pair = sb("va_pair", [P, 2, B, NPAIR, 2, DH + 1])
        va_left = sb("va_left", [LP, 2, B, HM, DH + 1])
        q16T = queries
        s16 = scratch[:].rearrange("p (z h k) -> p z h k", z=2, h=HM)
        neg_max16 = sb("neg_max16", [P, 2, HM])
        keep16 = sb("keep16", [P, HM])
        spoil16 = sb("spoil16", [P, 4, HM])
        inv16 = sb("inv16", [P, 2, HM])
        p16 = hT[:].rearrange("p a j b s -> p (a j b s)")[:, 0:2 * HM * NC].rearrange("p (z n) -> p z n", z=2)
        p16T = w2[:].rearrange("p e j d -> p (e j) d")[:, 0:NPAIR + 2, :]
        o16 = shared[:, 3 * mask_at // 2:3 * mask_at // 2 + NT * D].rearrange("p (t d) -> p t d", t=NT)

        def late(at, *dims):
            n = 1
            for d in dims:
                n *= d
            v = shared[:, at:at + n]
            return v.rearrange("p (i b s) -> p i b s", i=dims[0], b=dims[1]), at + n

        val, at = late(0, IT, B, S)
        val2, at = late(at, IT, B, S)
        tanh_out = shared[:, at:at + 2 * S].rearrange("p (n s) -> p n s", n=2)
        silu = shared[:, at + 2 * S:at + 4 * S].rearrange("p (n s) -> p n s", n=2)
        t3 = hT[:].rearrange("p a j b s -> p (a j b s)")[:, 0:IT * B * S].rearrange("p (i b s) -> p i b s", i=IT, b=B)
        w1_half = w1[:].rearrange("p e f -> p (e f)").bitcast(BF16)
        xqT = w1_half[:, 0:B * S].rearrange("p (b s) -> p b s", b=B)
        hq = w1_half[:, B * S:(1 + IT) * B * S].rearrange("p (i b s) -> p i b s", i=IT, b=B)
        wn2 = sb("wn2", [P, 3, IT * P])
        wmax2 = sb("wmax2", [P, 7])
        wscale2 = sb("wscale2", [P, 7])
        winv2 = sb("winv2", [P, 7])
        ab0_flat = ab0[:].rearrange("p h n -> p (h n)")
        w3T = ab0_flat[:, 0:3 * IT * P].rearrange("p (m n) -> p m n", m=3)
        w2T = ab0_flat[:, 3 * IT * P:3 * IT * P + 3 * IT * P // 2].bitcast(BF16).rearrange("p (m n) -> p m n", m=3)
        diag_down = sb("diag_down", [P, P])
        down_row = sb("down_row", [P, D])
        down_scale = sb("down_scale", [P, D])
        clip = sb("clip", [P, 2])
        clip_sig = sb("clip_sig", [P, 2])
        minus_rne = sb("minus_rne", [P, 1])
        plus_rne = sb("plus_rne", [P, 1])
        plus_rne_half = sb("plus_rne_half", [P, 1])
        wn3 = sb("wn3", [P, 3 * IT * 4, 32])
        wmax3 = sb("wmax3", [P, 3 * IT * 4])
        wscale3 = sb("wscale3", [P, 3 * IT * 4])
        winv3 = sb("winv3", [P, 3 * IT * 4])
        pmax = sb("pmax", [P, 2])
        gmax_row = sb("gmax_row", [1, 2])
        unit_max = sb("unit_max", [P, 2, IT * B])
        x_scale = sb("x_scale", [P, 1])
        x_inv = sb("x_inv", [P, 1])
        h_scale = sb("h_scale", [P, 1])
        h_inv = sb("h_inv", [P, 1])
        c_gate = sb("c_gate", [P, IT])
        c_both = sb("c_both", [P, IT])
        ug_scale = sb("ug_scale", [P, 2])
        ug_inv = sb("ug_inv", [P, 2])
        half_sg = sb("half_sg", [P, 1])
        amax3 = sb("amax3", [P, 2])
        scale3 = sb("scale3", [P, 2])
        inv3 = sb("inv3", [P, 2])
        ratio3 = sb("ratio3", [P, 2])

        in_x = [sem("in_x0"), sem("in_x1")]
        in_ctx = sem("in_ctx")
        in_vec0 = sem("in_vec0")
        in_vec = sem("in_vec")
        in_norm = sem("in_norm")
        in_w0 = [sem(f"in_w0_{n}") for n in range(2)]
        const_made = sem("const_made")
        ident_made = sem("ident_made")
        dve_step = sem("dve_step")
        pool_step = sem("pool_step")
        ctx_var_ok = sem("ctx_var_ok")
        ctx_rstd_ok = sem("ctx_rstd_ok")
        ctx_norm_ok = sem("ctx_norm_ok")
        var_ok = sem("var_ok")
        rstd_ok = sem("rstd_ok")
        xn_ok = sem("xn_ok")
        xT_in_psum = sem("xT_in_psum")
        xnT_b_ok = [sem("xnT0_ok"), sem("xnT1_ok")]
        cT_in_psum = sem("cT_in_psum")
        cT_ok = sem("cT_ok")
        vcol_in_psum = sem("vcol_in_psum")
        vcol_ok = sem("vcol_ok")
        bv_wide_ok = sem("bv_wide_ok")
        bv_used = sem("bv_used")
        wT_in_psum = sem("wT_in_psum")
        wT_ok = sem("wT_ok")
        ab_in_psum = sem("ab_in_psum")
        ab_ok = sem("ab_ok")
        a_now_ok = sem("a_now_ok")
        bias0_ok = sem("bias0_ok")
        x_biased = sem("x_biased")
        q_in_psum = sem("q_in_psum")
        q_full_ok = sem("q_full_ok")
        cT_lo_ok = sem("cT_lo_ok")
        q_ok = sem("q_ok")
        scores_ok = sem("scores_ok")
        max_ok = sem("max_ok")
        prob_ok = sem("prob_ok")
        pT_in_psum = sem("pT_in_psum")
        kv_lat_ok = sem("kv_lat_ok")
        xn_hi_ok = sem("xn_hi_ok")
        xn_lo_ok = sem("xn_lo_ok")
        kvT_hi_ok = [sem("kvT_hi_ok0"), sem("kvT_hi_ok1")]
        kvT_lo_ok = [sem("kvT_lo_ok0"), sem("kvT_lo_ok1")]
        pad_ok = sem("pad_ok")
        q_hi_ok = sem("q_hi_ok")
        pT_hi_ok = sem("pT_hi_ok")
        pT_lo_ok = sem("pT_lo_ok")
        pv_done = sem("pv_done")
        u_ok = sem("u_ok")
        o_in_psum = sem("o_in_psum")
        inv_ok = sem("inv_ok")
        o_added = sem("o_added")
        in_moe = sem("in_moe")
        in_l1 = sem("in_l1")
        rank_ok = sem("rank_ok")
        w1_upper_ok = sem("w1_upper_ok")
        w1_now_ok = sem("w1_now_ok")
        logit_in_psum = sem("logit_in_psum")
        diff_ok = sem("diff_ok")
        top_exp_ok = sem("top_exp_ok")
        gate_ok = sem("gate_ok")
        gT_in_psum = sem("gT_in_psum")
        gT_ok = sem("gT_ok")
        b2_in_psum = sem("b2_in_psum")
        b2_added = sem("b2_added")
        h_in_psum = sem("h_in_psum")
        h_ok = sem("h_ok")
        y_in_psum = sem("y_in_psum")
        y_added = sem("y_added")
        l1_in_psum = sem("l1_in_psum")
        l1_ok = sem("l1_ok")
        s1_in_psum = sem("s1_in_psum")
        s1_ok = sem("s1_ok")
        p1_ok = sem("p1_ok")
        p1T_in_psum = sem("p1T_in_psum")
        p1T_ok = sem("p1T_ok")
        o1_in_psum = sem("o1_in_psum")
        turned_ok = sem("turned_ok")
        res_in_psum = sem("res_in_psum")
        tanh_in_ok = sem("tanh_in_ok")
        tanh_ok = sem("tanh_ok")
        x_done = sem("x_done")
        in_mask = sem("in_mask")
        in_l16 = [sem("in_l2_attention"), sem("in_l3_attention")]
        in_f2 = sem("in_f2")
        in_f3 = sem("in_f3")
        mask_neg_ok = sem("mask_neg_ok")
        ctx_spread = sem("ctx_spread")
        kv16_in_psum = sem("kv16_in_psum")
        kv16_ok = sem("kv16_ok")
        kv16_spread = sem("kv16_spread")
        q16_in_psum = sem("q16_in_psum")
        q16_ok = sem("q16_ok")
        s16_in_psum = sem("s16_in_psum")
        s16_taken = sem("s16_taken")
        s16_ok = sem("s16_ok")
        max16_ok = sem("max16_ok")
        spoil16_ok = sem("spoil16_ok")
        p16_ok = sem("p16_ok")
        p16T_in_psum = sem("p16T_in_psum")
        p16T_ok = sem("p16T_ok")
        o16_in_psum = sem("o16_in_psum")
        o16_ok = sem("o16_ok")
        o16T_in_psum = sem("o16T_in_psum")
        o16T_ok = sem("o16T_ok")
        rne_made = sem("rne_made")
        clip_tanh_ok = sem("clip_tanh_ok")
        wmax_ok = sem("wmax_ok")
        wq2_ok = sem("wq2_ok")
        wq3_ok = sem("wq3_ok")
        w2T_in_psum = sem("w2T_in_psum")
        w2T_ok = sem("w2T_ok")
        w3T_in_psum = sem("w3T_in_psum")
        w3T_ok = sem("w3T_ok")
        xq_ok = sem("xq_ok")
        pmax_ok = sem("pmax_ok")
        pmaxT_in_psum = sem("pmaxT_in_psum")
        gmax_ok = sem("gmax_ok")
        gmax_in_psum = sem("gmax_in_psum")
        c_ok = sem("c_ok")
        gu_in_psum = sem("gu_in_psum")
        gu_tanh_ok = sem("gu_tanh_ok")
        gu_up_ok = sem("gu_up_ok")
        gu_silu_ok = sem("gu_silu_ok")
        gu_product_ok = sem("gu_product_ok")
        hscale_ok = sem("hscale_ok")
        h_rounded = sem("h_rounded")
        hq_ok = sem("hq_ok")
        ug_in_psum = sem("ug_in_psum")
        ug_copied = sem("ug_copied")
        ug_maxed = sem("ug_maxed")
        ug_scale_ok = sem("ug_scale_ok")
        gate_int_ok = sem("gate_int_ok")
        up_int_ok = sem("up_int_ok")
        tanh3_ok = sem("tanh3_ok")
        ratio_ok = sem("ratio_ok")
        act_rounded = sem("act_rounded")
        o3_ok = sem("o3_ok")
        x_final = sem("x_final")
        out_done = sem("out_done")

        block = ctx.enter_context(nc.Block())

        HALF = (NK // 2 + 3) // 4 * 4

        def chunk_keys(c):
            return P if c < TPB else NC

        def scores0(i):
            pair = bank[:, 2 * (i % 2):2 * (i % 2) + 2, :].rearrange("p b n -> p (b n)")
            return pair[:, S - HALF:S - HALF + NK]

        PT_BANK = ((4, 5, 4, 5, 4), (5, 4, 5, 4, 5))

        def wait_from(eng, semaphore, count):
            if not isinstance(count, int) or count > 0:
                eng.wait_ge(semaphore, count)

        def slot_free(eng, u, c):
            wait_from(eng, pv_done, NCH * u + c + 1 - (2, 2, NCH, 3, 3)[c])

        def run_heads(eng, step):
            def head(h, last=False):
                for b in range(B):
                    for c in range(NCH):
                        step(h, b, c, last and b == B - 1)
            head(0)
            head(1)
            with eng.Fori(2, H0 - 1) as h:
                head(h)
            head(H0 - 1, True)

        def from_unit(n, u):
            return not isinstance(u, int) or u >= n

        def split_matmul(out, lhsT, rhs, first=True, last=True):
            nc.tensor.matmul(out, lhsT[HI], rhs[HI], start=first, stop=False)
            nc.tensor.matmul(out, lhsT[HI], rhs[LO], start=False, stop=False)
            return nc.tensor.matmul(out, lhsT[LO], rhs[HI], start=False, stop=last)

        @block.sync
        def _(sp):
            half = H0 // 2
            for n in range(2):
                c = slice(n * half * D, (n + 1) * half * D)
                v = slice((H0 + n * half) * D, (H0 + (n + 1) * half) * D)
                sp.dma_start(wq0[:, c], a["L0_xattn_Wq"][:, c]).then_inc(in_w0[n], 16)
                sp.dma_start(wkv0[:, c], a["L0_xattn_Wkv"][:, c]).then_inc(in_w0[n], 16)
                sp.dma_start(wkv0[:, v], a["L0_xattn_Wkv"][:, v]).then_inc(in_w0[n], 16)
                sp.dma_start(wo0[:, n * half:(n + 1) * half, :],
                             a["L0_xattn_Wo"][c, :].rearrange("(h d) n -> d h n", d=D)).then_inc(in_w0[n], 16)
                if n == 0:
                    for dst, name in ((gamma_ctx, "L0_xattn_gamma_media"), (beta_ctx, "L0_xattn_beta_media"),
                                      (gamma_lat, "L0_xattn_gamma_lat"), (beta_lat, "L0_xattn_beta_lat"),
                                      (bo0, "L0_xattn_bo")):
                        sp.dma_start(dst[:], a[name].partition_broadcast(dst.shape[0])).then_inc(in_norm, 16)
            for n in VROWS[2:]:
                r, k = vrow[n]
                sp.dma_start(vec_rows[r - FIRST:r - FIRST + k, :], vsrc[n].rearrange("(r d) -> r d", d=D))\
                    .then_inc(in_vec, 16)
            sp.dma_start(w1[:], a["L0_ffn_W1"].rearrange("e h f -> h e f")).then_inc(in_moe, 16)
            sp.dma_start(w2[:], a["L0_ffn_W2"].rearrange("e (j p) o -> p e j o", p=P)).then_inc(in_moe, 16)
            sp.dma_start(wr[:], a["L0_ffn_Wr"]).then_inc(in_moe, 16)
            sp.dma_start(br[:], a["L0_ffn_br"].partition_broadcast(P)).then_inc(in_moe, 16)
            sp.dma_start(b2[:], a["L0_ffn_b2"]).then_inc(in_moe, 16)
            for n, name in ((L1Q, "xattn_Wq"), (L1K, "xattn_Wk"), (L1V, "xattn_Wv"), (L1P, "xattn_Wp"),
                            (L1F, "ffn_weight"), (L1A, "ffn_aux_weight1"), (L1B, "ffn_aux_weight2")):
                sp.dma_start(l1w[:, n, :], a["L1_" + name]).then_inc(in_l1, 16)
            sp.dma_start(bp1[:], a["L1_xattn_bp"].partition_broadcast(P)).then_inc(in_l1, 16)
            sp.dma_start(fbias1[:], a["L1_ffn_bias"].partition_broadcast(P)).then_inc(in_l1, 16)
            for n in range(2):
                for m, name in enumerate(("Wq", "Wk", "Wv", "Wo")):
                    sp.dma_start(w16[:, n, m, :], a[f"L{n + 2}_xattn_{name}"]).then_inc(in_l16[n], 16)
                sp.dma_start(bo16[:, n, :], a[f"L{n + 2}_xattn_bo"].partition_broadcast(P)).then_inc(in_l16[n], 16)
            for m, name in enumerate(("gate", "up")):
                w = a["L2_ffn_w_" + name]
                sp.dma_start(wn2[:, m, 0:2 * P].rearrange("p (i d) -> p i d", i=2),
                             w[0:2 * P, :].rearrange("(i p) d -> p i d", p=P)).then_inc(in_f2, 16)
                sp.dma_start(wn2[0:rows2[2], m, 2 * P:3 * P], w[2 * P:I2, :]).then_inc(in_f2, 16)
                sp.dma_start(wn3[:, 4 * IT * m:4 * IT * (m + 1), :].rearrange("p (i b) k -> p i (b k)", i=IT),
                             a["L3_ffn_w_" + name].rearrange("(i p) d -> p i d", p=P)).then_inc(in_f3, 16)
            sp.dma_start(wn2[:, 2, 0:I2], a["L2_ffn_w_down"]).then_inc(in_f2, 16)
            sp.dma_start(wn3[:, 8 * IT:12 * IT, :].rearrange("p b k -> p (b k)"), a["L3_ffn_w_down"])\
                .then_inc(in_f3, 16)
            sp.dma_start(clip[:, 0:1], a["L2_ffn_clip_x"].partition_broadcast(P)).then_inc(in_f2, 16)
            sp.dma_start(clip[:, 1:2], a["L2_ffn_clip_down"].partition_broadcast(P)).then_inc(in_f2, 16)
            sp.wait_ge(o_in_psum, U0)
            for t in range(NT):
                b, i = t // TPB, t % TPB
                sp.dma_start(maskb[:, t, :].rearrange("p (h k) -> p h k", h=HM),
                             a["mask_Bx16xSxS2_bk1"][b, :, i * P:(i + 1) * P, :].rearrange("h p k -> p h k"))\
                    .then_inc(in_mask, 16)
            sp.wait_ge(x_final, 1)
            sp.dma_start(out.rearrange("b (t p) d -> p b t d", p=P),
                         x[:].rearrange("p (b t) d -> p b t d", b=B)).then_inc(out_done, 16)
            sp.wait_ge(out_done, 16)

        @block.gpsimd
        def _(pool):
            own = Steps(pool, pool_step)
            nc.gpsimd.memset(ones[:], 1.0).then_inc(const_made, 1)
            nc.gpsimd.memset(minus_half[:], -0.5).then_inc(const_made, 1)
            own.add(nc.gpsimd.memset(ident[:], 0.0))
            own.settle()
            nc.gpsimd.affine_select(out=ident[:], in_=ident[:], compare_op=ALU.not_equal, fill=1.0, base=0,
                                    pattern=[[-1, P]], channel_multiplier=1).then_inc(ident_made, 1)
            pool.wait_ge(const_made, 2)
            pool.wait_ge(ctx_var_ok, 1)
            nc.gpsimd.tensor_tensor(ctx_rstd[:], ctx_var_eps[:], minus_half[0:NC, 0:B], ALU.pow)\
                .then_inc(ctx_rstd_ok, 1)
            for b in range(B):
                c = slice(TPB * b, TPB * (b + 1))
                pool.wait_ge(var_ok, b + 1)
                own.add(nc.gpsimd.tensor_tensor(rstd[:, c], var_eps[:, c], minus_half[:, 0:TPB], ALU.pow))
                own.settle()
                own.add(nc.gpsimd.tensor_tensor(rstd_again[:, c], rstd[:, c], rstd[:, c], ALU.mult))
                own.settle()
                own.add(nc.gpsimd.tensor_tensor(rstd_again[:, c], rstd_again[:, c], meanvar[:, c, 1], ALU.mult))
                own.settle()
                own.add(nc.gpsimd.tensor_scalar(rstd_again[:, c], rstd_again[:, c], EPS, None, ALU.add))
                own.settle()
                own.add(nc.gpsimd.tensor_tensor(rstd_again[:, c], rstd_again[:, c], minus_half[:, 0:TPB], ALU.pow))
                own.settle()
                nc.gpsimd.tensor_tensor(rstd[:, c], rstd[:, c], rstd_again[:, c], ALU.mult).then_inc(rstd_ok, 1)
            if NK % 2:
                for part in kvT:
                    nc.gpsimd.memset(part[:, :, NK:NK + 1].bitcast(F32), 0.0).then_inc(pad_ok, 1)
            def stationary(h):
                pool.wait_ge(ab_ok, h + 1)
                if h >= 1:
                    pool.wait_ge(q_in_psum, B * h)
                own.add(nc.gpsimd.tensor_copy(a_now[HI][:], ab0[:, h, 0:P]))
                own.settle()
                nc.gpsimd.tensor_tensor(a_now[LO][:], ab0[:, h, 0:P], a_now[HI][:].bitcast(F32), ALU.subtract)\
                    .then_inc(a_now_ok, 1)

            stationary(0)
            pool.wait_ge(bias0_ok, 1)
            pool.wait_ge(xn_ok, NT)
            nc.gpsimd.tensor_tensor(x[:], x[:], out_bias0[:].unsqueeze(1).to_broadcast([P, NT, D]), ALU.add)\
                .then_inc(x_biased, 1)
            nc.gpsimd.memset(plus_rne[:], RNE).then_inc(rne_made, 1)
            nc.gpsimd.memset(minus_rne[:], -RNE).then_inc(rne_made, 1)
            nc.gpsimd.memset(plus_rne_half[:], RNE + 32768).then_inc(rne_made, 1)
            for tile, width, count in ((head_of_row, DH, HM), (half_of_row, PK, 2), (left_of_row, LK, LH)):
                own.add(nc.gpsimd.memset(tile[:], 1.0))
                own.settle()
                own.add(nc.gpsimd.affine_select(out=tile[:], in_=tile[:], compare_op=ALU.is_ge, fill=0.0, base=0,
                                                pattern=[[-width, count]], channel_multiplier=1))
                own.settle()
                own.add(nc.gpsimd.affine_select(out=tile[:], in_=tile[:], compare_op=ALU.is_ge, fill=0.0,
                                                base=width - 1, pattern=[[width, count]], channel_multiplier=-1))
                own.settle()
            pool.wait_ge(cT_ok, 2)
            nc.gpsimd.tensor_copy(ctx_pair[:], ctxT[:, :, 0:PK].unsqueeze(2).to_broadcast([P, B, 2, PK]))\
                .then_inc(ctx_spread, 1)
            nc.gpsimd.tensor_copy(ctx_left[:], ctxT[:, :, PK:NC].unsqueeze(2).to_broadcast([P, B, LH, LK]))\
                .then_inc(ctx_spread, 1)
            for e in range(E):
                nc.gpsimd.memset(rank[:, :, e:e + 1], float(E - e)).then_inc(rank_ok, 1)

            def inverse_root(k):
                for b in range(B):
                    c = slice(TPB * b, TPB * (b + 1))
                    pool.wait_ge(var_ok, B * k + b + 1)
                    nc.gpsimd.tensor_tensor(rstd[:, c], var_eps[:, c], minus_half[:, 0:TPB], ALU.pow)\
                        .then_inc(rstd_ok, 1)

            def add_bias(k, bias):
                pool.wait_ge(xn_ok, NT * (k + 1))
                nc.gpsimd.tensor_tensor(x[:], x[:], bias.unsqueeze(1).to_broadcast([P, NT, D]), ALU.add)\
                    .then_inc(x_biased, 1)

            def whole_weights2():
                pool.wait_ge(wmax_ok, 1)
                for m in range(2):
                    for i in range(IT):
                        w, r = wn2[0:rows2[i], m, i * P:(i + 1) * P], rows2[i]
                        inverse = winv2[0:r, IT * m + i:IT * m + i + 1]
                        own.add(nc.gpsimd.tensor_scalar(w, w, inverse, RNE, ALU.mult, ALU.add))
                w = wn2[:, 2, 0:I2]
                own.add(nc.gpsimd.tensor_scalar(w, w, winv2[:, 6:7], RNE, ALU.mult, ALU.add))
                own.settle()
                for m in range(2):
                    for i in range(IT):
                        w = wn2[0:rows2[i], m, i * P:(i + 1) * P]
                        nc.gpsimd.tensor_scalar(w, w, -RNE, None, ALU.add).then_inc(wq2_ok, 1)
                w = wn2[:, 2, 0:I2]
                nc.gpsimd.tensor_scalar(w, w, -RNE, None, ALU.add).then_inc(wq2_ok, 1)
                nc.gpsimd.tensor_scalar(diag_down[:], ident[:], wscale2[:, 6:7], None, ALU.mult).then_inc(wq2_ok, 1)

            def whole_weights3(m):
                pool.wait_ge(wmax_ok, 2)
                w, c = wn3[:, 4 * IT * m:4 * IT * (m + 1), :], slice(4 * IT * m, 4 * IT * (m + 1))
                own.add(nc.gpsimd.tensor_tensor(w, w, winv3[:, c].unsqueeze(2).to_broadcast([P, 4 * IT, 32]), ALU.mult))
                own.settle()
                own.add(nc.gpsimd.tensor_scalar(w, w, RNE, None, ALU.add))
                own.settle()
                own.add(nc.gpsimd.tensor_scalar(w, w, -RNE, None, ALU.add))
                own.settle()
                nc.gpsimd.tensor_tensor(w, w, wscale3[:, c].unsqueeze(2).to_broadcast([P, 4 * IT, 32]), ALU.mult)\
                    .then_inc(wq3_ok, 1)

            for h in range(1, H0):
                stationary(h)
                if h == 3:
                    whole_weights2()
                if h in (4, 5, 6):
                    whole_weights3(h - 4)

            def spread_kv(n):
                pool.wait_ge(kv16_ok, 3 * (n + 1))
                if n:
                    pool.wait_ge(s16_in_psum, NT)
                for b in range(B):
                    nc.gpsimd.tensor_tensor(k_blocks[:, b], k16T[:, n, b, :].unsqueeze(1).to_broadcast([P, HM, NC]),
                                            head_of_row[:].unsqueeze(2).to_broadcast([P, HM, NC]), ALU.mult)\
                        .then_inc(kv16_spread, 1)
                    half = half_of_row[:].unsqueeze(1)
                    by_pair = v_pair[:, n, b, :].rearrange("p (c h d) -> p c h d", c=NPAIR, h=2)
                    for hd in range(2):
                        nc.gpsimd.tensor_scalar(va_pair[:, n, b, :, hd, 0:DH], by_pair[:, :, hd, :],
                                                half_of_row[:, hd:hd + 1], None, ALU.mult).then_inc(kv16_spread, 1)
                    nc.gpsimd.tensor_copy(va_pair[:, n, b, :, :, DH], half.to_broadcast([P, NPAIR, 2]))\
                        .then_inc(kv16_spread, 1)
                    by_head = v_left[:, n, b, :].rearrange("p (h d) -> p h d", h=HM)
                    for g in range(2):
                        nc.gpsimd.tensor_tensor(va_left[:, n, b, LH * g:LH * (g + 1), 0:DH],
                                                by_head[:, LH * g:LH * (g + 1), :],
                                                left_of_row[:].unsqueeze(2).to_broadcast([LP, LH, DH]), ALU.mult)\
                            .then_inc(kv16_spread, 1)
                        nc.gpsimd.tensor_copy(va_left[:, n, b, LH * g:LH * (g + 1), DH], left_of_row[:])\
                            .then_inc(kv16_spread, 1)

            def less_maximum(t, n):
                pool.wait_ge(max16_ok, NT * n + t + 1)
                nc.gpsimd.tensor_tensor(s16[:, t % 2], s16[:, t % 2],
                                        neg_max16[:, t % 2, :].unsqueeze(2).to_broadcast([P, HM, NC]), ALU.add)\
                    .then_inc(s16_ok, 1)

            pool.wait_ge(in_moe, 16 * 5)
            inverse_root(1)
            pool.wait_ge(pv_done, NCH * U0)

            def expert_weights(e, side):
                one = slice(e, e + 1)
                wait_from(pool, h_in_psum, FT * B * (e - 1))
                nc.gpsimd.tensor_copy(w1_now[HI][:, side:side + 1, :], w1[:, one, :]).then_inc(w1_upper_ok, 1)
                pool.wait_ge(w1_upper_ok, e + 1)
                nc.gpsimd.tensor_tensor(w1_now[LO][:, side:side + 1, :], w1[:, one, :],
                                        w1_now[HI][:, side:side + 1, :].bitcast(F32), ALU.subtract)\
                    .then_inc(w1_now_ok, 1)

            expert_weights(0, 0)
            for t in range(NT):
                if t + 1 < E:
                    expert_weights(t + 1, (t + 1) % 2)
                if t == 0:
                    pool.wait_ge(in_mask, 16 * NT)
                nc.gpsimd.tensor_scalar(mask_neg[:, t, :], maskb[:, t, :], MASKED, None, ALU.mult)\
                    .then_inc(mask_neg_ok, 1)
            inverse_root(2)
            pool.wait_ge(in_l1, 16 * 9)
            add_bias(2, bp1[:])
            spread_kv(0)
            inverse_root(3)
            inverse_root(4)
            add_bias(4, bo16[:, 0, :])
            for t in range(NT):
                less_maximum(t, 0)
                spoil = spoil16[:, t % 4, :]
                if t:
                    pool.wait_ge(spoil16_ok, t)
                if t >= 4:
                    pool.wait_ge(o16_ok, t - 3)
                own.add(nc.gpsimd.tensor_scalar(keep16[:], neg_max16[:, t % 2, :], 1e37, None, ALU.is_lt))
                own.settle()
                own.add(nc.gpsimd.tensor_scalar(spoil, keep16[:], -1.0, 3e38, ALU.add, ALU.mult))
                own.settle()
                own.add(nc.gpsimd.tensor_scalar(spoil, spoil, 3e38, None, ALU.mult))
                own.settle()
                nc.gpsimd.tensor_tensor(spoil, spoil, keep16[:], ALU.mult).then_inc(spoil16_ok, 1)
            inverse_root(5)
            spread_kv(1)
            for n in range(IT * B):
                b, i, r = n // IT, n % IT, rows2[n % IT]
                pool.wait_ge(gu_silu_ok, n + 1)
                pool.wait_ge(gu_up_ok, n + 1)
                nc.gpsimd.tensor_tensor(val[0:r, i, b, :], val[0:r, i, b, :], silu[0:r, n % 2, :], ALU.mult)\
                    .then_inc(gu_product_ok, 1)
            inverse_root(6)
            add_bias(6, bo16[:, 1, :])
            for t in range(NT):
                less_maximum(t, 1)
            inverse_root(7)
            pool.wait_ge(ug_scale_ok, 1)
            pool.wait_ge(ug_copied, 2 * IT * B)
            for b in range(B):
                up = val[:, :, b, :]
                own.add(nc.gpsimd.tensor_scalar(up, up, ug_inv[:, 1:2], RNE, ALU.mult, ALU.add))
                own.settle()
                nc.gpsimd.tensor_scalar(up, up, -RNE, None, ALU.add).then_inc(up_int_ok, 1)

        @block.tensor
        def _(pe):
            pe.wait_ge(ident_made, 1)

            def keys_transposes():
                pe.wait_ge(ctx_norm_ok, 1)
                for b in range(B):
                    nc.tensor.transpose(bank[:, 6, b * P:b * P + NC], ctx_norm[:, b, :], ident[0:NC, 0:NC])
                for b in range(B):
                    last = nc.tensor.transpose(bank[:, 6, (B + b) * P:(B + b) * P + NC], ctx_tok[:, b, :],
                                               ident[0:NC, 0:NC])
                last.then_inc(cT_in_psum, 1)
                for t in range(NT):
                    pe.wait_ge(xn_ok, t + 1)
                    nc.tensor.transpose(bank[:, 4 + t // TPB, (t % TPB) * P:(t % TPB + 1) * P], xn[:, t, :], ident[:])\
                        .then_inc(xT_in_psum, 1)

            for h in range(H0 + 1):
                if h < H0:
                    c = slice(h * D, (h + 1) * D)
                    v = slice((H0 + h) * D, (H0 + h + 1) * D)
                    pe.wait_ge(in_w0[2 * h // H0], 64)
                    if h >= 2:
                        pe.wait_ge(wT_ok, h - 1)
                    for n, w in enumerate((wq0[:, c], wkv0[:, c], wkv0[:, v])):
                        last = nc.tensor.transpose(bank[:, h % 2, n * P:(n + 1) * P], w, ident[:])
                    last.then_inc(wT_in_psum, 1)
                if h == 1:
                    pe.wait_ge(in_vec0, 32)
                    nc.tensor.transpose(bank[:, 6, 0:FIRST], vec_rows0[:], ident[0:FIRST, 0:FIRST])\
                        .then_inc(vcol_in_psum, 1)
                    pe.wait_ge(vcol_ok, 2)
                if h == H0 // 2:
                    keys_transposes()
                if h:
                    g = h - 1
                    rb = 2 + g % 2
                    pe.wait_ge(wT_ok, g + 1)
                    if g >= 2:
                        pe.wait_ge(ab_ok, g - 1)
                    nc.tensor.matmul(bank[:, rb, 0:P], wT0[:, g % 2, 0, :], wT0[:, g % 2, 1, :], start=True, stop=True)
                    nc.tensor.matmul(bank[:, rb, P:2 * P], wT0[:, g % 2, 2, :], wo0[:, g, :], start=True, stop=True)
                    nc.tensor.matmul(bank[:, rb, 2 * P:2 * P + 1], wT0[:, g % 2, 1, :], bq0_scaled[:, g:g + 1],
                                     start=True, stop=True).then_inc(ab_in_psum, 1)
                    pe.wait_ge(bv_wide_ok, g + 1)
                    nc.tensor.matmul(bank[:, 7, 0:D], bv0_wide[:, g % 2, :], wo0[:, g, :],
                                     start=(g == 0), stop=(g == H0 - 1)).then_inc(bv_used, 1)
            def query(h, b):
                u = B * h + b
                pe.wait_ge(a_now_ok, h + 1)
                wait_from(pe, o_added, u - 3)
                wait_from(pe, q_full_ok, u)
                split_matmul(bank[:, 7, :], [part[:] for part in a_now], [part[:, b, 0:S] for part in kvT])\
                    .then_inc(q_in_psum, 1)

            def scores(u, b, i):
                first = 2 * (i % 2)
                if i == 0:
                    pe.wait_ge(q_ok, u + 1)
                wait_from(pe, prob_ok, TPB * u + i - 1)
                q = [part[:, b, i * P:(i + 1) * P] for part in qT]
                wide = NK + NK % 2
                left, right = bank[:, first, S - HALF:S], bank[:, first + 1, 0:wide - HALF]
                for stationary, moving in ((HI, HI), (HI, LO), (LO, HI)):
                    begin, end = stationary == moving, stationary == LO
                    nc.tensor.matmul(left, q[stationary], kvT[moving][:, b, 0:HALF], start=begin, stop=end)
                    last = nc.tensor.matmul(right, q[stationary], kvT[moving][:, b, HALF:wide], start=begin, stop=end)
                last.then_inc(scores_ok, 1)

            def transpose_chunk(u, b, c):
                n = chunk_keys(c)
                if c == 0:
                    pe.wait_ge(prob_ok, TPB * (u + 1))
                wait_from(pe, pT_lo_ok, NCH * u + c - 1)
                for i in range(TPB):
                    last = nc.tensor.transpose(bank[0:n, PT_BANK[b][c], i * P:(i + 1) * P],
                                               prob[b][:, i, c * P:c * P + n], ident[:])
                last.then_inc(pT_in_psum, 1)

            def attend(u, b, c):
                n = chunk_keys(c)
                pe.wait_ge(pT_lo_ok, NCH * u + c + 1)
                if c == 0:
                    wait_from(pe, u_ok, u)
                kv = [kv_lat[m][:, TPB * b + c, :] if c < TPB else kv_ctx[m][:, b, :] for m in (HI, LO)]
                split_matmul(bank[:, 6, :], kv, [part[0:n, SLOT[c], :] for part in probT], c == 0, c == NCH - 1)\
                    .then_inc(pv_done, 1)

            def output(h, b, asked):
                u = B * h + b
                pe.wait_ge(u_ok, u + 1)
                pe.wait_ge(q_full_ok, asked)
                wait_from(pe, o_added, u)
                for i in range(TPB):
                    last = nc.tensor.matmul(bank[:, 7, i * P:(i + 1) * P], uT[:, i * P:(i + 1) * P],
                                            ab0[:, bass.ds(h, 1), P:2 * P].rearrange("p n m -> p (n m)"),
                                            start=True, stop=True)
                last.then_inc(o_in_psum, 1)

            def step(h, b, c, last):
                u = B * h + b
                if c == 2 and not last:
                    query(h + b, 1 - b)
                if c < TPB:
                    scores(u, b, c)
                if from_unit(1, u):
                    transpose_chunk(u - 1, 1 - b, c)
                if c == TPB and from_unit(2, u):
                    output(h - 1, b, U0 if last else u + 2)
                if c == 0 and from_unit(2, u):
                    attend(u - 2, b, NCH - 1)
                if c and from_unit(1, u):
                    attend(u - 1, 1 - b, c - 1)

            pe.wait_ge(in_vec, 16 * (len(VROWS) - 2))
            pe.wait_ge(wT_ok, H0)
            nc.tensor.transpose(bank[:, 1, 0:nrow - FIRST], vec_rows[:], ident[0:nrow - FIRST, 0:nrow - FIRST])\
                .then_inc(vcol_in_psum, 1)
            pe.wait_ge(bias0_ok, 1)
            pe.wait_ge(ab_ok, H0)
            for b in range(B):
                pe.wait_ge(kvT_lo_ok[b], 1)
            query(0, 0)
            pe.wait_ge(cT_lo_ok, 1)
            pe.wait_ge(kv_lat_ok, 2 * (B + 1))
            pe.wait_ge(pad_ok, 2)
            pe.wait_ge(vcol_ok, 5)
            run_heads(pe, step)
            def l1_products(n):
                if n == 0:
                    pe.wait_ge(in_l1, 16 * 9)
                    pe.wait_ge(prob_ok, TPB * U0)
                    nc.tensor.transpose(bank[:, 0, 0:P], l1w[:, L1Q, :], ident[:])
                    nc.tensor.transpose(bank[:, 0, P:2 * P], l1w[:, L1F, :], ident[:])
                    nc.tensor.matmul(bank[:, 1, 0:B * NC], l1w[:, L1K, :], ctxT[:].rearrange("p b k -> p (b k)"),
                                     start=True, stop=True)
                    for b in range(B):
                        last = nc.tensor.matmul(bank[0:NC, 2, b * D:(b + 1) * D], ctxT[:, b, :], l1w[:, L1V, :],
                                                start=True, stop=True)
                    last.then_inc(l1_in_psum, 1)
                elif n == 1:
                    pe.wait_ge(l1_ok, 3)
                    nc.tensor.matmul(bank[:, 3, 0:B * NC], l1T[:, 0, :], k1T[:].rearrange("p b k -> p (b k)"),
                                     start=True, stop=True)
                    nc.tensor.matmul(bank[:, 3, 256:256 + P], l1w[:, L1A, :], l1T[:, 1, :], start=True, stop=True)\
                        .then_inc(l1_in_psum, 1)
                else:
                    pe.wait_ge(l1_ok, 5)
                    nc.tensor.matmul(bank[:, 0, 0:D], wa1T[:], l1w[:, L1B, :], start=True, stop=True)\
                        .then_inc(l1_in_psum, 1)

            for c in range(NCH):
                transpose_chunk(U0 - 1, B - 1, c)
                attend(U0 - 1 if c else U0 - 2, B - 1 if c else 0, (c - 1) % NCH)
                if c in (0, 2, 3):
                    l1_products((0, 2, 3).index(c))
            output(H0 - 1, 0, U0)
            attend(U0 - 1, B - 1, NCH - 1)
            output(H0 - 1, B - 1, U0)

            def norm_transposes(k, quantised=None):
                for t in range(NT):
                    if quantised is None:
                        pe.wait_ge(xn_ok, NT * k + t + 1)
                    else:
                        pe.wait_ge(xq_ok, B * quantised + t // TPB + 1)
                    nc.tensor.transpose(bank[:, 4 + t // TPB, (t % TPB) * P:(t % TPB + 1) * P], xn[:, t, :], ident[:])\
                        .then_inc(xT_in_psum, 1)

            def tile_T(t):
                return xnT[:, t // TPB, (t % TPB) * P:(t % TPB + 1) * P]

            def normed(k):
                for b in range(B):
                    pe.wait_ge(xnT_b_ok[b], k)

            norm_transposes(1)
            normed(1)

            def hidden(e, side):
                pe.wait_ge(w1_now_ok, e + 1)
                for j in range(FT):
                    for b in range(B):
                        n = j * B + b
                        if isinstance(e, int) and e == 0:
                            pe.wait_ge(xn_lo_ok, b + 1)
                            pe.wait_ge(l1_ok, 6)
                        else:
                            pe.wait_ge(h_ok, FT * B * (e - 1) + n + 1)
                        split_matmul(bank[:, n, :], [part[:, side, j * P:(j + 1) * P] for part in w1_now],
                                     [part[:, b, :] for part in qT]).then_inc(h_in_psum, 1)

            def expert_out(e, side):
                for b in range(B):
                    pe.wait_ge(h_ok, FT * B * e + FT * B)
                    if isinstance(e, int) and e == 0:
                        pe.wait_ge(o_added, U0)
                    else:
                        pe.wait_ge(y_added, B * (e - 1) + b + 1)
                    for i in range(TPB):
                        for j in range(FT):
                            last = nc.tensor.matmul(bank[:, 6 + b, i * P:(i + 1) * P],
                                                    hT[:, side, j, b, i * P:(i + 1) * P],
                                                    w2[:, bass.ds(e, 1), j, :].rearrange("p n d -> p (n d)"),
                                                    start=(j == 0), stop=(j == FT - 1))
                    last.then_inc(y_in_psum, 1)

            hidden(0, 0)
            pe.wait_ge(in_moe, 16 * 5)
            for t in range(NT):
                last = nc.tensor.matmul(bank[:, 4, t * E:(t + 1) * E], tile_T(t), wr[:], start=True, stop=True)
            last.then_inc(logit_in_psum, 1)
            hidden(1, 1)
            expert_out(0, 0)
            pe.wait_ge(gate_ok, 1)
            for t in range(NT):
                last = nc.tensor.transpose(bank[0:E, 4 + t // TPB, (t % TPB) * P:(t % TPB + 1) * P],
                                           gate[:, t, :], ident[:])
            last.then_inc(gT_in_psum, 1)
            pe.wait_ge(gT_ok, 1)
            for t in range(NT):
                last = nc.tensor.matmul(bank[:, 4 + t // TPB, (t % TPB) * P:(t % TPB + 1) * P], gateT[:, t, :], b2[:],
                                        start=True, stop=True)
            last.then_inc(b2_in_psum, 1)
            with pe.Fori(1, E // 2) as pair:
                for side in range(2):
                    hidden(pair * 2 + side, side)
                    expert_out(pair * 2 + (side - 1), 1 - side)
            expert_out(E - 1, 1)

            def residual_out(k, weight, ready):
                for b in range(B):
                    ready(b)
                    for i in range(TPB):
                        last = nc.tensor.matmul(bank[:, 6 + b, i * P:(i + 1) * P], weight[0](TPB * b + i), weight[1],
                                                start=True, stop=True)
                    last.then_inc(res_in_psum, 1)

            def keys_values(n):
                pe.wait_ge(in_l16[n], 80)
                pe.wait_ge(ctx_spread, 2)
                if n:
                    pe.wait_ge(s1_ok, B * n)
                else:
                    pe.wait_ge(h_ok, FT * B * E)
                nc.tensor.matmul(bank[:, 0, 0:B * NC], w16[:, n, WK, :], ctxT[:].rearrange("p b k -> p (b k)"),
                                 start=True, stop=True)
                for b in range(B):
                    nc.tensor.matmul(bank[:, 1, b * D:(b + 1) * D], ctx_pair[:, b].rearrange("p n k -> p (n k)"),
                                     w16[:, n, WV, :], start=True, stop=True)
                for b in range(B):
                    last = nc.tensor.matmul(bank[0:LP, 1, (B + b) * D:(B + b + 1) * D],
                                            ctx_left[:, b].rearrange("p n k -> p (n k)"), w16[:, n, WV, :],
                                            start=True, stop=True)
                last.then_inc(kv16_in_psum, 1)

            def global_max(j, count):
                pe.wait_ge(pmax_ok, j + 1)
                for c in range(count):
                    last = nc.tensor.transpose(bank[0:1, 7, c * P:(c + 1) * P], pmax[:, c:c + 1], ident[:])
                last.then_inc(pmaxT_in_psum, 1)
                pe.wait_ge(gmax_ok, j + 1)
                nc.tensor.matmul(bank[:, 7, 2 * P:2 * P + count], ones[0:1, :], gmax_row[:, 0:count],
                                 start=True, stop=True).then_inc(gmax_in_psum, 1)

            def attention16(n, k):
                norm_transposes(k)

                def queries_of(b):
                    pe.wait_ge(xnT_b_ok[b], k)
                    nc.tensor.matmul(bank[:, 6 + b, :], w16[:, n, WQ, :], xnT[:, b, :], start=True, stop=True)\
                        .then_inc(q16_in_psum, 1)

                def scores(t):
                    b, m = t // TPB, NT * n + t
                    pe.wait_ge(q16_ok, B * n + b + 1)
                    q = q16T[:, b, (t % TPB) * P:(t % TPB + 1) * P]
                    if t:
                        pe.wait_ge(s16_taken, m)
                    for g in range(4):
                        last = nc.tensor.matmul(bank[:, g, 0:BK * NC], q,
                                                k_blocks[:, b, BK * g:BK * (g + 1), :].rearrange("p h k -> p (h k)"),
                                                start=True, stop=True)
                    last.then_inc(s16_in_psum, 1)

                def transposes(t):
                    m, z = NT * n + t, t % 2
                    pe.wait_ge(p16_ok, 2 * (m + 1))
                    if t:
                        pe.wait_ge(p16T_ok, 2 * m)
                    else:
                        pe.wait_ge(q16_ok, B * (n + 1))
                    for c in range(NPAIR):
                        last = nc.tensor.transpose(bank[:, 4 + c // 4, (c % 4) * P:(c % 4 + 1) * P],
                                                   p16[:, z, 2 * PK * c:2 * PK * (c + 1)], ident[:])
                    last.then_inc(p16T_in_psum, 1)
                    for g in range(2):
                        first = HM * PK + LP * g
                        last = nc.tensor.transpose(bank[0:LP, 6, g * P:(g + 1) * P], p16[:, z, first:first + LP],
                                                   ident[:])
                    last.then_inc(p16T_in_psum, 1)

                def averages(t):
                    b, m = t // TPB, NT * n + t
                    pe.wait_ge(p16T_ok, 2 * m + 2)
                    if m >= 1:
                        pe.wait_ge(o16_ok, m)
                    o, w = bank[:, 7, 0:HM * (DH + 1)], DH + 1
                    for g in range(2):
                        nc.tensor.matmul(o[:, LH * w * g:LH * w * (g + 1)], p16T[0:LP, NPAIR + g, :],
                                         va_left[:, n, b, LH * g:LH * (g + 1), :].rearrange("p h d -> p (h d)"),
                                         start=(g == 0), stop=False, skip_group_check=True)
                    for c in range(NPAIR):
                        last = nc.tensor.matmul(o[:, 2 * w * c:2 * w * (c + 1)], p16T[:, c, :],
                                                va_pair[:, n, b, c].rearrange("p h d -> p (h d)"),
                                                start=False, stop=(c == NPAIR - 1), skip_group_check=True)
                    last.then_inc(o16_in_psum, 1)

                queries_of(0)
                pe.wait_ge(kv16_spread, 8 * B * (n + 1))
                scores(0)
                scores(1)
                queries_of(1)
                for t in range(NT + 1):
                    if t + 2 < NT:
                        scores(t + 2)
                    if t:
                        averages(t - 1)
                    if t < NT:
                        transposes(t)
                pe.wait_ge(s16_taken, NT * (n + 1))
                for t in range(NT):
                    pe.wait_ge(o16_ok, NT * n + t + 1)
                    last = nc.tensor.transpose(bank[:, t // TPB, (t % TPB) * P:(t % TPB + 1) * P], o16[:, t, :],
                                               ident[:])
                    if t % TPB == TPB - 1:
                        last.then_inc(o16T_in_psum, 1)
                residual_out(2 + 2 * n, (lambda t: q16T[:, t // TPB, (t % TPB) * P:(t % TPB + 1) * P],
                                         w16[:, n, WO, :]),
                             lambda b: pe.wait_ge(o16T_ok, B * n + b + 1))

            keys_values(0)
            norm_transposes(2)
            for t in range(NT):
                b, i = t // TPB, t % TPB
                if i == 0:
                    pe.wait_ge(xnT_b_ok[b], 2)
                last = nc.tensor.matmul(bank[:, b, i * NC:(i + 1) * NC], tile_T(t), kq1[:, b, :],
                                        start=True, stop=True)
                if i == TPB - 1:
                    last.then_inc(s1_in_psum, 1)
            for b in range(B):
                pe.wait_ge(p1_ok, b + 1)
                for i in range(TPB):
                    last = nc.tensor.transpose(bank[0:NC, 2 + b, i * P:(i + 1) * P], s1[:, TPB * b + i, :], ident[:])
                last.then_inc(p1T_in_psum, 1)
            for b in range(B):
                pe.wait_ge(p1T_ok, b + 1)
                for i in range(TPB):
                    last = nc.tensor.matmul(bank[:, 4 + b, i * P:(i + 1) * P], p1T[:, TPB * b + i, :], v1[:, b, :],
                                            start=True, stop=True)
                last.then_inc(o1_in_psum, 1)
            pe.wait_ge(y_added, B * E)
            residual_out(0, (lambda t: turned[:, t // TPB, (t % TPB) * P:(t % TPB + 1) * P], l1w[:, L1P, :]),
                         lambda b: pe.wait_ge(turned_ok, b + 1))
            keys_values(1)
            norm_transposes(3)

            def ready(b):
                pe.wait_ge(xnT_b_ok[b], 3)
                pe.wait_ge(x_done, b + 1)

            residual_out(1, (tile_T, waa1[:]), ready)
            pe.wait_ge(wq2_ok, 8)
            pe.wait_ge(kv16_ok, 6)
            for m in range(3):
                for i in range(IT):
                    r, to = rows2[i], bank[:, m, i * P:i * P + rows2[i]]
                    if m < 2:
                        nc.tensor.transpose(to, wn2[0:r, m, i * P:(i + 1) * P], ident[0:r, 0:r])
                    else:
                        nc.tensor.transpose(bank[0:r, m, i * P:(i + 1) * P], wn2[:, m, i * P:i * P + r], ident[:])
            nc.tensor.matmul(bank[:, 3, 0:P], ones[:], diag_down[:], start=True, stop=True).then_inc(w2T_in_psum, 1)
            attention16(0, 4)
            pe.wait_ge(wq3_ok, 3)
            pe.wait_ge(o16T_ok, B)
            w3 = wn3[:].rearrange("p (m i b) k -> p m i (b k)", m=3, i=IT)
            for m in range(3):
                for i in range(IT):
                    last = nc.tensor.transpose(bank[:, m, i * P:(i + 1) * P], w3[:, m, i, :], ident[:])
            last.then_inc(w3T_in_psum, 1)
            global_max(0, 1)
            norm_transposes(5, 0)
            normed(5)
            pe.wait_ge(w2T_ok, 5)
            pe.wait_ge(w3T_ok, 1)
            for b in range(B):
                for i in range(IT):
                    n, r = IT * b + i, rows2[i]
                    if n >= 3:
                        pe.wait_ge(gu_silu_ok, n - 2)
                        pe.wait_ge(gu_up_ok, n - 2)
                    for m in range(2):
                        last = nc.tensor.matmul(bank[0:r, 2 * (n % 3) + m, :], w2T[:, m, i * P:i * P + r], xqT[:, b, :],
                                                start=True, stop=True)
                    last.then_inc(gu_in_psum, 1)
            global_max(1, 1)
            for b in range(B):
                pe.wait_ge(hq_ok, IT * (b + 1))
                for t in range(TPB):
                    for i in range(IT):
                        r = rows2[i]
                        last = nc.tensor.matmul(bank[:, 6 + b, t * P:(t + 1) * P], hq[0:r, i, b, t * P:(t + 1) * P],
                                                w2T[0:r, 2, i * P:(i + 1) * P], start=(i == 0), stop=(i == IT - 1))
                last.then_inc(res_in_psum, 1)
            attention16(1, 6)
            global_max(2, 1)
            norm_transposes(7, 1)
            normed(7)
            pe.wait_ge(o16T_ok, 2 * B)
            for b in range(B):
                for i in range(IT):
                    n = IT * b + i
                    if n >= 3:
                        pe.wait_ge(ug_copied, 2 * (n - 2))
                    for m in range(2):
                        nc.tensor.matmul(bank[:, 2 * (n % 3) + m, :], w3T[:, m, i * P:(i + 1) * P], xnT[:, b, :],
                                         start=True, stop=True).then_inc(ug_in_psum, 1)
            for j, count in ((3, 2), (4, 1), (5, 1)):
                global_max(j, count)
            for b in range(B):
                pe.wait_ge(o3_ok, b + 1)
                for t in range(TPB):
                    for i in range(IT):
                        last = nc.tensor.matmul(bank[:, 6 + b, t * P:(t + 1) * P], t3[:, i, b, t * P:(t + 1) * P],
                                                w3T[:, 2, i * P:(i + 1) * P], start=(i == 0), stop=(i == IT - 1))
                last.then_inc(res_in_psum, 1)

        @block.scalar
        def _(act):
            xs = a["x"].rearrange("b (t p) d -> b p t d", p=P)
            act.dma_start(ctx_tok[:], a["ctx_1024"].rearrange("b k d -> k b d")).then_inc(in_ctx, 16)
            for b in range(B):
                act.dma_start(x[:, TPB * b:TPB * (b + 1), :], xs[b]).then_inc(in_x[b], 16)
            for n in VROWS[:2]:
                r, k = vrow[n]
                act.dma_start(vec_rows0[r:r + k, :], vsrc[n].rearrange("(r d) -> r d", d=D)).then_inc(in_vec0, 16)
            for h in range(H0 + 1):
                if h < H0:
                    act.wait_ge(wT_in_psum, h + 1)
                    if h >= 2:
                        act.wait_ge(ab_in_psum, h - 1)
                    nc.scalar.activation(wT0[:, h % 2, :, :],
                                         bank[:, h % 2, 0:3 * P].rearrange("p (n m) -> p n m", n=3), ACT.Copy)\
                        .then_inc(wT_ok, 1)
                if h == 0:
                    act.wait_ge(vcol_in_psum, 1)
                    nc.scalar.activation(vec_cols[:, 0:FIRST], bank[:, 6, 0:FIRST], ACT.Copy).then_inc(vcol_ok, 1)
                    nc.scalar.activation(bq0_scaled[:], bank[:, 6, 0:H0], ACT.Copy, scale=SC0).then_inc(vcol_ok, 1)
                    act.wait_ge(vcol_ok, 2)
                    act.wait_ge(const_made, 1)
                if h < H0:
                    if h >= 2:
                        act.wait_ge(bv_used, h - 1)
                    col = vrow["bv0"][0] + h
                    nc.scalar.activation(bv0_wide[:, h % 2, :], ones[:], ACT.Identity, scale=vec_cols[:, col:col + 1])\
                        .then_inc(bv_wide_ok, 1)
                if h:
                    act.wait_ge(ab_in_psum, h)
                    nc.scalar.activation(ab0[:, h - 1, :], bank[:, 2 + (h - 1) % 2, 0:2 * P + 1], ACT.Copy)\
                        .then_inc(ab_ok, 1)
                if h == H0 // 2:
                    act.wait_ge(cT_in_psum, 1)
                    cT = bank[:, 6, :].rearrange("p (n b k) -> p n b k", n=2, b=B)
                    nc.scalar.activation(kvT[HI][:, :, S:NK], cT[:, 0, :, 0:NC], ACT.Copy).then_inc(cT_ok, 1)
                    nc.scalar.activation(ctxT[:], cT[:, 1, :, 0:NC], ACT.Copy).then_inc(cT_ok, 1)
                    for b in range(B):
                        act.wait_ge(xT_in_psum, TPB * (b + 1))
                        nc.scalar.activation(kvT[HI][:, b, 0:S], bank[:, 4 + b, :], ACT.Copy).then_inc(kvT_hi_ok[b], 1)

            def query(h, b):
                u = B * h + b
                act.wait_ge(q_in_psum, u + 1)
                wait_from(act, scores_ok, TPB * (u - 1))
                wait_from(act, q_ok, u)
                nc.scalar.activation(q_full, bank[:, 7, :], ACT.Identity,
                                     bias=ab0[:, bass.ds(h, 1), 2 * P:2 * P + 1].rearrange("p n m -> p (n m)"),
                                     scale=SC0).then_inc(q_full_ok, 1)
                act.wait_ge(q_full_ok, u + 1)
                nc.scalar.activation(qT[HI][:, b, :], q_full, ACT.Copy).then_inc(q_hi_ok, 1)

            def exponent(u, b, i):
                act.wait_ge(max_ok, TPB * u + i + 1)
                wait_from(act, pT_in_psum, NCH * (u - 1))
                wait_from(act, inv_ok, u - 1)
                nc.scalar.activation(prob[b][:, i, :], scores0(i), ACT.Exp, bias=neg_max[:, b, i:i + 1],
                                     accum_out=row_sum[:, b, i:i + 1])\
                    .then_inc(prob_ok, 1)

            def evacuate(u, b, c):
                n = chunk_keys(c)
                act.wait_ge(pT_in_psum, NCH * u + c + 1)
                slot_free(act, u, c)
                nc.scalar.activation(probT[HI][0:n, SLOT[c], :], bank[0:n, PT_BANK[b][c], :], ACT.Copy)\
                    .then_inc(pT_hi_ok, 1)

            def copy_u(u):
                act.wait_ge(pv_done, NCH * (u + 1))
                wait_from(act, o_in_psum, u)
                nc.scalar.activation(uT, bank[:, 6, :], ACT.Copy).then_inc(u_ok, 1)

            def step(h, b, c, last):
                u = B * h + b
                if c == 2 and not last:
                    query(h + b, 1 - b)
                if from_unit(1, u):
                    evacuate(u - 1, 1 - b, c)
                if c == 0 and from_unit(2, u):
                    copy_u(u - 2)
                if c < TPB:
                    exponent(u, b, c)

            def l1_products(n):
                act.wait_ge(l1_in_psum, n + 1)
                if n == 0:
                    nc.scalar.activation(l1T[:], bank[:, 0, 0:2 * P].rearrange("p (n m) -> p n m", n=2), ACT.Copy)\
                        .then_inc(l1_ok, 1)
                    nc.scalar.activation(k1T[:], bank[:, 1, 0:B * NC].rearrange("p (b k) -> p b k", b=B), ACT.Copy)\
                        .then_inc(l1_ok, 1)
                    nc.scalar.activation(v1[:], bank[0:NC, 2, 0:B * D].rearrange("p (b d) -> p b d", b=B), ACT.Copy)\
                        .then_inc(l1_ok, 1)
                elif n == 1:
                    nc.scalar.activation(kq1[:], bank[:, 3, 0:B * NC].rearrange("p (b k) -> p b k", b=B), ACT.Copy)\
                        .then_inc(l1_ok, 1)
                    nc.scalar.activation(wa1T[:], bank[:, 3, 256:256 + P], ACT.Copy).then_inc(l1_ok, 1)
                else:
                    nc.scalar.activation(waa1[:], bank[:, 0, 0:D], ACT.Copy).then_inc(l1_ok, 1)

            act.wait_ge(vcol_in_psum, 2)
            nc.scalar.activation(vec_cols[:, FIRST:nrow], bank[:, 1, 0:nrow - FIRST], ACT.Copy).then_inc(vcol_ok, 1)
            for n in range(2):
                row = vrow[f"L{n + 2}_xattn_bq"][0] - FIRST
                nc.scalar.activation(bq16[:, n:n + 1], bank[:, 1, row:row + 1], ACT.Copy, scale=SC16)\
                    .then_inc(vcol_ok, 1)
            act.wait_ge(ab_ok, H0)
            query(0, 0)
            run_heads(act, step)
            for c in range(NCH):
                evacuate(U0 - 1, B - 1, c)
                if c == 0:
                    copy_u(U0 - 2)
                if c in (0, 2, 3):
                    l1_products((0, 2, 3).index(c))
            copy_u(U0 - 1)

            def norm_copy(k):
                act.wait_ge(xT_in_psum, NT * k + TPB)
                nc.scalar.activation(xnT[:, 0, :], bank[:, 4, :], ACT.Copy).then_inc(xnT_b_ok[0], 1)

            norm_copy(1)
            for b in range(B):
                act.wait_ge(xnT_b_ok[b], 1)
                nc.scalar.activation(qT[HI][:, b, :], xnT[:, b, :], ACT.Copy).then_inc(xn_hi_ok, 1)

            def relu(e, side):
                for j in range(FT):
                    for b in range(B):
                        act.wait_ge(h_in_psum, FT * B * e + j * B + b + 1)
                        wait_from(act, y_in_psum, B * (e - 1))
                        row = vrow["L0_ffn_b1"][0] + FT * e + j
                        nc.scalar.activation(hT[:, side, j, b, :], bank[:, j * B + b, :], ACT.Relu,
                                             bias=vec_cols[:, row:row + 1]).then_inc(h_ok, 1)

            relu(0, 0)
            relu(1, 1)
            act.wait_ge(diff_ok, 1)
            nc.scalar.activation(top_exp[:], top_diff[:], ACT.Exp).then_inc(top_exp_ok, 1)
            act.wait_ge(gT_in_psum, 1)
            nc.scalar.activation(gateT[:].rearrange("e t p -> e (t p)"),
                                 bank[0:E, 4:6, :].rearrange("e b n -> e (b n)"), ACT.Copy).then_inc(gT_ok, 1)
            for e in range(2, E):
                relu(e, e % 2)
            def keys_values(n):
                act.wait_ge(kv16_in_psum, n + 1)
                row = vrow[f"L{n + 2}_xattn_bk"][0]
                nc.scalar.activation(k16T[:, n], bank[:, 0, 0:B * NC].rearrange("p (b k) -> p b k", b=B), ACT.Identity,
                                     bias=vec_cols[:, row:row + 1]).then_inc(kv16_ok, 1)
                nc.scalar.activation(v_pair[:, n], bank[:, 1, 0:B * D].rearrange("p (b d) -> p b d", b=B), ACT.Copy)\
                    .then_inc(kv16_ok, 1)
                nc.scalar.activation(v_left[:, n], bank[0:LP, 1, B * D:2 * B * D].rearrange("p (b d) -> p b d", b=B),
                                     ACT.Copy).then_inc(kv16_ok, 1)

            def attention16(n, k):
                norm_copy(k)
                for b in range(B):
                    act.wait_ge(q16_in_psum, B * n + b + 1)
                    nc.scalar.activation(q16T[:, b, :], bank[:, 6 + b, :], ACT.Identity, bias=bq16[:, n:n + 1],
                                         scale=SC16).then_inc(q16_ok, 1)
                for t in range(NT + 1):
                    if t < NT:
                        m = NT * n + t
                        act.wait_ge(s16_ok, m + 1)
                        if t >= 2:
                            act.wait_ge(p16T_in_psum, 2 * (m - 1))
                        pair, left = p16[:, t % 2, 0:HM * PK], p16[:, t % 2, HM * PK:HM * NC]
                        nc.scalar.activation(pair.rearrange("p (h k) -> p h k", h=HM), s16[:, t % 2, :, 0:PK], ACT.Exp)\
                            .then_inc(p16_ok, 1)
                        nc.scalar.activation(left.rearrange("p (h k) -> p h k", h=HM), s16[:, t % 2, :, PK:NC], ACT.Exp)\
                            .then_inc(p16_ok, 1)
                    if t:
                        m = NT * n + t - 1
                        act.wait_ge(p16T_in_psum, 2 * m + 1)
                        if m:
                            act.wait_ge(o16_in_psum, m)
                        nc.scalar.activation(p16T[:, 0:NPAIR, :],
                                             bank[:, 4:6, :].rearrange("p b (c q) -> p (b c) q", c=4), ACT.Copy)\
                            .then_inc(p16T_ok, 1)
                        act.wait_ge(p16T_in_psum, 2 * m + 2)
                        nc.scalar.activation(p16T[0:LP, NPAIR:NPAIR + 2, :],
                                             bank[0:LP, 6, 0:2 * P].rearrange("p (c q) -> p c q", c=2), ACT.Copy)\
                            .then_inc(p16T_ok, 1)
                row = vrow[f"L{n + 2}_xattn_bv"][0]
                for b in range(B):
                    act.wait_ge(o16T_in_psum, B * n + b + 1)
                    nc.scalar.activation(q16T[:, b, :], bank[:, b, :], ACT.Identity, bias=vec_cols[:, row:row + 1])\
                        .then_inc(o16T_ok, 1)

            keys_values(0)
            norm_copy(2)
            for b in range(B):
                act.wait_ge(s1_ok, b + 1)
                part = s1[:, TPB * b:TPB * (b + 1), :]
                nc.scalar.activation(part, part, ACT.Exp, scale=SC1).then_inc(p1_ok, 1)
            for b in range(B):
                act.wait_ge(p1T_in_psum, b + 1)
                nc.scalar.activation(p1T[:, TPB * b:TPB * (b + 1), :],
                                     bank[0:NC, 2 + b, :].rearrange("p (i q) -> p i q", i=TPB), ACT.Copy)\
                    .then_inc(p1T_ok, 1)
            keys_values(1)
            norm_copy(3)
            for b in range(B):
                act.wait_ge(tanh_in_ok, b + 1)
                part = tanh_in[:, TPB * b:TPB * (b + 1), :]
                nc.scalar.activation(part, part, ACT.Tanh).then_inc(tanh_ok, 1)
            act.wait_ge(w2T_in_psum, 1)
            act.wait_ge(rne_made, 3)
            for m in range(2):
                nc.scalar.activation(w2T[:, m, 0:I2], bank[:, m, 0:I2], ACT.Copy).then_inc(w2T_ok, 1)
            nc.scalar.activation(w2T[:, 2, 0:2 * P], bank[:, 2, 0:2 * P], ACT.Copy).then_inc(w2T_ok, 1)
            nc.scalar.activation(w2T[0:rows2[2], 2, 2 * P:3 * P], bank[0:rows2[2], 2, 2 * P:3 * P], ACT.Copy)\
                .then_inc(w2T_ok, 1)
            nc.scalar.activation(down_row[:], bank[:, 3, 0:P], ACT.Copy).then_inc(w2T_ok, 1)
            act.wait_ge(in_f2, 16 * 7)
            nc.scalar.activation(clip_sig[:], clip[:], ACT.Tanh, scale=0.5).then_inc(clip_tanh_ok, 1)
            attention16(0, 4)
            act.wait_ge(w3T_in_psum, 1)
            nc.scalar.activation(w3T, bank[:, 0:3, 0:IT * P], ACT.Copy).then_inc(w3T_ok, 1)
            act.wait_ge(xT_in_psum, NT * 5 + TPB)
            nc.scalar.activation(xqT[:, 0, :], bank[:, 4, :], ACT.Identity, bias=minus_rne[:]).then_inc(xnT_b_ok[0], 1)
            act.wait_ge(c_ok, 1)
            for b in range(B):
                for i in range(IT):
                    n, r = IT * b + i, rows2[i]
                    act.wait_ge(gu_in_psum, n + 1)
                    if n >= 2:
                        act.wait_ge(gu_silu_ok, n - 1)
                    nc.scalar.activation(tanh_out[0:r, n % 2, :], bank[0:r, 2 * (n % 3), :], ACT.Tanh,
                                         scale=c_gate[0:r, i:i + 1]).then_inc(gu_tanh_ok, 1)
                    nc.scalar.activation(val[0:r, i, b, :], bank[0:r, 2 * (n % 3) + 1, :], ACT.Identity,
                                         scale=c_both[0:r, i:i + 1]).then_inc(gu_up_ok, 1)
            act.wait_ge(hscale_ok, 1)
            for b in range(B):
                for i in range(IT):
                    h = val[0:rows2[i], i, b, :]
                    nc.scalar.activation(h, h, ACT.Identity, bias=plus_rne[0:rows2[i], :],
                                         scale=h_inv[0:rows2[i], :]).then_inc(h_rounded, 1)
            attention16(1, 6)
            norm_copy(7)
            for b in range(B):
                for i in range(IT):
                    n = IT * b + i
                    for m, to in enumerate((val2, val)):
                        act.wait_ge(ug_in_psum, 2 * n + m + 1)
                        nc.scalar.activation(to[:, i, b, :], bank[:, 2 * (n % 3) + m, :], ACT.Copy)\
                            .then_inc(ug_copied, 1)
            last = B - 1
            act.wait_ge(ug_scale_ok, 1)
            act.wait_ge(ug_maxed, 2 * IT * B)
            nc.scalar.activation(val2[:, :, last, :], val2[:, :, last, :], ACT.Identity, bias=plus_rne[:],
                                 scale=ug_inv[:, 0:1]).then_inc(act_rounded, 1)
            for b in range(B):
                act.wait_ge(gate_int_ok, b + 1)
                nc.scalar.activation(t3[:, :, b, :], val2[:, :, b, :], ACT.Tanh, scale=half_sg[:]).then_inc(tanh3_ok, 1)
            act.wait_ge(tanh3_ok, B)
            nc.scalar.activation(t3[:, :, last, :], t3[:, :, last, :], ACT.Identity, bias=plus_rne_half[:],
                                 scale=32768.0).then_inc(act_rounded, 1)
            for n in range(2):
                act.wait_ge(ratio_ok, n + 1)
                nc.scalar.activation(t3[:, :, last, :], t3[:, :, last, :], ACT.Identity, bias=plus_rne[:],
                                     scale=ratio3[:, n:n + 1]).then_inc(act_rounded, 1)

        @block.vector
        def _(dve):
            own = Steps(dve, dve_step)
            dve.wait_ge(in_ctx, 16)
            for b in range(B):
                own.add(nc.vector.bn_stats(ctx_stats[:, b, :], ctx_tok[:, b, :]))
            own.settle()
            for b in range(B):
                own.add(nc.vector.bn_aggr(ctx_meanvar[:, b, :], ctx_stats[:, b, :]))
            own.settle()
            nc.vector.tensor_scalar(ctx_var_eps[:], ctx_meanvar[:, :, 1], EPS, None, ALU.add).then_inc(ctx_var_ok, 1)

            def layer_stats(b):
                tiles = range(TPB * b, TPB * (b + 1))
                for t in tiles:
                    own.add(nc.vector.bn_stats(stats[:, t, :], x[:, t, :]))
                own.settle()
                for t in tiles:
                    own.add(nc.vector.bn_aggr(meanvar[:, t, :], stats[:, t, :]))
                own.settle()
                c = slice(TPB * b, TPB * (b + 1))
                nc.vector.tensor_scalar(var_eps[:, c], meanvar[:, c, 1], EPS, None, ALU.add).then_inc(var_ok, 1)

            for b in range(B):
                dve.wait_ge(in_x[b], 16)
                layer_stats(b)
            dve.wait_ge(ctx_rstd_ok, 1)
            for b in range(B):
                own.add(nc.vector.tensor_scalar(ctx_norm[:, b, :], ctx_tok[:, b, :], ctx_meanvar[:, b, 0:1],
                                                ctx_rstd[:, b:b + 1], ALU.subtract, ALU.mult))
            own.settle()
            dve.wait_ge(in_norm, 16 * 5)
            own.add(nc.vector.tensor_tensor(ctx_norm[:], ctx_norm[:],
                                            gamma_ctx[:].unsqueeze(1).to_broadcast([NC, B, D]), ALU.mult))
            own.settle()
            nc.vector.tensor_tensor(ctx_norm[:], ctx_norm[:], beta_ctx[:].unsqueeze(1).to_broadcast([NC, B, D]),
                                    ALU.add).then_inc(ctx_norm_ok, 1)
            for b in range(B):
                dve.wait_ge(rstd_ok, b + 1)
                for t in range(TPB * b, TPB * (b + 1)):
                    own.add(nc.vector.tensor_scalar(xn[:, t, :], x[:, t, :], meanvar[:, t, 0:1], rstd[:, t:t + 1],
                                                    ALU.subtract, ALU.mult))
                own.settle()
                part = xn[:, TPB * b:TPB * (b + 1), :]
                own.add(nc.vector.tensor_tensor(part, part, gamma_lat[:].unsqueeze(1).to_broadcast([P, TPB, D]),
                                                ALU.mult))
                own.settle()
                for t in range(TPB * b, TPB * (b + 1)):
                    nc.vector.tensor_tensor(xn[:, t, :], xn[:, t, :], beta_lat[:], ALU.add).then_inc(xn_ok, 1)
            dve.wait_ge(cT_ok, 2)
            cT = bank[:, 6, :].rearrange("p (n b k) -> p n b k", n=2, b=B)
            nc.vector.tensor_tensor(kvT[LO][:, :, S:NK], cT[:, 0, :, 0:NC],
                                    kvT[HI][:, :, S:NK].bitcast(F32), ALU.subtract).then_inc(cT_lo_ok, 1)
            for b in range(B):
                dve.wait_ge(kvT_hi_ok[b], 1)
                nc.vector.tensor_tensor(kvT[LO][:, b, 0:S], bank[:, 4 + b, :], kvT[HI][:, b, 0:S].bitcast(F32),
                                        ALU.subtract).then_inc(kvT_lo_ok[b], 1)
            dve.wait_ge(xn_ok, NT)
            for b in range(B):
                c = slice(TPB * b, TPB * (b + 1))
                nc.vector.tensor_copy(kv_lat[HI][:, c, :], xn[:, c, :]).then_inc(kv_lat_ok, 1)
                dve.wait_ge(kv_lat_ok, 2 * b + 1)
                nc.vector.tensor_tensor(kv_lat[LO][:, c, :], xn[:, c, :], kv_lat[HI][:, c, :].bitcast(F32),
                                        ALU.subtract)\
                    .then_inc(kv_lat_ok, 1)
            dve.wait_ge(ctx_norm_ok, 1)
            nc.vector.tensor_copy(kv_ctx[HI][:], ctx_norm[:]).then_inc(kv_lat_ok, 1)
            dve.wait_ge(kv_lat_ok, 2 * B + 1)
            nc.vector.tensor_tensor(kv_ctx[LO][:], ctx_norm[:], kv_ctx[HI][:].bitcast(F32), ALU.subtract)\
                .then_inc(kv_lat_ok, 1)
            dve.wait_ge(bv_used, H0)
            nc.vector.tensor_tensor(out_bias0[:], bank[:, 7, 0:D], bo0[:], ALU.add).then_inc(bias0_ok, 1)

            def maximum(u, b, i):
                dve.wait_ge(scores_ok, TPB * u + i + 1)
                wait_from(dve, prob_ok, TPB * (u - 1))
                nc.vector.tensor_reduce(neg_max[:, b, i:i + 1], scores0(i), AX.X, ALU.max, negate=True)\
                    .then_inc(max_ok, 1)

            def evacuate(u, b, c):
                n = chunk_keys(c)
                dve.wait_ge(pT_hi_ok, NCH * u + c + 1)
                nc.vector.tensor_tensor(probT[LO][0:n, SLOT[c], :], bank[0:n, PT_BANK[b][c], :],
                                        probT[HI][0:n, SLOT[c], :].bitcast(F32), ALU.subtract).then_inc(pT_lo_ok, 1)

            def query(u, b):
                dve.wait_ge(q_hi_ok, u + 1)
                nc.vector.tensor_tensor(qT[LO][:, b, :], q_full, qT[HI][:, b, :].bitcast(F32), ALU.subtract)\
                    .then_inc(q_ok, 1)

            def add_output(u, b):
                dve.wait_ge(o_in_psum, u + 1)
                dve.wait_ge(inv_ok, u + 1)
                if not from_unit(1, u):
                    dve.wait_ge(x_biased, 1)
                wait_from(dve, o_added, u - 1)
                for i in range(TPB):
                    t = TPB * b + i
                    last = nc.vector.scalar_tensor_tensor(out=x[:, t, :], in0=bank[:, 7, i * P:(i + 1) * P],
                                                          scalar=row_inv[:, b, i:i + 1], in1=x[:, t, :],
                                                          op0=ALU.mult, op1=ALU.add)
                last.then_inc(o_added, 1)

            def invert(u, b):
                dve.wait_ge(prob_ok, TPB * (u + 1))
                wait_from(dve, o_added, u - 1)
                nc.vector.reciprocal(row_inv[:, b, :], row_sum[:, b, :]).then_inc(inv_ok, 1)

            def row_max(to, src, axis=AX.X):
                return nc.vector.tensor_reduce(to, src, axis, ALU.max, apply_absolute_value=True)

            def weight_scales2():
                own.add(nc.vector.memset(wmax2[:], 1.0))
                dve.wait_ge(in_f2, 16 * 7)
                own.settle()
                for m in range(2):
                    own.add(row_max(wmax2[:, IT * m:IT * m + 2], wn2[:, m, 0:2 * P].rearrange("p (i d) -> p i d", i=2)))
                    own.add(row_max(wmax2[0:rows2[2], IT * m + 2:IT * m + 3], wn2[0:rows2[2], m, 2 * P:3 * P]))
                own.add(row_max(wmax2[:, 6:7], wn2[:, 2, 0:I2]))
                own.settle()
                own.add(nc.vector.tensor_scalar(wscale2[:], wmax2[:], 1.0 / 127, None, ALU.mult))
                own.settle()
                nc.vector.reciprocal(winv2[:], wscale2[:]).then_inc(wmax_ok, 1)

            def weight_scales3():
                dve.wait_ge(in_f3, 16 * 3)
                own.add(nc.vector.tensor_reduce(wmax3[:], wn3[:], AX.X, ALU.max, apply_absolute_value=True))
                own.settle()
                own.add(nc.vector.tensor_scalar(wscale3[:], wmax3[:], 1.0 / 7, 1e-12, ALU.mult, ALU.max))
                own.settle()
                nc.vector.reciprocal(winv3[:], wscale3[:]).then_inc(wmax_ok, 1)

            def step(h, b, c, last):
                u = B * h + b
                if c < TPB:
                    maximum(u, b, c)
                if c == 2 and not last:
                    query(u + 1, 1 - b)
                if from_unit(1, u):
                    evacuate(u - 1, 1 - b, c)
                if c == 0 and from_unit(1, u):
                    invert(u - 1, 1 - b)
                if c == TPB and from_unit(2, u):
                    add_output(u - 2, b)
                if c == TPB and isinstance(u, int) and u == 1:
                    weight_scales2()
                if c == TPB and isinstance(u, int) and u == B + 1:
                    weight_scales3()

            query(0, 0)
            run_heads(dve, step)
            for c in range(NCH):
                evacuate(U0 - 1, B - 1, c)
                if c == 0:
                    invert(U0 - 1, B - 1)
            add_output(U0 - 2, 0)

            def layer_norm(k, result):
                def normalise(b):
                    dve.wait_ge(rstd_ok, B * k + b + 1)
                    for t in range(TPB * b, TPB * (b + 1)):
                        nc.vector.tensor_scalar(xn[:, t, :], x[:, t, :], meanvar[:, t, 0:1], rstd[:, t:t + 1],
                                                ALU.subtract, ALU.mult).then_inc(xn_ok, 1)

                for b in range(B):
                    result(b)
                    layer_stats(b)
                for b in range(B):
                    normalise(b)

            def norm_copy(k):
                dve.wait_ge(xT_in_psum, NT * (k + 1))
                nc.vector.tensor_copy(xnT[:, 1, :], bank[:, 5, :]).then_inc(xnT_b_ok[1], 1)

            def moe_norm_copy():
                norm_copy(1)
                for b in range(B):
                    dve.wait_ge(xn_hi_ok, b + 1)
                    nc.vector.tensor_tensor(qT[LO][:, b, :], xnT[:, b, :], qT[HI][:, b, :].bitcast(F32), ALU.subtract)\
                        .then_inc(xn_lo_ok, 1)

            def per_tile(v, n=E):
                return v.unsqueeze(2).to_broadcast([P, NT, n])

            def batch(tile, b):
                return tile[:, TPB * b:TPB * (b + 1), :]

            def add_result(k, b):
                dve.wait_ge(res_in_psum, B * k + b + 1)
                nc.vector.tensor_tensor(batch(x, b), bank[:, 6 + b, :].rearrange("p (i d) -> p i d", i=TPB),
                                        batch(x, b), ALU.add).then_inc(x_done, 1)
                dve.wait_ge(x_done, B * k + b + 1)

            def result0(b):
                if b:
                    add_output(U0 - 1, B - 1)
                dve.wait_ge(o_added, U0 - 1 + b)

            layer_norm(1, result0)
            moe_norm_copy()
            dve.wait_ge(logit_in_psum, 1)
            dve.wait_ge(rank_ok, E)
            dve.wait_ge(in_moe, 16 * 5)
            own.add(nc.vector.tensor_tensor(logit[:], bank[:, 4, 0:NT * E].rearrange("p (t e) -> p t e", t=NT),
                                            br[:].unsqueeze(1).to_broadcast([P, NT, E]), ALU.add))
            own.settle()
            for i, src in ((0, logit), (1, logit2)):
                own.add(nc.vector.tensor_reduce(top[i][:], src[:], AX.X, ALU.max))
                own.settle()
                own.add(nc.vector.tensor_tensor(key[:], src[:], per_tile(top[i][:]), ALU.is_equal))
                own.settle()
                own.add(nc.vector.tensor_tensor(key[:], key[:], rank[:], ALU.mult))
                own.settle()
                own.add(nc.vector.tensor_reduce(top_key[:], key[:], AX.X, ALU.max))
                own.settle()
                own.add(nc.vector.tensor_tensor(pick[i][:], key[:], per_tile(top_key[:]), ALU.is_equal))
                own.settle()
                if i == 0:
                    own.add(nc.vector.scalar_tensor_tensor(out=logit2[:], in0=pick[0][:], scalar=-3e38, in1=logit[:],
                                                           op0=ALU.mult, op1=ALU.add))
                    own.settle()
            nc.vector.tensor_tensor(top_diff[:], top[1][:], top[0][:], ALU.subtract).then_inc(diff_ok, 1)
            dve.wait_ge(top_exp_ok, 1)
            own.add(nc.vector.tensor_scalar(top_den[:], top_exp[:], 1.0, None, ALU.add))
            own.settle()
            own.add(nc.vector.reciprocal(top_w[0][:], top_den[:]))
            own.settle()
            own.add(nc.vector.tensor_tensor(top_w[1][:], top_exp[:], top_w[0][:], ALU.mult))
            own.add(nc.vector.tensor_tensor(pick[0][:], pick[0][:], per_tile(top_w[0][:]), ALU.mult))
            own.settle()
            own.add(nc.vector.tensor_tensor(pick[1][:], pick[1][:], per_tile(top_w[1][:]), ALU.mult))
            own.settle()
            nc.vector.tensor_tensor(gate[:], pick[0][:], pick[1][:], ALU.add).then_inc(gate_ok, 1)
            dve.wait_ge(gate_ok, 1)

            def add_expert(e, b):
                dve.wait_ge(y_in_psum, B * e + b + 1)
                if not isinstance(e, int) or e:
                    dve.wait_ge(y_added, B * (e - 1) + b + 1)
                for i in range(TPB):
                    t = TPB * b + i
                    last = nc.vector.scalar_tensor_tensor(out=x[:, t, :], in0=bank[:, 6 + b, i * P:(i + 1) * P],
                                                          scalar=gate[:, t, bass.ds(e, 1)], in1=x[:, t, :],
                                                          op0=ALU.mult, op1=ALU.add)
                last.then_inc(y_added, 1)

            for b in range(B):
                add_expert(0, b)
            dve.wait_ge(b2_in_psum, 1)
            for b in range(B):
                dve.wait_ge(y_added, b + 1)
                nc.vector.tensor_tensor(batch(x, b), bank[:, 4 + b, :].rearrange("p (i d) -> p i d", i=TPB),
                                        batch(x, b), ALU.add).then_inc(b2_added, 1)
            dve.wait_ge(b2_added, B)
            with dve.Fori(1, E - 1) as e:
                for b in range(B):
                    add_expert(e, b)

            def result1(b):
                add_expert(E - 1, b)
                dve.wait_ge(y_added, B * (E - 1) + b + 1)

            layer_norm(2, result1)
            norm_copy(2)
            for b in range(B):
                dve.wait_ge(s1_in_psum, b + 1)
                src = bank[:, b, 0:TPB * NC].rearrange("p (i k) -> p i k", i=TPB)
                own.add(nc.vector.tensor_reduce(neg_max1[:, TPB * b:TPB * (b + 1)], src, AX.X, ALU.max, negate=True))
                own.settle()
                nc.vector.tensor_tensor(batch(s1, b), src,
                                        neg_max1[:, TPB * b:TPB * (b + 1)].unsqueeze(2).to_broadcast([P, TPB, NC]),
                                        ALU.add).then_inc(s1_ok, 1)
            for b in range(B):
                dve.wait_ge(p1_ok, b + 1)
                own.add(nc.vector.tensor_reduce(sum1[:, TPB * b:TPB * (b + 1)], batch(s1, b), AX.X, ALU.add))
            own.settle()
            own.add(nc.vector.reciprocal(inv1[:], sum1[:]))
            own.settle()
            for b in range(B):
                dve.wait_ge(o1_in_psum, b + 1)
                nc.vector.tensor_tensor(turned[:, b, :].rearrange("p (c i) -> p i c", i=TPB),
                                        bank[:, 4 + b, :].rearrange("p (i c) -> p i c", i=TPB),
                                        inv1[:, TPB * b:TPB * (b + 1)].unsqueeze(2).to_broadcast([P, TPB, D]),
                                        ALU.mult).then_inc(turned_ok, 1)
            dve.wait_ge(x_biased, 2)
            layer_norm(3, lambda b: add_result(0, b))
            norm_copy(3)
            dve.wait_ge(in_l1, 16 * 9)
            for b in range(B):
                dve.wait_ge(res_in_psum, B + b + 1)
                nc.vector.tensor_tensor(batch(tanh_in, b), bank[:, 6 + b, :].rearrange("p (i d) -> p i d", i=TPB),
                                        fbias1[:].unsqueeze(1).to_broadcast([P, TPB, D]), ALU.add)\
                    .then_inc(tanh_in_ok, 1)

            def result3(b):
                dve.wait_ge(tanh_ok, b + 1)
                nc.vector.tensor_tensor(batch(x, b), batch(tanh_in, b), batch(x, b), ALU.add).then_inc(x_done, 1)
                dve.wait_ge(x_done, B + b + 1)


            def attention16(n, k, result):
                layer_norm(k, result)
                norm_copy(k)
                if n == 0:
                    dve.wait_ge(mask_neg_ok, NT)
                LAG = 3
                for t in range(NT + LAG):
                    m, z = NT * n + t, t % 2
                    if t < NT:
                        scores, to = bank[:, 0:4, 0:BK * NC], s16[:, z].rearrange("p (g h) k -> p g (h k)", g=4)
                        dve.wait_ge(s16_in_psum, m + 1)
                        if m >= 2:
                            dve.wait_ge(p16_ok, 2 * (m - 1))
                        if n == 0:
                            nc.vector.tensor_tensor(to, scores, mask_neg[:, t, :].rearrange("p (g n) -> p g n", g=4),
                                                    ALU.add).then_inc(s16_taken, 1)
                        else:
                            nc.vector.tensor_copy(to, scores).then_inc(s16_taken, 1)
                    if t >= LAG:
                        d, y = NT * n + t - LAG, (t - LAG) % 2
                        o = bank[:, 7, 0:HM * (DH + 1)].rearrange("p (h d) -> p h d", h=HM)
                        dve.wait_ge(o16_in_psum, d + 1)
                        if d >= 2:
                            dve.wait_ge(o16_ok, d - 1)
                        own.add(nc.vector.reciprocal(inv16[:, y, :], o[:, :, DH]))
                        own.settle()
                        if n == 0:
                            dve.wait_ge(spoil16_ok, d + 1)
                            own.add(nc.vector.tensor_tensor(inv16[:, y, :], inv16[:, y, :], spoil16[:, d % 4, :],
                                                            ALU.add))
                            own.settle()
                        nc.vector.tensor_tensor(o16[:, t - LAG, :].rearrange("p (h d) -> p h d", h=HM), o[:, :, 0:DH],
                                                inv16[:, y, :].unsqueeze(2).to_broadcast([P, HM, DH]), ALU.mult)\
                            .then_inc(o16_ok, 1)
                    if t < NT:
                        dve.wait_ge(s16_taken, m + 1)
                        if m >= 2 and n == 0:
                            dve.wait_ge(spoil16_ok, m - 1)
                        nc.vector.tensor_reduce(neg_max16[:, z, :], s16[:, z], AX.X, ALU.max, negate=True)\
                            .then_inc(max16_ok, 1)
                dve.wait_ge(x_biased, 3 + n)

            def global_max(j, count):
                dve.wait_ge(pmaxT_in_psum, j + 1)
                columns = bank[0:1, 7, 0:count * P].rearrange("p (c q) -> p c q", c=count)
                nc.vector.tensor_reduce(gmax_row[:, 0:count], columns, AX.X, ALU.max).then_inc(gmax_ok, 1)
                dve.wait_ge(gmax_in_psum, j + 1)
                return bank[:, 7, 2 * P:2 * P + count]

            def scalars(to, src, s1, s2, op0, op1):
                own.add(nc.vector.tensor_scalar(to, src, s1, s2, op0, op1))
                own.settle()

            attention16(0, 4, result3)
            dve.wait_ge(clip_tanh_ok, 1)
            scalars(clip_sig[:], clip_sig[:], 0.5, 0.5, ALU.mult, ALU.add)
            layer_norm(5, lambda b: add_result(2, b))
            dve.wait_ge(xn_ok, NT * 6)
            row_max(pmax[:, 0:1], xn[:], AX.XY).then_inc(pmax_ok, 1)
            m = global_max(0, 1)
            scalars(x_scale[:], m, clip_sig[:, 0:1], 1.0 / 127, ALU.mult, ALU.mult)
            own.add(nc.vector.reciprocal(x_inv[:], x_scale[:]))
            own.settle()
            for b in range(B):
                scalars(batch(xn, b), batch(xn, b), x_inv[:], RNE, ALU.mult, ALU.add)
                nc.vector.tensor_scalar(batch(xn, b), batch(xn, b), RNE + 127, RNE - 128, ALU.min, ALU.max)\
                    .then_inc(xq_ok, 1)
            scalars(c_gate[:], wscale2[:, 0:IT], x_scale[:], 0.5, ALU.mult, ALU.mult)
            scalars(c_both[:], wscale2[:, IT:2 * IT], x_scale[:], None, ALU.mult, ALU.bypass)
            nc.vector.tensor_tensor(c_both[:], c_both[:], c_gate[:], ALU.mult).then_inc(c_ok, 1)
            own.add(nc.vector.memset(unit_max[:], 0.0))
            dve.wait_ge(c_ok, 1)
            own.settle()
            dve.wait_ge(xT_in_psum, NT * 6)
            nc.vector.tensor_scalar(xqT[:, 1, :], bank[:, 5, :], -RNE, None, ALU.add).then_inc(xnT_b_ok[1], 1)

            def product_max(n):
                b, i = n // IT, n % IT
                dve.wait_ge(gu_product_ok, n + 1)
                own.add(row_max(unit_max[0:rows2[i], 0, n:n + 1], val[0:rows2[i], i, b, :]))

            for n in range(IT * B):
                r = rows2[n % IT]
                dve.wait_ge(gu_tanh_ok, n + 1)
                if n >= 2:
                    dve.wait_ge(gu_product_ok, n - 1)
                nc.vector.scalar_tensor_tensor(out=silu[0:r, n % 2, :], in0=tanh_out[0:r, n % 2, :], scalar=1.0,
                                               in1=bank[0:r, 2 * (n % 3), :], op0=ALU.add, op1=ALU.mult)\
                    .then_inc(gu_silu_ok, 1)
                if n:
                    product_max(n - 1)
            product_max(IT * B - 1)
            own.settle()
            row_max(pmax[:, 0:1], unit_max[:, 0, :]).then_inc(pmax_ok, 1)
            m = global_max(1, 1)
            scalars(h_scale[:], m, clip_sig[:, 1:2], 1.0 / 127, ALU.mult, ALU.mult)
            nc.vector.reciprocal(h_inv[:], h_scale[:]).then_inc(hscale_ok, 1)
            dve.wait_ge(w2T_ok, 5)
            own.add(nc.vector.tensor_scalar(down_scale[:], down_row[:], h_scale[:], None, ALU.mult))
            for b in range(B):
                for i in range(IT):
                    n, r = IT * b + i, rows2[i]
                    dve.wait_ge(h_rounded, n + 1)
                    h = val[0:r, i, b, :]
                    scalars(h, h, RNE + 127, RNE - 128, ALU.min, ALU.max)
                    nc.vector.tensor_scalar(hq[0:r, i, b, :], h, -RNE, None, ALU.add).then_inc(hq_ok, 1)

            def result5(b):
                dve.wait_ge(res_in_psum, B * 3 + b + 1)
                own.add(nc.vector.tensor_tensor(batch(tanh_in, b),
                                                bank[:, 6 + b, :].rearrange("p (i d) -> p i d", i=TPB),
                                                down_scale[:].unsqueeze(1).to_broadcast([P, TPB, D]), ALU.mult))
                own.settle()
                nc.vector.tensor_tensor(batch(x, b), batch(tanh_in, b), batch(x, b), ALU.add).then_inc(x_done, 1)
                dve.wait_ge(x_done, B * 3 + b + 1)

            attention16(1, 6, result5)
            def rounded(v, b, factor, offset, n):
                if b < B - 1:
                    scalars(v, v, factor, offset, ALU.mult, ALU.add)
                else:
                    dve.wait_ge(act_rounded, n)

            Q16 = 32767.0
            layer_norm(7, lambda b: add_result(4, b))
            dve.wait_ge(xn_ok, NT * 8)
            row_max(pmax[:, 0:1], xn[:], AX.XY).then_inc(pmax_ok, 1)
            m = global_max(2, 1)
            scalars(x_scale[:], m, 1 / Q16, 1e-12, ALU.mult, ALU.max)
            own.add(nc.vector.reciprocal(x_inv[:], x_scale[:]))
            own.settle()
            for b in range(B):
                scalars(batch(xn, b), batch(xn, b), x_inv[:], RNE, ALU.mult, ALU.add)
                nc.vector.tensor_scalar(batch(xn, b), batch(xn, b), -RNE, x_scale[:], ALU.add, ALU.mult)\
                    .then_inc(xq_ok, 1)
            norm_copy(7)
            for b in range(B):
                for i in range(IT):
                    n = IT * b + i
                    for m in range(2):
                        dve.wait_ge(ug_copied, 2 * n + m + 1)
                        row_max(unit_max[:, m, n:n + 1], (val2, val)[m][:, i, b, :]).then_inc(ug_maxed, 1)
            dve.wait_ge(ug_maxed, 2 * IT * B)
            row_max(pmax[:], unit_max[:]).then_inc(pmax_ok, 1)
            m = global_max(3, 2)
            scalars(ug_scale[:], m, 1 / Q16, 1e-12, ALU.mult, ALU.max)
            sg, su = ug_scale[:, 0:1], ug_scale[:, 1:2]
            own.add(nc.vector.tensor_scalar(half_sg[:], sg, 0.5, None, ALU.mult))
            nc.vector.reciprocal(ug_inv[:], ug_scale[:]).then_inc(ug_scale_ok, 1)
            dve.wait_ge(ug_scale_ok, 1)
            own.settle()
            dve.wait_ge(ug_copied, 2 * IT * B)
            for b in range(B):
                g = val2[:, :, b, :]
                rounded(g, b, ug_inv[:, 0:1], RNE, 1)
                nc.vector.tensor_scalar(g, g, -RNE, None, ALU.add).then_inc(gate_int_ok, 1)
            for b in range(B):
                g, t = val2[:, :, b, :], t3[:, :, b, :]
                dve.wait_ge(tanh3_ok, b + 1)
                rounded(t, b, 32768.0, RNE + 32768, 2)
                scalars(t, t, RNE + 65535, -RNE, ALU.min, ALU.add)
                own.add(nc.vector.tensor_tensor(t, g, t, ALU.mult))
                own.settle()
                own.add(row_max(unit_max[:, 0, b:b + 1], t, AX.XY))
            own.settle()
            row_max(pmax[:, 0:1], unit_max[:, 0, 0:B]).then_inc(pmax_ok, 1)
            m = global_max(4, 1)
            scalars(amax3[:, 0:1], m, sg, 2.0 ** -16, ALU.mult, ALU.mult)
            scalars(scale3[:, 0:1], amax3[:, 0:1], 1 / Q16, 1e-12, ALU.mult, ALU.max)
            own.add(nc.vector.reciprocal(inv3[:, 0:1], scale3[:, 0:1]))
            own.settle()
            nc.vector.tensor_scalar(ratio3[:, 0:1], inv3[:, 0:1], sg, 2.0 ** -16, ALU.mult, ALU.mult)\
                .then_inc(ratio_ok, 1)
            dve.wait_ge(ratio_ok, 1)
            for b in range(B):
                dve.wait_ge(up_int_ok, b + 1)
                t, u = t3[:, :, b, :], val[:, :, b, :]
                rounded(t, b, ratio3[:, 0:1], RNE, 3)
                own.add(nc.vector.scalar_tensor_tensor(out=t, in0=t, scalar=-RNE, in1=u, op0=ALU.add, op1=ALU.mult))
                own.settle()
                own.add(row_max(unit_max[:, 0, b:b + 1], t, AX.XY))
            own.settle()
            row_max(pmax[:, 0:1], unit_max[:, 0, 0:B]).then_inc(pmax_ok, 1)
            m = global_max(5, 1)
            scalars(amax3[:, 1:2], m, scale3[:, 0:1], su, ALU.mult, ALU.mult)
            scalars(scale3[:, 1:2], amax3[:, 1:2], 1 / Q16, 1e-12, ALU.mult, ALU.max)
            own.add(nc.vector.reciprocal(inv3[:, 1:2], scale3[:, 1:2]))
            own.settle()
            nc.vector.tensor_scalar(ratio3[:, 1:2], inv3[:, 1:2], scale3[:, 0:1], su, ALU.mult, ALU.mult)\
                .then_inc(ratio_ok, 1)
            dve.wait_ge(ratio_ok, 2)
            for b in range(B):
                t = t3[:, :, b, :]
                rounded(t, b, ratio3[:, 1:2], RNE, 4)
                nc.vector.tensor_scalar(t, t, -RNE, scale3[:, 1:2], ALU.add, ALU.mult).then_inc(o3_ok, 1)
            for b in range(B):
                add_result(5, b)
            nc.vector.memset(stats[:, 0, 0:1], 0.0).then_inc(x_final, 1)


def kernel(**inputs):
    import numpy as np
    import concourse.bacc as bacc
    from concourse.bass_utils import run_bass_kernel_spmd

    nc = bacc.Bacc("TRN2", target_bir_lowering=False, num_devices=1)
    arrays, handles = {}, {}
    for name, value in inputs.items():
        array = np.ascontiguousarray(value)
        arrays["in_" + name] = array
        handles[name] = nc.dram_tensor("in_" + name, array.shape, mybir.dt.from_np(array.dtype),
                                       kind="ExternalInput").ap()
    out = nc.dram_tensor("out_x", inputs["x"].shape, F32, kind="ExternalOutput").ap()
    build(nc, handles, out)
    result = run_bass_kernel_spmd(nc, [arrays], core_ids=[0])
    return result.results[0]["out_x"]
```
